# Optimizing a Trainium2 kernel written in Bass

```python
import numpy as np
import jax
import jax.numpy as jnp

def _softmax(x, axis=-1):
    return jax.nn.softmax(x, axis=axis)

def _gelu(x):
    return jax.nn.gelu(x, approximate=True)

def _silu(x):
    return jax.nn.silu(x)

def _sigmoid(x):
    return jax.nn.sigmoid(x)

def _layernorm(x, axis=-1, eps=1e-05):
    m = jnp.mean(x, axis=axis, keepdims=True)
    v = jnp.var(x, axis=axis, keepdims=True)
    return (x - m) / jnp.sqrt(v + eps)

def _scatter_add(tgt, idx, src, axis=0):
    return tgt.at[idx].add(src)

def _segment_sum(src, seg, n):
    return jax.ops.segment_sum(src, seg, n)
kernel_name = 'mk_decoder_preln_d2_seqx_r8_905611'

def setup_inputs(seed: int=0):
    np.random.seed(seed)
    _w = jnp.asarray

    def _rec_inputs():
        import jax
        import jax.numpy as jnp
        _rk = jax.random.key(seed)
        x = -0.0002928 + 1 * jax.random.normal(jax.random.fold_in(_rk, 1), (1, 1024, 128), jnp.float32)
        _lenS = 1024 - jax.random.randint(jax.random.fold_in(_rk, 7), (1,), 0, max(1, 1024 // 4) + 1, jnp.int32)
        _lenS2 = 6404 - jax.random.randint(jax.random.fold_in(_rk, 8), (1,), 0, max(1, 6404 // 4) + 1, jnp.int32)
        _ctx_1024P = jax.random.normal(jax.random.fold_in(_rk, 11), (1, 16, 128), jnp.float32)
        _ctx_1024c = jax.random.dirichlet(jax.random.fold_in(_rk, 511), 0.3 * jnp.ones((16,), jnp.float32), (1, 6404))
        _ctx_1024t = jnp.einsum('bsk,bkd->bsd', _ctx_1024c, _ctx_1024P)
        _ctx_1024t = _ctx_1024t * jax.lax.rsqrt(jnp.mean(jnp.square(_ctx_1024t)) + 1e-12) * 0.953939
        ctx_1024 = -1.39393e-06 + 0.999914 * (_ctx_1024t + 0.3 * jax.random.normal(jax.random.fold_in(_rk, 611), (1, 6404, 128), jnp.float32))
        _validS = jnp.arange(1024)[None, :] < _lenS[:, None]
        _validS2 = jnp.arange(6404)[None, :] < _lenS2[:, None]
        _causal = jnp.tril(jnp.ones((1024, 1024), dtype=bool))
        mask_Bx1xSxS2_ff0 = jnp.where(jnp.ones((1, 1, 1024, 6404), dtype=bool), 0.0, -1000000000.0).astype(jnp.float32)
        mask_1x1xSxS2_ik0 = jnp.where(jnp.broadcast_to(_validS2[0:1, None, None, :], (1, 1, 1024, 6404)), 0, 1).astype(jnp.int32)
        return (x, ctx_1024, mask_Bx1xSxS2_ff0, mask_1x1xSxS2_ik0)
    x, ctx_1024, mask_Bx1xSxS2_ff0, mask_1x1xSxS2_ik0 = _rec_inputs()

    def _L0_attn_setup():
        import jax, jax.numpy as jnp
        import numpy as np
        NUM_HEADS = 16
        EPS = 1e-05
        key = jax.random.key(seed)
        k1, k2, k3 = jax.random.split(key, 3)
        b, n, d = (2, 256, 128)
        x = jax.random.normal(k1, (b, n, d), dtype=jnp.float32)
        wqkv = jax.random.normal(k2, (d, 3 * d), dtype=jnp.float32) * (1.0 / np.sqrt(d))
        wo = jax.random.normal(k3, (d, d), dtype=jnp.float32) * (1.0 / np.sqrt(d))
        return {'x': x, 'wqkv': wqkv, 'wo': wo}
    _L0_attn_all = _L0_attn_setup()
    _L0_attn_in = {k: v for k, v in _L0_attn_all.items() if k in ('wqkv', 'wo')}
    del _L0_attn_all

    def _L0_xattn_setup():
        import jax, jax.numpy as jnp
        import numpy as np
        HIDDEN = 128
        HEADS = 16
        DPH = HIDDEN // HEADS
        B, F, T = (2, 256, 256)
        key = jax.random.key(seed)
        ks = jax.random.split(key, 7)
        s = 1.0 / np.sqrt(HIDDEN)
        return {'query_input': jax.random.normal(ks[0], (B, F, HIDDEN), jnp.float32), 'source_input': jax.random.normal(ks[1], (B, T, HIDDEN), jnp.float32), 'bias': jnp.zeros((B, 1, F, T), jnp.float32), 'wq': jax.random.normal(ks[2], (HIDDEN, HEADS, DPH), jnp.float32) * s, 'wk': jax.random.normal(ks[3], (HIDDEN, HEADS, DPH), jnp.float32) * s, 'wv': jax.random.normal(ks[4], (HIDDEN, HEADS, DPH), jnp.float32) * s, 'wo': jax.random.normal(ks[5], (HEADS, DPH, HIDDEN), jnp.float32) * s}
    _L0_xattn_all = _L0_xattn_setup()
    _L0_xattn_in = {k: v for k, v in _L0_xattn_all.items() if k in ('wq', 'wk', 'wv', 'wo')}
    del _L0_xattn_all

    def _L0_ffn_setup():
        import jax, jax.numpy as jnp
        import numpy as np
        H = 8
        KD = 128
        TOPK = 8
        NUM_KEYS = 32
        N_EXPERTS = NUM_KEYS * NUM_KEYS
        N_DIM = 128
        BN_EPS = 1e-05

        def gelu_new(x):
            c = jnp.sqrt(jnp.asarray(2.0 / jnp.pi, x.dtype))
            return 0.5 * x * (1.0 + jnp.tanh(c * (x + 0.044715 * x * x * x)))
        key = jax.random.key(seed)
        ks = jax.random.split(key, 5)
        b, s = (2, 128)
        x = jax.random.normal(ks[0], (b, s, N_DIM), dtype=jnp.float32)
        w_q = jax.random.normal(ks[1], (N_DIM, 2 * H * KD), dtype=jnp.float32) * 0.02
        bn_gamma = jnp.ones((2 * H * KD,), dtype=jnp.float32)
        bn_beta = jnp.zeros((2 * H * KD,), dtype=jnp.float32)
        keys = jax.random.normal(ks[2], (H, NUM_KEYS, 2, KD), dtype=jnp.float32) * 0.02
        down_embed = jax.random.normal(ks[3], (N_EXPERTS, N_DIM), dtype=jnp.float32) * 0.02
        up_embed = jax.random.normal(ks[4], (N_EXPERTS, N_DIM), dtype=jnp.float32) * 0.02
        return {'x': x, 'w_q': w_q, 'bn_gamma': bn_gamma, 'bn_beta': bn_beta, 'keys': keys, 'down_embed': down_embed, 'up_embed': up_embed}
    _L0_ffn_all = _L0_ffn_setup()
    _L0_ffn_in = {k: v for k, v in _L0_ffn_all.items() if k in ('w_q', 'bn_gamma', 'bn_beta', 'keys', 'down_embed', 'up_embed')}
    del _L0_ffn_all

    def _L1_attn_setup():
        import jax, jax.numpy as jnp
        import numpy as np
        BATCH, SEQ = (2, 256)
        D_MODEL, D_STATE, D_CONV, EXPAND = (128, 16, 4, 2)
        D_INNER = EXPAND * D_MODEL

        def _selective_scan(xc, delta, A, Bm, Cm):
            dA = jnp.exp(delta[..., None] * A)
            dBx = delta[..., None] * Bm[:, :, None, :] * xc[..., None]
            h0 = jnp.zeros((xc.shape[0], xc.shape[2], A.shape[1]), xc.dtype)

            def step(h, inp):
                dA_t, dBx_t, c_t = inp
                h = dA_t * h + dBx_t
                y = jnp.einsum('bdn,bn->bd', h, c_t)
                return (h, y)
            _, ys = jax.lax.scan(step, h0, (dA.swapaxes(0, 1), dBx.swapaxes(0, 1), Cm.swapaxes(0, 1)))
            return ys.swapaxes(0, 1)

        def _forward(x, W_in, conv_w, conv_b, W_xproj, w_dt, b_dt, A_log, D_param, W_out):
            xz = x @ W_in
            x_inner, z = jnp.split(xz, 2, axis=-1)
            xc = jax.lax.conv_general_dilated(x_inner.swapaxes(1, 2), conv_w, window_strides=(1,), padding=[(D_CONV - 1, 0)], dimension_numbers=('NCH', 'OIH', 'NCH'), feature_group_count=D_INNER) + conv_b[None, :, None]
            xc = jax.nn.silu(xc.swapaxes(1, 2))
            x_ssm = xc @ W_xproj
            delta_raw = x_ssm[..., :1]
            Bm = x_ssm[..., 1:1 + D_STATE]
            Cm = x_ssm[..., 1 + D_STATE:]
            delta = jax.nn.softplus(delta_raw * w_dt + b_dt)
            A = -jnp.exp(A_log)
            y = _selective_scan(xc, delta, A, Bm, Cm)
            y = y + xc * D_param
            y = y * jax.nn.silu(z)
            return y @ W_out
        key = jax.random.key(seed)
        ks = jax.random.split(key, 8)
        x = jax.random.normal(ks[0], (BATCH, SEQ, D_MODEL), jnp.float32)
        W_in = jax.random.normal(ks[1], (D_MODEL, 2 * D_INNER), jnp.float32) * D_MODEL ** (-0.5)
        conv_w = jax.random.normal(ks[2], (D_INNER, 1, D_CONV), jnp.float32) * D_CONV ** (-0.5)
        conv_b = jnp.zeros((D_INNER,), jnp.float32)
        W_xproj = jax.random.normal(ks[3], (D_INNER, 2 * D_STATE + 1), jnp.float32) * D_INNER ** (-0.5)
        w_dt = jax.random.normal(ks[4], (D_INNER,), jnp.float32)
        b_dt = jnp.zeros((D_INNER,), jnp.float32)
        A_log = jnp.log(jnp.tile(jnp.arange(1, D_STATE + 1, dtype=jnp.float32), (D_INNER, 1)))
        D_param = jnp.ones((D_INNER,), jnp.float32)
        W_out = jax.random.normal(ks[5], (D_INNER, D_MODEL), jnp.float32) * D_INNER ** (-0.5)
        return dict(x=x, W_in=W_in, conv_w=conv_w, conv_b=conv_b, W_xproj=W_xproj, w_dt=w_dt, b_dt=b_dt, A_log=A_log, D_param=D_param, W_out=W_out)
    _L1_attn_all = _L1_attn_setup()
    _L1_attn_in = {k: v for k, v in _L1_attn_all.items() if k in ('W_in', 'conv_w', 'conv_b', 'W_xproj', 'w_dt', 'b_dt', 'A_log', 'D_param', 'W_out')}
    del _L1_attn_all

    def _L1_xattn_setup():
        import jax, jax.numpy as jnp
        import numpy as np
        D_MODEL = 128
        NUM_HEADS = 16
        D_K = D_MODEL // NUM_HEADS
        B, S = (4, 256)
        NEG = -1000000000.0

        def _split_heads(x):
            b, s, _ = x.shape
            return x.reshape(b, s, NUM_HEADS, D_K).transpose(0, 2, 1, 3)
        key = jax.random.key(seed)
        ks = jax.random.split(key, 12)
        s = 1.0 / np.sqrt(D_MODEL)
        inp = {'q': jax.random.normal(ks[0], (B, S, D_MODEL), jnp.float32), 'k': jax.random.normal(ks[1], (B, S, D_MODEL), jnp.float32), 'v': jax.random.normal(ks[2], (B, S, D_MODEL), jnp.float32), 'mask': jnp.tril(jnp.ones((S, S), jnp.int32))[None, None], 'Wq': jax.random.normal(ks[3], (D_MODEL, D_MODEL), jnp.float32) * s, 'bq': jnp.zeros((D_MODEL,), jnp.float32), 'Wk': jax.random.normal(ks[4], (D_MODEL, D_MODEL), jnp.float32) * s, 'bk': jnp.zeros((D_MODEL,), jnp.float32), 'Wv': jax.random.normal(ks[5], (D_MODEL, D_MODEL), jnp.float32) * s, 'bv': jnp.zeros((D_MODEL,), jnp.float32), 'Wo': jax.random.normal(ks[6], (D_MODEL, D_MODEL), jnp.float32) * s, 'bo': jnp.zeros((D_MODEL,), jnp.float32)}
        return inp
    _L1_xattn_all = _L1_xattn_setup()
    _L1_xattn_in = {k: v for k, v in _L1_xattn_all.items() if k in ('Wq', 'bq', 'Wk', 'bk', 'Wv', 'bv', 'Wo', 'bo')}
    del _L1_xattn_all

    def _L1_ffn_setup():
        import jax, jax.numpy as jnp
        import numpy as np
        CAPACITY_FACTOR = 1.0
        key = jax.random.key(seed)
        ks = jax.random.split(key, 5)
        B, S, D, E, F = (2, 256, 128, 8, 512)
        x = jax.random.normal(ks[0], (B, S, D), dtype=jnp.float32)
        Ws = jax.random.normal(ks[1], (D, E), dtype=jnp.float32) * (1.0 / np.sqrt(D))
        bs = jnp.zeros((E,), dtype=jnp.float32)
        W1 = jax.random.normal(ks[2], (E, D, F), dtype=jnp.float32) * (1.0 / np.sqrt(D))
        b1 = jnp.zeros((E, F), dtype=jnp.float32)
        W2 = jax.random.normal(ks[3], (E, F, D), dtype=jnp.float32) * (1.0 / np.sqrt(F))
        b2 = jnp.zeros((E, D), dtype=jnp.float32)
        return {'x': x, 'Ws': Ws, 'bs': bs, 'W1': W1, 'b1': b1, 'W2': W2, 'b2': b2}
    _L1_ffn_all = _L1_ffn_setup()
    _L1_ffn_in = {k: v for k, v in _L1_ffn_all.items() if k in ('Ws', 'bs', 'W1', 'b1', 'W2', 'b2')}
    del _L1_ffn_all
    return {'x': x, 'ctx_1024': ctx_1024, 'mask_Bx1xSxS2_ff0': mask_Bx1xSxS2_ff0, 'mask_1x1xSxS2_ik0': mask_1x1xSxS2_ik0, 'L0_attn_wqkv': _L0_attn_in['wqkv'], 'L0_attn_wo': _L0_attn_in['wo'], 'L0_xattn_wq': _L0_xattn_in['wq'], 'L0_xattn_wk': _L0_xattn_in['wk'], 'L0_xattn_wv': _L0_xattn_in['wv'], 'L0_xattn_wo': _L0_xattn_in['wo'], 'L0_ffn_w_q': _L0_ffn_in['w_q'], 'L0_ffn_bn_gamma': _L0_ffn_in['bn_gamma'], 'L0_ffn_bn_beta': _L0_ffn_in['bn_beta'], 'L0_ffn_keys': _L0_ffn_in['keys'], 'L0_ffn_down_embed': _L0_ffn_in['down_embed'], 'L0_ffn_up_embed': _L0_ffn_in['up_embed'], 'L1_attn_W_in': _L1_attn_in['W_in'], 'L1_attn_conv_w': _L1_attn_in['conv_w'], 'L1_attn_conv_b': _L1_attn_in['conv_b'], 'L1_attn_W_xproj': _L1_attn_in['W_xproj'], 'L1_attn_w_dt': _L1_attn_in['w_dt'], 'L1_attn_b_dt': _L1_attn_in['b_dt'], 'L1_attn_A_log': _L1_attn_in['A_log'], 'L1_attn_D_param': _L1_attn_in['D_param'], 'L1_attn_W_out': _L1_attn_in['W_out'], 'L1_xattn_Wq': _L1_xattn_in['Wq'], 'L1_xattn_bq': _L1_xattn_in['bq'], 'L1_xattn_Wk': _L1_xattn_in['Wk'], 'L1_xattn_bk': _L1_xattn_in['bk'], 'L1_xattn_Wv': _L1_xattn_in['Wv'], 'L1_xattn_bv': _L1_xattn_in['bv'], 'L1_xattn_Wo': _L1_xattn_in['Wo'], 'L1_xattn_bo': _L1_xattn_in['bo'], 'L1_ffn_Ws': _L1_ffn_in['Ws'], 'L1_ffn_bs': _L1_ffn_in['bs'], 'L1_ffn_W1': _L1_ffn_in['W1'], 'L1_ffn_b1': _L1_ffn_in['b1'], 'L1_ffn_W2': _L1_ffn_in['W2'], 'L1_ffn_b2': _L1_ffn_in['b2']}

def reference(x, ctx_1024, mask_Bx1xSxS2_ff0, mask_1x1xSxS2_ik0, L0_attn_wqkv, L0_attn_wo, L0_xattn_wq, L0_xattn_wk, L0_xattn_wv, L0_xattn_wo, L0_ffn_w_q, L0_ffn_bn_gamma, L0_ffn_bn_beta, L0_ffn_keys, L0_ffn_down_embed, L0_ffn_up_embed, L1_attn_W_in, L1_attn_conv_w, L1_attn_conv_b, L1_attn_W_xproj, L1_attn_w_dt, L1_attn_b_dt, L1_attn_A_log, L1_attn_D_param, L1_attn_W_out, L1_xattn_Wq, L1_xattn_bq, L1_xattn_Wk, L1_xattn_bk, L1_xattn_Wv, L1_xattn_bv, L1_xattn_Wo, L1_xattn_bo, L1_ffn_Ws, L1_ffn_bs, L1_ffn_W1, L1_ffn_b1, L1_ffn_W2, L1_ffn_b2):
    import jax
    import jax.numpy as jnp

    def _L0_attn_ref(x, wqkv, wo):
        import jax, jax.numpy as jnp
        import numpy as np
        NUM_HEADS = 16
        EPS = 1e-05
        b, n, d = x.shape
        h = NUM_HEADS
        hd = d // h
        qkv = x @ wqkv
        q, k, v = jnp.split(qkv, 3, axis=-1)
        q = jax.nn.relu(q)
        k = jax.nn.relu(k)
        split_heads = lambda t: t.reshape(b, n, h, hd).transpose(0, 2, 1, 3)
        q, k, v = (split_heads(q), split_heads(k), split_heads(v))
        kv = jnp.cumsum(k[..., :, None] * v[..., None, :], axis=2)
        num = jnp.einsum('bhnd,bhnde->bhne', q, kv)
        k_sum = jnp.cumsum(k, axis=2)
        den = jnp.einsum('bhnd,bhnd->bhn', q, k_sum)[..., None] + EPS
        y = num / den
        y = y.transpose(0, 2, 1, 3).reshape(b, n, d)
        return y @ wo

    def _L0_xattn_ref(query_input, source_input, bias, wq, wk, wv, wo):
        import jax, jax.numpy as jnp
        import numpy as np
        HIDDEN = 128
        HEADS = 16
        DPH = HIDDEN // HEADS
        B, F, T = (2, 256, 256)
        q = jnp.einsum('bfh,hnd->bfnd', query_input, wq)
        k = jnp.einsum('bth,hnd->btnd', source_input, wk)
        v = jnp.einsum('bth,hnd->btnd', source_input, wv)
        q = q * DPH ** (-0.5)
        logits = jnp.einsum('btnd,bfnd->bnft', k, q) + bias
        weights = jax.nn.softmax(logits, axis=-1)
        attn = jnp.einsum('bnft,btnd->bfnd', weights, v)
        return jnp.einsum('bfnd,ndh->bfh', attn, wo)

    def _L0_ffn_ref(x, w_q, bn_gamma, bn_beta, keys, down_embed, up_embed):
        import jax, jax.numpy as jnp
        import numpy as np
        H = 8
        KD = 128
        TOPK = 8
        NUM_KEYS = 32
        N_EXPERTS = NUM_KEYS * NUM_KEYS
        N_DIM = 128
        BN_EPS = 1e-05

        def gelu_new(x):
            c = jnp.sqrt(jnp.asarray(2.0 / jnp.pi, x.dtype))
            return 0.5 * x * (1.0 + jnp.tanh(c * (x + 0.044715 * x * x * x)))
        b, n, d = x.shape
        q = jnp.einsum('bnd,de->bne', x, w_q)
        mean = jnp.mean(q, axis=(0, 1))
        var = jnp.var(q, axis=(0, 1))
        q = (q - mean) * jax.lax.rsqrt(var + BN_EPS) * bn_gamma + bn_beta
        q = q.reshape(b, n, 2, H, KD).transpose(2, 0, 1, 3, 4)
        sim = jnp.einsum('pbnhd,hkpd->pbnhk', q, keys)
        sx, ix = jax.lax.top_k(sim[0], TOPK)
        sy, iy = jax.lax.top_k(sim[1], TOPK)
        all_scores = (sx[..., :, None] + sy[..., None, :]).reshape(b, n, H, TOPK * TOPK)
        all_indices = (ix[..., :, None] * NUM_KEYS + iy[..., None, :]).reshape(b, n, H, TOPK * TOPK)
        scores, pk = jax.lax.top_k(all_scores, TOPK)
        indices = jnp.take_along_axis(all_indices, pk, axis=-1)
        wd = down_embed[indices]
        wu = up_embed[indices]
        h = jnp.einsum('bnd,bnhkd->bnhk', x, wd)
        h = gelu_new(h)
        h = jax.nn.softmax(scores, axis=-1) * h
        out = jnp.einsum('bnhk,bnhkd->bnd', h, wu)
        return out

    def _L1_attn_ref(x, W_in, conv_w, conv_b, W_xproj, w_dt, b_dt, A_log, D_param, W_out):
        import jax, jax.numpy as jnp
        import numpy as np
        BATCH, SEQ = (2, 256)
        D_MODEL, D_STATE, D_CONV, EXPAND = (128, 16, 4, 2)
        D_INNER = EXPAND * D_MODEL

        def _selective_scan(xc, delta, A, Bm, Cm):
            dA = jnp.exp(delta[..., None] * A)
            dBx = delta[..., None] * Bm[:, :, None, :] * xc[..., None]
            h0 = jnp.zeros((xc.shape[0], xc.shape[2], A.shape[1]), xc.dtype)

            def step(h, inp):
                dA_t, dBx_t, c_t = inp
                h = dA_t * h + dBx_t
                y = jnp.einsum('bdn,bn->bd', h, c_t)
                return (h, y)
            _, ys = jax.lax.scan(step, h0, (dA.swapaxes(0, 1), dBx.swapaxes(0, 1), Cm.swapaxes(0, 1)))
            return ys.swapaxes(0, 1)

        def _forward(x, W_in, conv_w, conv_b, W_xproj, w_dt, b_dt, A_log, D_param, W_out):
            xz = x @ W_in
            x_inner, z = jnp.split(xz, 2, axis=-1)
            xc = jax.lax.conv_general_dilated(x_inner.swapaxes(1, 2), conv_w, window_strides=(1,), padding=[(D_CONV - 1, 0)], dimension_numbers=('NCH', 'OIH', 'NCH'), feature_group_count=D_INNER) + conv_b[None, :, None]
            xc = jax.nn.silu(xc.swapaxes(1, 2))
            x_ssm = xc @ W_xproj
            delta_raw = x_ssm[..., :1]
            Bm = x_ssm[..., 1:1 + D_STATE]
            Cm = x_ssm[..., 1 + D_STATE:]
            delta = jax.nn.softplus(delta_raw * w_dt + b_dt)
            A = -jnp.exp(A_log)
            y = _selective_scan(xc, delta, A, Bm, Cm)
            y = y + xc * D_param
            y = y * jax.nn.silu(z)
            return y @ W_out
        return _forward(x, W_in, conv_w, conv_b, W_xproj, w_dt, b_dt, A_log, D_param, W_out)

    def _L1_xattn_ref(q, k, v, mask, Wq, bq, Wk, bk, Wv, bv, Wo, bo):
        import jax, jax.numpy as jnp
        import numpy as np
        D_MODEL = 128
        NUM_HEADS = 16
        D_K = D_MODEL // NUM_HEADS
        B, S = (4, 256)
        NEG = -1000000000.0

        def _split_heads(x):
            b, s, _ = x.shape
            return x.reshape(b, s, NUM_HEADS, D_K).transpose(0, 2, 1, 3)
        Q = _split_heads(q @ Wq.T + bq)
        K = _split_heads(k @ Wk.T + bk)
        V = _split_heads(v @ Wv.T + bv)
        scores = jnp.einsum('bhqd,bhkd->bhqk', Q, K) / jnp.sqrt(jnp.float32(D_K))
        scores = jnp.where(mask == 0, NEG, scores)
        weights = jax.nn.softmax(scores, axis=-1)
        context = jnp.einsum('bhqk,bhkd->bhqd', weights, V)
        context = context.transpose(0, 2, 1, 3).reshape(q.shape[0], q.shape[1], D_MODEL)
        return context @ Wo.T + bo

    def _L1_ffn_ref(x, Ws, bs, W1, b1, W2, b2):
        import jax, jax.numpy as jnp
        import numpy as np
        CAPACITY_FACTOR = 1.0
        B, S, D = x.shape
        E = Ws.shape[1]
        N = B * S
        k = int(CAPACITY_FACTOR * N / E)
        xf = x.reshape(N, D)
        route_prob = jax.nn.softmax(xf @ Ws + bs, axis=-1).T
        route_vals, routes = jax.lax.top_k(route_prob, k)
        xin = xf[routes]
        h = jax.nn.gelu(jnp.einsum('ekd,edf->ekf', xin, W1) + b1[:, None, :])
        out = jnp.einsum('ekf,efd->ekd', h, W2) + b2[:, None, :]
        out = out * route_vals[..., None]
        final = jnp.zeros((N, D), dtype=x.dtype).at[routes.reshape(-1)].add(out.reshape(-1, D))
        return final.reshape(B, S, D)
    x = x + _L0_attn_ref(_layernorm(x, axis=-1), L0_attn_wqkv, L0_attn_wo)
    x = x + _L0_xattn_ref(_layernorm(x, axis=-1), ctx_1024, mask_Bx1xSxS2_ff0, L0_xattn_wq, L0_xattn_wk, L0_xattn_wv, L0_xattn_wo)
    x = x + _L0_ffn_ref(_layernorm(x, axis=-1), L0_ffn_w_q, L0_ffn_bn_gamma, L0_ffn_bn_beta, L0_ffn_keys, L0_ffn_down_embed, L0_ffn_up_embed)
    x = x + _L1_attn_ref(_layernorm(x, axis=-1), L1_attn_W_in, L1_attn_conv_w, L1_attn_conv_b, L1_attn_W_xproj, L1_attn_w_dt, L1_attn_b_dt, L1_attn_A_log, L1_attn_D_param, L1_attn_W_out)
    x = x + _L1_xattn_ref(_layernorm(x, axis=-1), ctx_1024, ctx_1024, mask_1x1xSxS2_ik0, L1_xattn_Wq, L1_xattn_bq, L1_xattn_Wk, L1_xattn_bk, L1_xattn_Wv, L1_xattn_bv, L1_xattn_Wo, L1_xattn_bo)
    x = x + _L1_ffn_ref(_layernorm(x, axis=-1), L1_ffn_Ws, L1_ffn_bs, L1_ffn_W1, L1_ffn_b1, L1_ffn_W2, L1_ffn_b2)
    return x

_drawn_inputs = setup_inputs


def setup_inputs(seed=0):
    import zlib

    import numpy as np

    out = dict(_drawn_inputs(seed))
    spreads = {'L0_ffn_bn_gamma': (1.0, 0.6),
     'L0_ffn_bn_beta': (0.0, 0.8),
     'L1_attn_conv_b': (0.0, 0.1),
     'L1_attn_b_dt': (0.0, 0.304),
     'L1_attn_D_param': (1.0, 0.2),
     'L1_xattn_bq': (0.0, 0.398),
     'L1_xattn_bk': (0.0, 0.8),
     'L1_xattn_bv': (0.0, 0.1),
     'L1_xattn_bo': (0.0, 0.1),
     'L1_ffn_bs': (0.0, 0.329),
     'L1_ffn_b1': (0.0, 0.455),
     'L1_ffn_b2': (0.0, 0.296)}
    factors = {'L0_ffn_w_q': 8.0, 'L0_ffn_keys': 5.961, 'L0_ffn_down_embed': 8.0, 'L0_ffn_up_embed': 8.0}
    for name, (base, spread) in spreads.items():
        noise = np.random.default_rng([zlib.crc32(name.encode()), seed]).standard_normal(out[name].shape)
        drawn = base * np.exp(spread * noise) if base else spread * noise
        out[name] = jnp.asarray(drawn.astype(out[name].dtype))
    for name, factor in factors.items():
        out[name] = (out[name] * factor).astype(out[name].dtype)
    return out
```

```python
from contextlib import ExitStack

import concourse.bass as bass
from concourse import mybir

ALU = mybir.AluOpType
ACT = mybir.ActivationFunctionType
AX = mybir.AxisListType
F32 = mybir.dt.float32
BF16 = mybir.dt.bfloat16
I32 = mybir.dt.int32
U32 = mybir.dt.uint32

P = 128
N = 1024
D = 128
NT = N // P
H = 16
DH = D // H
T = 6404
LN_EPS = 1e-5
NEG = -1e9


def clear(nc, sems):
    with nc.Block() as between:
        @between.gpsimd
        def _(pool):
            for sem in sems:
                pool.sem_clear(sem)


class Stage:

    def __init__(self, nc, tag):
        self.nc, self.tag, self.memory, self.work, self.sems = nc, tag, ExitStack(), ExitStack(), []

    def __enter__(self):
        return self

    def __exit__(self, *e):
        self.work.close()
        if e[0] is None:
            clear(self.nc, self.sems)
        self.memory.close()

    def sb(self, name, shape, dt=F32):
        return self.memory.enter_context(self.nc.sbuf_tensor(f"{self.tag}_{name}", shape, dt))

    def ps(self, name, shape, dt=F32):
        return self.memory.enter_context(self.nc.psum_tensor(f"{self.tag}_{name}", shape, dt))

    def sem(self, name):
        self.sems.append(self.memory.enter_context(self.nc.semaphore(f"{self.tag}_{name}")))
        return self.sems[-1]

    def block(self):
        return self.work.enter_context(self.nc.Block())


class Chain:

    def __init__(self, eng, sem):
        self.eng, self.sem, self.n = eng, sem, 0

    def __call__(self, ins):
        self.n += 1
        ins.then_inc(self.sem, 1)
        self.eng.wait_ge(self.sem, self.n)


def row(ap, n):
    return ap.rearrange("(a n) -> a n", a=1)


def spread(ap, n):
    return row(ap, n).partition_broadcast(n)


def constants_stage(nc, x, x_sb, ident):
    with Stage(nc, "const") as st:
        x_loaded, ident_step = st.sem("x_loaded"), st.sem("ident_step")
        block = st.block()

        @block.sync
        def _(sp):
            sp.dma_start(x_sb[:], x[0].rearrange("(t p) d -> p t d", p=P)).then_inc(x_loaded, 16)
            sp.wait_ge(x_loaded, 16)

        @block.gpsimd
        def _(pool):
            pool.memset(ident[:], 0.0).then_inc(ident_step, 1)
            pool.wait_ge(ident_step, 1)
            pool.affine_select(out=ident[:], in_=ident[:], compare_op=ALU.not_equal, fill=1.0,
                               base=0, pattern=[[-1, P]], channel_multiplier=1).then_inc(ident_step, 1)
            pool.wait_ge(ident_step, 2)


def layernorm_stage(nc, tag, x_sb, xnT, ident):
    with Stage(nc, tag) as st:
        xn = st.sb("xn", [P, NT, D])
        stats = st.sb("stats", [P, NT, 6])
        mv = st.sb("mv", [P, NT, 2])
        var_eps = st.sb("var_eps", [P, NT])
        std = st.sb("std", [P, NT])
        rstd = st.sb("rstd", [P, NT])
        turned = st.ps("turned", [P, 2, 512])
        stats_done, moments_done = st.sem("stats_done"), st.sem("moments_done")
        var_ready, std_ready, rstd_ready = st.sem("var_ready"), st.sem("std_ready"), st.sem("rstd_ready")
        xn_ready, turned_ready, xnT_ready = st.sem("xn_ready"), st.sem("turned_ready"), st.sem("xnT_ready")
        block = st.block()

        @block.vector
        def _(dve):
            for t in range(NT):
                dve.bn_stats(stats[:, t, :], x_sb[:, t, :]).then_inc(stats_done, 1)
            for t in range(NT):
                dve.wait_ge(stats_done, t + 1)
                dve.bn_aggr(mv[:, t, :], stats[:, t, :]).then_inc(moments_done, 1)
            dve.wait_ge(moments_done, NT)
            dve.tensor_scalar(var_eps[:], mv[:, :, 1], LN_EPS, None, ALU.add).then_inc(var_ready, 1)
            dve.wait_ge(std_ready, 1)
            dve.reciprocal(rstd[:], std[:]).then_inc(rstd_ready, 1)
            dve.wait_ge(rstd_ready, 1)
            for t in range(NT):
                dve.tensor_scalar(xn[:, t, :], x_sb[:, t, :], mv[:, t, 0:1], rstd[:, t:t + 1],
                                  ALU.subtract, ALU.mult).then_inc(xn_ready, 1)

        @block.scalar
        def _(act):
            act.wait_ge(var_ready, 1)
            act.activation(std[:], var_eps[:], ACT.Sqrt).then_inc(std_ready, 1)
            for h in range(2):
                act.wait_ge(turned_ready, 4 * h + 4)
                act.activation(xnT[:, 512 * h:512 * h + 512], turned[:, h, :], ACT.Copy).then_inc(xnT_ready, 1)
            act.wait_ge(xnT_ready, 2)

        @block.tensor
        def _(pe):
            for t in range(NT):
                pe.wait_ge(xn_ready, t + 1)
                pe.transpose(turned[:, t // 4, (t % 4) * P:(t % 4 + 1) * P], xn[:, t, :],
                             ident[:]).then_inc(turned_ready, 1)


def linear_attention_stage(nc, wqkv, wo, x_sb, xnT, ident):
    C = P
    E = DH + 1
    with Stage(nc, "lin") as st:
        w_sb = st.sb("w_sb", [P, 3 * D])
        wo_sb = st.sb("wo_sb", [P, D])
        head_mask = st.sb("head_mask", [P, H])
        block_mask = st.sb("block_mask", [P, H, E])
        causal = st.sb("causal", [P, C])
        qT = st.sb("qT", [P, N])
        kT = st.sb("kT", [P, N])
        k_tok = st.sb("k_tok", [P, NT, D])
        v_tok = st.sb("v_tok", [P, NT, H, E])
        q_heads = st.sb("q_heads", [P, 2, H, C])
        scores = st.sb("scores", [P, H, C])
        state = st.sb("state", [P, H, E])
        fresh = st.sb("fresh", [P, H, E])
        den = st.sb("den", [P, H])
        rden = st.sb("rden", [P, H])
        y = st.sb("y", [P, D])
        yT = st.sb("yT", [P, D])
        ps_a = st.ps("ps_a", [P, 4, 512])
        ps_n = st.ps("ps_n", [P, 512])
        ps_s = st.ps("ps_s", [P, 512])
        ps_y = st.ps("ps_y", [P, 512])
        ps_o = st.ps("ps_o", [P, 512])
        w_loaded, wo_loaded, masks, ones_set = st.sem("w_loaded"), st.sem("wo_loaded"), st.sem("masks"), st.sem("ones_set")
        proj_ready, proj_used = st.sem("proj_ready"), st.sem("proj_used")
        q_split = st.sem("q_split")
        scores_ready, scores_masked = st.sem("scores_ready"), st.sem("scores_masked")
        sum_ready, num_ready = st.sem("sum_ready"), st.sem("num_ready")
        y_ready, yT_psum, yT_ready, out_ready = st.sem("y_ready"), st.sem("yT_psum"), st.sem("yT_ready"), st.sem("out_ready")
        state_ready, dve_step, out_added = st.sem("state_ready"), st.sem("dve_step"), st.sem("out_added")
        block = st.block()

        @block.sync
        def _(sp):
            sp.dma_start(w_sb[:], wqkv).then_inc(w_loaded, 16)
            sp.dma_start(wo_sb[:], wo).then_inc(wo_loaded, 16)

        @block.gpsimd
        def _(pool):
            pool.memset(head_mask[:], 1.0).then_inc(masks, 1)
            pool.memset(block_mask[:], 1.0).then_inc(masks, 1)
            pool.memset(causal[:], 1.0).then_inc(masks, 1)
            pool.memset(v_tok[:], 1.0).then_inc(ones_set, 1)
            pool.wait_ge(masks, 3)
            pool.affine_select(out=head_mask[:], in_=head_mask[:], compare_op=ALU.is_ge, fill=0.0, base=0,
                               pattern=[[-DH, H]], channel_multiplier=1).then_inc(masks, 1)
            pool.affine_select(out=block_mask[:], in_=block_mask[:], compare_op=ALU.is_ge, fill=0.0, base=0,
                               pattern=[[-DH, H], [0, E]], channel_multiplier=1).then_inc(masks, 1)
            pool.affine_select(out=causal[:], in_=causal[:], compare_op=ALU.is_ge, fill=0.0, base=0,
                               pattern=[[1, C]], channel_multiplier=-1).then_inc(masks, 1)
            pool.wait_ge(masks, 6)
            pool.affine_select(out=head_mask[:], in_=head_mask[:], compare_op=ALU.is_ge, fill=0.0,
                               base=DH - 1, pattern=[[DH, H]], channel_multiplier=-1).then_inc(masks, 1)
            pool.affine_select(out=block_mask[:], in_=block_mask[:], compare_op=ALU.is_ge, fill=0.0,
                               base=DH - 1, pattern=[[DH, H], [0, E]], channel_multiplier=-1).then_inc(masks, 1)
            pool.wait_ge(masks, 8)
            for c in range(NT):
                pool.wait_ge(proj_used, 4)
                if c >= 2:
                    pool.wait_ge(scores_ready, 4 * (c - 1))
                pool.tensor_tensor(q_heads[:, c % 2], qT[:, None, c * C:(c + 1) * C].to_broadcast([P, H, C]),
                                   head_mask[:, :, None].to_broadcast([P, H, C]), ALU.mult).then_inc(q_split, 1)

        @block.tensor
        def _(pe):
            pe.wait_ge(w_loaded, 16)
            for i in range(4):
                pe.matmul(ps_a[:, i, :], w_sb[:, (i // 2) * D:(i // 2 + 1) * D],
                          xnT[:, (i % 2) * 512:(i % 2) * 512 + 512], start=True, stop=True).then_inc(proj_ready, 1)
            for t in range(NT):
                if t % 2 == 0:
                    pe.wait_ge(proj_used, t // 2 + 1)
                pe.matmul(ps_a[:, t // 2, (t % 2) * 256:(t % 2) * 256 + 256], xnT[:, t * P:(t + 1) * P],
                          w_sb[:, D:3 * D], start=True, stop=True).then_inc(proj_ready, 1)
            pe.wait_ge(proj_used, 4 + 2 * NT)
            for c in range(NT):
                pe.wait_ge(q_split, c + 1)
                if c >= 1:
                    pe.wait_ge(scores_masked, 4 * c)
                for g in range(4):
                    mm = pe.matmul(ps_a[:, g, :], kT[:, c * C:(c + 1) * C], q_heads[:, c % 2, 4 * g:4 * g + 4, :],
                                   start=True, stop=True)
                    mm.then_inc(scores_ready, 1)
                pe.matmul(ps_s[:, 0:H * E], k_tok[:, c, :], v_tok[:, c, :, :], start=True,
                          stop=True).then_inc(sum_ready, 1)
                if c >= 1:
                    pe.wait_ge(y_ready, c)
                for h in range(H):
                    if h % 4 == 0:
                        pe.wait_ge(scores_masked, 4 * c + h // 4 + 1)
                    pe.matmul(ps_n[:, h * E:(h + 1) * E], scores[:, h, :], v_tok[:, c, h, :],
                              start=(h == 0), stop=False, skip_group_check=True)
                pe.wait_ge(state_ready, c + 1)
                pe.matmul(ps_n[:, 0:H * E], qT[:, c * C:(c + 1) * C], state[:], start=False,
                          stop=True, skip_group_check=True).then_inc(num_ready, 1)
                pe.wait_ge(y_ready, c + 1)
                pe.transpose(ps_y[:, 0:P], y[:], ident[:]).then_inc(yT_psum, 1)
                pe.wait_ge(yT_ready, c + 1)
                if c == 0:
                    pe.wait_ge(wo_loaded, 16)
                if c >= 1:
                    pe.wait_ge(out_added, c)
                pe.matmul(ps_o[:, 0:D], yT[:], wo_sb[:], start=True, stop=True).then_inc(out_ready, 1)

        @block.scalar
        def _(act):
            for i in range(4):
                act.wait_ge(proj_ready, i + 1)
                dst = qT if i < 2 else kT
                act.activation(dst[:, (i % 2) * 512:(i % 2) * 512 + 512], ps_a[:, i, :],
                               ACT.Relu).then_inc(proj_used, 1)
            act.wait_ge(ones_set, 1)
            for t in range(NT):
                act.wait_ge(proj_ready, 4 + 2 * (t // 2) + 2)
                bank = ps_a[:, t // 2, (t % 2) * 256:(t % 2) * 256 + 256]
                act.activation(k_tok[:, t, :], bank[:, 0:D], ACT.Relu).then_inc(proj_used, 1)
                act.activation(v_tok[:, t, :, 0:DH], bank[:, D:2 * D].rearrange("p (h e) -> p h e", h=H),
                               ACT.Copy).then_inc(proj_used, 1)
            for c in range(NT):
                act.wait_ge(yT_psum, c + 1)
                if c >= 1:
                    act.wait_ge(out_ready, c)
                act.activation(yT[:], ps_y[:, 0:P], ACT.Copy).then_inc(yT_ready, 1)

        @block.vector
        def _(dve):
            chain = Chain(dve, dve_step)
            dve.memset(state[:], 0.0).then_inc(state_ready, 1)
            dve.wait_ge(state_ready, 1)
            dve.wait_ge(masks, 8)
            for c in range(NT):
                for g in range(4):
                    dve.wait_ge(scores_ready, 4 * c + g + 1)
                    if c >= 1:
                        dve.wait_ge(num_ready, c)
                    dve.tensor_tensor(scores[:, 4 * g:4 * g + 4, :],
                                      ps_a[:, g, :].rearrange("p (h i) -> p h i", h=4),
                                      causal[:, None, :].to_broadcast([P, 4, C]), ALU.mult).then_inc(scores_masked, 1)
                dve.wait_ge(sum_ready, c + 1)
                sums = ps_s[:, 0:H * E].rearrange("p (h e) -> p h e", h=H)
                chain(dve.tensor_tensor(fresh[:], sums, block_mask[:], ALU.mult))
                dve.wait_ge(num_ready, c + 1)
                dve.tensor_tensor(state[:], state[:], fresh[:], ALU.add).then_inc(state_ready, 1)
                num = ps_n[:, 0:H * E].rearrange("p (h e) -> p h e", h=H)
                chain(dve.tensor_scalar(den[:], num[:, :, DH], LN_EPS, None, ALU.add))
                chain(dve.reciprocal(rden[:], den[:]))
                if c >= 1:
                    dve.wait_ge(yT_psum, c)
                dve.tensor_tensor(y[:].rearrange("p (h e) -> p h e", h=H), num[:, :, 0:DH],
                                  rden[:, :, None].to_broadcast([P, H, DH]), ALU.mult).then_inc(y_ready, 1)
                dve.wait_ge(out_ready, c + 1)
                dve.tensor_tensor(x_sb[:, c, :], x_sb[:, c, :], ps_o[:, 0:D], ALU.add).then_inc(out_added, 1)
            dve.wait_ge(out_added, NT)




PAIRS = H // 2
KT = -(-T // P)
T_LAST = T - (KT - 1) * P
VW = 2 * DH + 1
Q_PART = [0, 0, 1, 1, 0, 2]
K_PART = [0, 1, 0, 1, 2, 0]
NPROD = len(Q_PART)
ROW_M = NPROD * DH
HALF = 64




def kv_stage(nc, ctx, k_weights, v_weights, k_bias, v_bias, ident, k_scr, v_scr):
    CH = 512
    NC = -(-T // CH)
    W = [min(CH, T - c * CH) for c in range(NC)]
    L = 2
    with Stage(nc, "kv") as st:
        wk = [st.sb(f"wk{l}", [P, D]) for l in range(L)]
        wv = [st.sb(f"wv{l}", [P, D]) for l in range(L)]
        raw_k, raw_v = st.sb("raw_k", [P, D]), st.sb("raw_v", [P, D])
        bk = st.sb("bk", [P, 1])
        bv = st.sb("bv", [P, D])
        c_in = st.sb("c_in", [P, 2, 4, D])
        c_T = st.sb("c_T", [P, 2, CH])
        k_f = st.sb("k_f", [P, 2, L, CH])
        k_r = st.sb("k_r", [P, L, CH])
        k_p = st.sb("k_p", [P, 2, L, 3, CH], BF16)
        v_o = st.sb("v_o", [P, 2, L, 4, PAIRS, VW])
        ps_t = st.ps("ps_t", [P, 2, 512])
        ps_k = st.ps("ps_k", [P, L, 512])
        ps_v = st.ps("ps_v", [P, L, 512])
        ps_w = st.ps("ps_w", [P, 512])
        w_loaded, w_turned, w_ready = st.sem("w_loaded"), st.sem("w_turned"), st.sem("w_ready")
        c_loaded = [st.sem(f"c_loaded{i}") for i in range(2)]
        c_turned, cT_ready = st.sem("c_turned"), st.sem("cT_ready")
        k_ready, v_ready = st.sem("k_ready"), st.sem("v_ready")
        kf_ready, k1_ready, k2_ready, k3_ready = st.sem("kf_ready"), st.sem("k1_ready"), st.sem("k2_ready"), st.sem("k3_ready")
        r_ready, vo_ready, ones_set = st.sem("r_ready"), st.sem("vo_ready"), st.sem("ones_set")
        k_stored = [st.sem(f"k_stored{i}") for i in range(2)]
        v_stored = [st.sem(f"v_stored{i}") for i in range(2)]
        block = st.block()

        def tiles(c):
            return [(j, min(P, W[c] - j * P)) for j in range(-(-W[c] // P))]

        n_loads = [0, 0]
        loads_after = []
        for c in range(NC):
            n_loads[c % 2] += 1 if W[c] % P == 0 else 2
            loads_after.append(16 * n_loads[c % 2])
        stores_after, n_st = [], [0, 0]
        for c in range(NC):
            n_st[c % 2] += L * (1 if W[c] % P == 0 else 2)
            stores_after.append(16 * n_st[c % 2])

        def store_k(sp, c):
            for l in range(L):
                sp.wait_ge(k3_ready, L * c + l + 1)
                sp.wait_ge(k1_ready, L * c + l + 1)
                sp.wait_ge(k2_ready, L * c + l + 1)
                sp.dma_start(k_scr[l][:, :, c * CH:c * CH + W[c]].rearrange("a p t -> p a t"),
                             k_p[:, c % 2, l, :, 0:W[c]]).then_inc(k_stored[c % 2], 16)

        def store_v(act, c):
            full = W[c] // P
            for l in range(L):
                act.wait_ge(vo_ready, L * c + l + 1)
                act.dma_start(v_scr[l][:, 4 * c:4 * c + full, :, :], v_o[:, c % 2, l, 0:full]).then_inc(v_stored[c % 2], 16)
                if W[c] % P:
                    act.dma_start(v_scr[l][0:T_LAST, KT - 1, :, :], v_o[0:T_LAST, c % 2, l, full]).then_inc(v_stored[c % 2], 16)

        @block.sync
        def _(sp):
            sp.dma_start(wk[0][:], k_weights[0]).then_inc(w_loaded, 16)
            sp.dma_start(wv[0][:], v_weights[0]).then_inc(w_loaded, 16)
            sp.dma_start(raw_k[:], k_weights[1]).then_inc(w_loaded, 16)
            sp.dma_start(raw_v[:], v_weights[1]).then_inc(w_loaded, 16)
            sp.dma_start(bk[:], k_bias.rearrange("(p a) -> p a", a=1)).then_inc(w_loaded, 16)
            sp.dma_start(bv[:], row(v_bias, D).partition_broadcast(P)).then_inc(w_loaded, 16)
            for c in range(NC):
                if c >= 2:
                    sp.wait_ge(c_turned, c - 1)
                full = W[c] // P
                sp.dma_start(c_in[:, c % 2, 0:full, :],
                             ctx[c * CH:c * CH + full * P, :].rearrange("(j p) d -> p j d", p=P)
                             ).then_inc(c_loaded[c % 2], 16)
                if W[c] % P:
                    sp.dma_start(c_in[0:T_LAST, c % 2, full, :], ctx[T - T_LAST:T, :]).then_inc(c_loaded[c % 2], 16)
                if c >= 1:
                    store_k(sp, c - 1)
            store_k(sp, NC - 1)
            for i in range(2):
                sp.wait_ge(k_stored[i], 16 * L * len(range(i, NC, 2)))

        @block.tensor
        def _(pe):
            pe.wait_ge(w_loaded, 16 * 6)
            pe.transpose(ps_w[:, 0:P], raw_k[:], ident[:])
            pe.transpose(ps_w[:, P:2 * P], raw_v[:], ident[:]).then_inc(w_turned, 1)

            def turn(c):
                pe.wait_ge(c_loaded[c % 2], loads_after[c])
                if c >= 2:
                    pe.wait_ge(cT_ready, c - 1)
                for j, n in tiles(c):
                    mm = pe.transpose(ps_t[:, c % 2, j * P:j * P + n], c_in[0:n, c % 2, j, :], ident[0:n, 0:n])
                mm.then_inc(c_turned, 1)

            turn(0)
            pe.wait_ge(w_ready, 2)
            for c in range(NC):
                if c + 1 < NC:
                    turn(c + 1)
                pe.wait_ge(cT_ready, c + 1)
                for l in range(L):
                    if c >= 1:
                        pe.wait_ge(kf_ready, L * (c - 1) + l + 1)
                        pe.wait_ge(k1_ready, L * (c - 1) + l + 1)
                    pe.matmul(ps_k[:, l, 0:W[c]], wk[l][:], c_T[:, c % 2, 0:W[c]], start=True,
                              stop=True).then_inc(k_ready, 1)
                for l in range(L):
                    if c >= 1:
                        pe.wait_ge(vo_ready, L * (c - 1) + l + 1)
                    for j, n in tiles(c):
                        mm = pe.matmul(ps_v[0:n, l, j * D:(j + 1) * D], c_T[:, c % 2, j * P:j * P + n], wv[l][:],
                                       start=True, stop=True)
                    mm.then_inc(v_ready, 1)

        @block.scalar
        def _(act):
            act.wait_ge(w_turned, 1)
            act.activation(wk[1][:], ps_w[:, 0:P], ACT.Copy).then_inc(w_ready, 1)
            act.activation(wv[1][:], ps_w[:, P:2 * P], ACT.Copy).then_inc(w_ready, 1)
            for c in range(NC):
                w = W[c]
                act.wait_ge(c_turned, c + 1)
                if c >= 2:
                    act.wait_ge(v_ready, L * (c - 1))
                act.activation(c_T[:, c % 2, 0:w], ps_t[:, c % 2, 0:w], ACT.Copy).then_inc(cT_ready, 1)
                for l in range(L):
                    act.wait_ge(k_ready, L * c + l + 1)
                    if c >= 2:
                        act.wait_ge(k3_ready, L * (c - 2) + l + 1)
                        act.wait_ge(k_stored[c % 2], 16 * L * (c // 2))
                    bias = 0.0 if l == 0 else bk[:, 0:1]
                    act.activation(k_f[:, c % 2, l, 0:w], ps_k[:, l, 0:w], ACT.Identity,
                                   bias=bias).then_inc(kf_ready, 1)
                    act.activation(k_p[:, c % 2, l, 0, 0:w], ps_k[:, l, 0:w], ACT.Identity,
                                   bias=bias).then_inc(k1_ready, 1)
                if c >= 1:
                    store_v(act, c - 1)
            store_v(act, NC - 1)
            for i in range(2):
                act.wait_ge(v_stored[i], 16 * n_st[i])

        @block.gpsimd
        def _(pool):
            pool.memset(v_o[:], 1.0).then_inc(ones_set, 1)
            for c in range(NC):
                for l in range(L):
                    pool.wait_ge(r_ready, L * c + l + 1)
                    if c >= 2:
                        pool.wait_ge(k_stored[c % 2], 16 * L * (c // 2))
                    pool.tensor_copy(k_p[:, c % 2, l, 1, 0:W[c]], k_r[:, l, 0:W[c]]).then_inc(k2_ready, 1)

        @block.vector
        def _(dve):
            dve.wait_ge(w_loaded, 16 * 6)
            dve.wait_ge(ones_set, 1)
            for c in range(NC):
                w = W[c]
                for l in range(L):
                    dve.wait_ge(kf_ready, L * c + l + 1)
                    dve.wait_ge(k1_ready, L * c + l + 1)
                    if c >= 1:
                        dve.wait_ge(k3_ready, L * (c - 1) + l + 1)
                        dve.wait_ge(k2_ready, L * (c - 1) + l + 1)
                    dve.tensor_tensor(k_r[:, l, 0:w], k_f[:, c % 2, l, 0:w], k_p[:, c % 2, l, 0, 0:w],
                                      ALU.subtract).then_inc(r_ready, 1)
                for l in range(L):
                    dve.wait_ge(v_ready, L * c + l + 1)
                    if c >= 2:
                        dve.wait_ge(v_stored[c % 2], stores_after[c - 2])
                    whole = [(0, P, sum(n == P for _, n in tiles(c)))] + [(j, n, 1) for j, n in tiles(c) if n < P]
                    for k, (j, n, m) in enumerate(whole):
                        out = v_o[0:n, c % 2, l, j:j + m, :, 0:2 * DH]
                        src = ps_v[0:n, l, j * D:(j + m) * D].rearrange("p (m a e) -> p m a e", m=m, a=PAIRS)
                        if l == 0:
                            ins = dve.tensor_copy(out, src)
                        else:
                            ins = dve.tensor_tensor(out, src,
                                                    bv[0:n].rearrange("p (a e) -> p a e", a=PAIRS)[:, None]
                                                    .to_broadcast([n, m, PAIRS, 2 * DH]), ALU.add)
                        if k == len(whole) - 1:
                            ins.then_inc(vo_ready, 1)
                for l in range(L):
                    dve.wait_ge(k2_ready, L * c + l + 1)
                    dve.tensor_tensor(k_p[:, c % 2, l, 2, 0:w], k_r[:, l, 0:w], k_p[:, c % 2, l, 1, 0:w],
                                      ALU.subtract).then_inc(k3_ready, 1)


import numpy as np

QB = 256
NB = N // QB
QT = QB // P
GROUPS = 2
GP = PAIRS // GROUPS
STEPS = GROUPS * KT
MAXW = 1024
PIECES = [(0, 2048), (2048, 2048), (4096, T - 4096)]
OPS = [[(o, min(MAXW, w - o)) for o in range(0, w, MAXW)] for _, w in PIECES]
NOPS = sum(map(len, OPS))
PIECE_W = max(w for _, w in PIECES)
NPIECE = QT * len(PIECES)
LOW = -3.0e38
FOLD = 1024
FOLDS = [(qt * len(PIECES) + i, o, min(FOLD, w - o)) for qt in range(QT) for i, (_, w) in enumerate(PIECES)
         for o in range(0, w, FOLD)]
NFOLDS = len(FOLDS)
FOLD_END = [sum(f[0] <= n for f in FOLDS) for n in range(NPIECE)]


def after(eng, sem, k):
    if k > 0:
        eng.wait_ge(sem, k)


def span(b, start, width):
    if isinstance(b, int):
        return slice(b * QB + start, b * QB + start + width)
    return bass.ds(b * QB + start, width)


def q_stage(nc, tag, wq, bq, scale, xnT, ident, q_scr):
    with Stage(nc, tag) as st:
        w_sb = st.sb("w_sb", [P, D])
        raw = st.sb("raw", [P, D])
        b_sb = st.sb("b_sb", [P, 1])
        q_f = st.sb("q_f", [P, N])
        q_r = st.sb("q_r", [P, N])
        q_p = st.sb("q_p", [P, 3, N], BF16)
        ps = st.ps("ps", [P, 2, 512])
        ps_w = st.ps("ps_w", [P, 512])
        loaded, turned, w_ready, q_ready = st.sem("loaded"), st.sem("turned"), st.sem("w_ready"), st.sem("q_ready")
        f_ready, split, stored, b_ready = st.sem("f_ready"), st.sem("split"), st.sem("stored"), st.sem("b_ready")
        block = st.block()
        n_loads = 1 if bq is None else 2

        @block.sync
        def _(sp):
            sp.dma_start(w_sb[:] if bq is None else raw[:], wq).then_inc(loaded, 16)
            if bq is not None:
                sp.dma_start(b_sb[:], bq.rearrange("(p a) -> p a", a=1)).then_inc(loaded, 16)
            sp.wait_ge(split, 5)
            for j in range(NPROD):
                for a in range(2):
                    for pair in range(PAIRS):
                        r = 2 * DH * pair + DH * a
                        sp.dma_start(q_scr[a, DH * j:DH * j + DH, pair, :],
                                     q_p[r:r + DH, Q_PART[j], :]).then_inc(stored, 16)
            sp.wait_ge(stored, 16 * NPROD * H)

        @block.tensor
        def _(pe):
            pe.wait_ge(loaded, 16 * n_loads)
            if bq is not None:
                pe.transpose(ps_w[:, 0:P], raw[:], ident[:]).then_inc(turned, 1)
                pe.wait_ge(w_ready, 1)
            for i in range(2):
                pe.matmul(ps[:, i, :], w_sb[:], xnT[:, 512 * i:512 * i + 512], start=True,
                          stop=True).then_inc(q_ready, 1)

        @block.scalar
        def _(act):
            if bq is not None:
                act.wait_ge(turned, 1)
                act.activation(w_sb[:], ps_w[:, 0:P], ACT.Copy).then_inc(w_ready, 1)
                act.wait_ge(b_ready, 1)
            for i in range(2):
                act.wait_ge(q_ready, i + 1)
                act.activation(q_f[:, 512 * i:512 * i + 512], ps[:, i, :], ACT.Identity, scale=scale,
                               bias=0.0 if bq is None else b_sb[:, 0:1]).then_inc(f_ready, 1)

        @block.vector
        def _(dve):
            if bq is not None:
                dve.wait_ge(loaded, 16 * n_loads)
                dve.tensor_scalar(b_sb[:], b_sb[:], scale, None, ALU.mult).then_inc(b_ready, 1)
            chain = Chain(dve, split)
            dve.wait_ge(f_ready, 2)
            chain(dve.tensor_copy(q_p[:, 0, :], q_f[:]))
            chain(dve.tensor_tensor(q_r[:], q_f[:], q_p[:, 0, :], ALU.subtract))
            chain(dve.tensor_copy(q_p[:, 1, :], q_r[:]))
            chain(dve.tensor_tensor(q_f[:], q_r[:], q_p[:, 1, :], ALU.subtract))
            chain(dve.tensor_copy(q_p[:, 2, :], q_f[:]))


def even_rows_stage(nc, first_mask, rows_scr):
    F = 4
    hi, parts = NEG, []
    for _ in range(3):
        bits = int(np.float32(hi).view(np.uint32)) & 0xFFFF0000
        parts.append(float(np.uint32(bits).view(np.float32)))
        hi -= parts[-1]
    assert hi == 0.0
    with Stage(nc, "even") as st:
        mask = st.sb("mask", [F, T // F], I32)
        rows = st.sb("rows", [F, 5, T // F], BF16)
        loaded, made, stored = st.sem("loaded"), st.sem("made"), st.sem("stored")
        block = st.block()

        @block.sync
        def _(sp):
            sp.dma_start(mask[:], first_mask.rearrange("a (f t) -> (a f) t", f=F)).then_inc(loaded, 16)
            sp.wait_ge(made, 5)
            sp.dma_start(rows_scr.rearrange("r (f t) -> f r t", f=F), rows[:]).then_inc(stored, 16)
            sp.wait_ge(stored, 16)

        @block.vector
        def _(dve):
            dve.memset(rows[:, 0, :], 1.0).then_inc(made, 1)
            dve.wait_ge(loaded, 16)
            for i, part in enumerate(parts + [-parts[0]]):
                dve.tensor_scalar(rows[:, 1 + i, :], mask[:], 0, part, ALU.is_equal, ALU.mult).then_inc(made, 1)


def cross_attention_stage(nc, tag, bias, masked, wo, bo, x_sb, ident, q_scr, k_scr, v_scr, bias_scr, rows_scr):
    with Stage(nc, tag) as st:
        k_side = st.sb("k_side", [P, PAIRS, T], BF16)
        q_max = st.sb("q_max", [P, PAIRS, 2, QB], BF16)
        q_att = st.sb("q_att", [P, PAIRS, 2, QB], BF16)
        v_sb = st.sb("v_sb", [P, KT, PAIRS, VW])
        piece = st.sb("piece", [P, 2, PIECE_W])
        chunk = st.sb("chunk", [P, 3, QT, P])
        probs = st.sb("probs", [P, 3, 2, QB])
        part_max = st.sb("part_max", [P, QT, H, NOPS])
        neg_max = st.sb("neg_max", [P, QT, H])
        m_rest = st.sb("m_rest", [H, QT, 2, P])
        m_parts = st.sb("m_parts", [H, 3, QT, P], BF16)
        apart = st.sb("apart", [P, 2, FOLD], BF16)
        apart_sum = st.sb("apart_sum", [P, NFOLDS])
        apart_max = st.sb("apart_max", [P, 1])
        worst = st.sb("worst", [1, 1])
        uneven_f = st.sb("uneven_f", [1, 1])
        uneven = st.sb("uneven", [1, 1], I32)
        if masked:
            first_row = st.sb("first_row", [P, T], BF16)
            shut = st.sb("shut", [1, 1])
            ones_sb = st.sb("ones_sb", [1, QB])
            even_row = st.sb("even_row", [1, QB], BF16)
        summed = st.sb("summed", [P, 2, QT, P])
        recip = st.sb("recip", [P, 2, QT, GP])
        y = st.sb("y", [P, QT, PAIRS, 2, DH])
        yT = st.sb("yT", [P, QT, P])
        wo_sb = st.sb("wo_sb", [P, D])
        raw = st.sb("raw", [P, D])
        bo_sb = st.sb("bo_sb", [P, D])
        ps_max = st.ps("ps_max", [P, 2, MAXW])
        ps_att = st.ps("ps_att", [P, 3, 512])
        ps_acc = st.ps("ps_acc", [P, 512])

        units1 = [(qt, i, h, o, w) for qt in range(QT) for i in range(len(PIECES)) for h in range(H)
                  for o, w in OPS[i]]
        n_u1 = len(units1) + QT + 1
        piece_last = {}
        for n, (qt, i, *_r) in enumerate(units1):
            piece_last[qt * len(PIECES) + i] = n + 1
        units2 = [("exp", g, kt, j) for g in range(GROUPS) for kt in range(KT) for j in range(GP)]
        per_group = KT * GP
        LATE = 3 * GP
        units2 = (units2[:per_group + LATE] + [("sums", 0, 0, 0)] + units2[per_group + LATE:]
                  + [("sums", 1, 0, 0)] + [("turn", 0, qt, 0) for qt in range(QT)]
                  + [("out", 0, qt, 0) for qt in range(QT)])
        n_u2 = len(units2)
        n_exp = GROUPS * per_group
        nth = []
        seen = {}
        for k, *_r in units2:
            seen[k] = seen.get(k, 0) + 1
            nth.append(seen[k])

        EVERY = STEPS // NPIECE

        w_loaded, w_turned, w_ready, filled = st.sem("w_loaded"), st.sem("w_turned"), st.sem("w_ready"), st.sem("filled")
        first_in, shut_ready = st.sem("first_in"), st.sem("shut_ready")
        qk_loaded, bo_added = st.sem("qk_loaded"), st.sem("bo_added")
        scored1, maxed = st.sem("scored1"), st.sem("maxed")
        piece_in = [st.sem(f"piece_in{i}") for i in range(2)]
        piece_ready = st.sem("piece_ready")
        reduced, max_split = st.sem("reduced"), st.sem("max_split")
        apart_ready, folds = st.sem("apart_ready"), st.sem("folds")
        judged = st.sem("judged")
        m_stored, qm_in, q_in = st.sem("m_stored"), st.sem("qm_in"), st.sem("q_in")
        chunk_in = [st.sem(f"chunk_in{i}") for i in range(3)]
        chunk_ready, bias_in = st.sem("chunk_ready"), st.sem("bias_in")
        scored2, valued = st.sem("scored2"), st.sem("valued")
        read2 = {"exp": st.sem("exp_done"), "sums": st.sem("sums_read"), "turn": st.sem("turn_read"),
                 "out": st.sem("out_read")}
        copied, y_recip, y_half = st.sem("copied"), st.sem("y_recip"), st.sem("y_half")
        block_sems = [scored1, maxed, *piece_in, piece_ready, reduced, max_split,
                      apart_ready, folds, judged, m_stored, qm_in, q_in, bias_in, *chunk_in,
                      chunk_ready, scored2, valued, *read2.values(), copied, y_recip, y_half]

        def fold_after(k):
            n = FOLDS[k][0]
            start = FOLD_END[n - 1] if n else 0
            return int((n + (k - start + 1) / (FOLD_END[n] - start + 1)) / NPIECE * (n_exp - 10 * GP))

        def interleaved(first, second):
            n1, n2 = (n_u1 if first is not None else 0), (n_u2 if second is not None else 0)
            if not n2:
                return [(1, i) for i in range(n1)]
            out, done = [], 0
            for u in range(n2):
                out.append((2, u))
                want = min(n1, -(-(u + 1) * n1 // (n2 - 24)))
                out += [(1, i) for i in range(done, want)]
                done = want
            assert done == n1
            return out

        sums_at = [u for u, unit in enumerate(units2) if unit[0] == "sums"]
        step_end = {}
        for u, (kind, g, kt, j) in enumerate(units2):
            if kind == "exp":
                step_end[g * KT + kt] = u + 1

        block = nc.Block()
        with block:
            @block.sync
            def _(sp):
                sp.dma_start(wo_sb[:] if bo is None else raw[:], wo).then_inc(w_loaded, 16)
                if bo is not None:
                    sp.dma_start(bo_sb[:], row(bo, D).partition_broadcast(P)).then_inc(w_loaded, 16)
                for a in range(2):
                    for j in range(NPROD):
                        rows = slice(HALF * a + DH * j, HALF * a + DH * (j + 1))
                        src = k_scr[K_PART[j]].rearrange("(p a d) t -> a d p t", a=2, d=DH)[a]
                        sp.dma_start(k_side[rows, :, :], src).then_inc(qk_loaded, 16)
                    r = HALF * a + ROW_M
                    if masked:
                        sp.dma_start(k_side[r:r + 3, :, :], rows_scr[0:1, None, :].to_broadcast([3, PAIRS, T])).then_inc(qk_loaded, 16)
                        sp.dma_start(k_side[r + 3:r + 6, :, :], rows_scr[1:4, None, :].to_broadcast([3, PAIRS, T])).then_inc(qk_loaded, 16)
                        r += 6
                    rest = HALF * (a + 1) - r
                    sp.dma_start(k_side[r:r + rest, :, :], rows_scr[0:1, None, :].to_broadcast([rest, PAIRS, T])).then_inc(qk_loaded, 16)
                sp.dma_start(v_sb[:, 0:KT - 1], v_scr[:, 0:KT - 1]).then_inc(qk_loaded, 16)
                sp.dma_start(v_sb[0:T_LAST, KT - 1], v_scr[0:T_LAST, KT - 1]).then_inc(qk_loaded, 16)
                if masked:
                    sp.dma_start(first_row[:], rows_scr[4:5, :].to_broadcast([P, T])).then_inc(first_in, 16)
                    sp.wait_ge(first_in, 16)
                sp.wait_ge(qk_loaded, 16 * (2 * (NPROD + (3 if masked else 1)) + 2))

            @block.gpsimd
            def _(pool):
                pool.memset(q_max[:], 0.0).then_inc(filled, 1)
                pool.memset(q_att[:], 0.0).then_inc(filled, 1)
                pool.memset(summed[:], 0.0).then_inc(filled, 1)
                if masked:
                    pool.memset(ones_sb[:], 1.0).then_inc(filled, 1)

            @block.tensor
            def _(pe):
                if bo is not None:
                    pe.wait_ge(w_loaded, 32)
                    pe.transpose(ps_acc[:, 0:P], raw[:], ident[:]).then_inc(w_turned, 1)

            @block.scalar
            def _(act):
                if bo is not None:
                    act.wait_ge(w_turned, 1)
                    act.activation(wo_sb[:], ps_acc[:, 0:P], ACT.Copy).then_inc(w_ready, 1)

            @block.vector
            def _(dve):
                if bo is not None:
                    dve.wait_ge(w_loaded, 32)
                    for t in range(NT):
                        dve.tensor_tensor(x_sb[:, t, :], x_sb[:, t, :], bo_sb[:], ALU.add).then_inc(bo_added, 1)
                if masked:
                    dve.wait_ge(first_in, 16)
                    dve.tensor_reduce(shut[:], first_row[0:1, :], AX.X, ALU.min).then_inc(shut_ready, 1)

        def run_block(first, second):
            order = interleaved(first, second)
            block = nc.Block()
            with block:
                def by_flag(eng, program):
                    if second is None:
                        return program(False)
                    flag = eng.value_load(uneven[0:1, 0:1], min_val=0, max_val=1)
                    with eng.If(flag > 0):
                        program(True)
                    with eng.Else():
                        program(False)

                @block.sync
                def _(sp):
                    q_rows = ROW_M + (6 if masked else 3)

                    def load_piece(n):
                        if n >= 2:
                            sp.wait_ge(maxed, piece_last[n - 2])
                            sp.wait_ge(folds, FOLD_END[n - 2])
                        qt, i = divmod(n, len(PIECES))
                        o, w = PIECES[i]
                        dst = piece[:, n % 2, 0:w]
                        sp.dma_start(dst.bitcast(I32) if masked else dst,
                                     bias[span(first, qt * P, P), o:o + w]).then_inc(piece_in[n % 2], 16)

                    def fetch(s):
                        if s >= 3:
                            sp.wait_ge(scored2, step_end[s - 3])
                        g, kt = divmod(s, KT)
                        n = P if kt < KT - 1 else T_LAST
                        for qt in range(QT):
                            dst = chunk[:, s % 3, qt, 0:n]
                            sp.dma_start(dst.bitcast(I32) if masked else dst,
                                         bias_scr[qt * P:(qt + 1) * P, kt * P:kt * P + n]
                                         ).then_inc(chunk_in[s % 3], 16)

                    def program(uneven_block):
                        if second is not None:
                            for a in range(2):
                                sp.dma_start(q_att[HALF * a:HALF * a + q_rows, :, a, :],
                                             q_scr[a, 0:q_rows, :, span(second, 0, QB)]).then_inc(q_in, 16)
                        if first is not None:
                            for a in range(2):
                                sp.dma_start(q_max[HALF * a:HALF * a + ROW_M, :, a, :],
                                             q_scr[a, 0:ROW_M, :, span(first, 0, QB)]).then_inc(qm_in, 16)
                        pieces = list(range(NPIECE)) if first is not None else []
                        while pieces[0:1] in ([0], [1]):
                            load_piece(pieces.pop(0))
                        if uneven_block:
                            sp.dma_start(bias_scr, bias[span(second, 0, QB), :]).then_inc(bias_in, 16)
                            sp.wait_ge(bias_in, 16)
                            for s in range(STEPS):
                                fetch(s)
                                if pieces and s == (pieces[0] - 1) * EVERY + 6:
                                    load_piece(pieces.pop(0))
                        for n in pieces:
                            load_piece(n)
                        if second is not None:
                            sp.wait_ge(q_in, 32)

                    by_flag(sp, program)
                    if first is None:
                        return
                    sp.wait_ge(max_split, 4 * QT)
                    for a in range(2):
                        sp.dma_start(q_scr[a, ROW_M:ROW_M + 3, :, span(first, 0, QB)].rearrange("c p q -> p c q"),
                                     m_parts[a:H:2].rearrange("h a t q -> h a (t q)")).then_inc(m_stored, 16)
                    if masked:
                        sp.wait_ge(judged, 4)
                        for a in range(2):
                            sp.dma_start(q_scr[a:a + 1, ROW_M + 3:ROW_M + 6, :, span(first, 0, QB)].rearrange(
                                             "a c p q -> a (c p) q"),
                                         even_row[:, None, :].to_broadcast([1, 3 * PAIRS, QB])).then_inc(m_stored, 16)
                    sp.wait_ge(m_stored, 16 * (4 if masked else 2))

                @block.tensor
                def _(pe):
                    def max_unit(u):
                        after(pe, maxed, u - 1)
                        dst = ps_max[:, u % 2, :]
                        if u == n_u1 - 1:
                            pe.wait_ge(judged, 1)
                            pe.transpose(dst[0:1, 0:P], apart_max[:], ident[:]).then_inc(scored1, 1)
                            return
                        if u >= len(units1):
                            pe.wait_ge(reduced, 1)
                            pe.transpose(dst[0:H, 0:P], neg_max[:, u - len(units1), :], ident[:]).then_inc(scored1, 1)
                            return
                        qt, i, h, o, w = units1[u]
                        for c in range(0, w, 512):
                            n = min(512, w - c)
                            k0 = PIECES[i][0] + o + c
                            mm = pe.matmul(dst[:, c:c + n], q_max[:, h // 2, h % 2, qt * P:(qt + 1) * P],
                                           k_side[:, h // 2, k0:k0 + n], start=True, stop=True)
                        mm.then_inc(scored1, 1)

                    def scores(u, uneven_block):
                        kind, g, kt, j = units2[u]
                        if u >= 3:
                            pe.wait_ge(read2[units2[u - 3][0]], nth[u - 3])
                        if kind == "exp":
                            n = P if kt < KT - 1 else T_LAST
                            step = g * KT + kt
                            if uneven_block and j == 0 and masked:
                                pe.wait_ge(chunk_ready, step + 1)
                            elif uneven_block and j == 0:
                                pe.wait_ge(chunk_in[step % 3], 16 * QT * (step // 3 + 1))
                            dst = ps_att[0:n, u % 3, :].rearrange("p (a q) -> p a q", a=2)
                            for qt in range(QT if uneven_block else 0):
                                pe.matmul(dst[:, :, qt * P:(qt + 1) * P], chunk[:, step % 3, qt, 0:n],
                                          ident[:, None, :].to_broadcast([P, 2, P]), start=(qt == 0), stop=False,
                                          skip_group_check=True)
                            pair = GP * g + j
                            pe.matmul(dst, k_side[:, pair, kt * P:kt * P + n], q_att[:, pair, :, :],
                                      start=not uneven_block, stop=True, skip_group_check=True).then_inc(scored2, 1)
                        elif kind == "sums":
                            pe.wait_ge(copied, GP * (g + 1))
                            for i in range(2 * QT):
                                mm = pe.transpose(ps_att[:, u % 3, i * P:(i + 1) * P], summed[:, i // QT, i % QT, :],
                                                  ident[:])
                            mm.then_inc(scored2, 1)
                        elif kind == "turn":
                            pe.wait_ge(read2["sums"], GROUPS)
                            pe.transpose(ps_att[:, u % 3, 0:P], y[:, kt].rearrange("p a b e -> p (a b e)"),
                                         ident[:]).then_inc(scored2, 1)
                        else:
                            pe.wait_ge(read2["turn"], kt + 1)
                            pe.matmul(ps_att[:, u % 3, 0:D], yT[:, kt, :], wo_sb[:], start=True,
                                      stop=True).then_inc(scored2, 1)

                    def values(u):
                        kind, g, kt, j = units2[u]
                        n = P if kt < KT - 1 else T_LAST
                        pe.wait_ge(read2["exp"], nth[u])
                        if kt == 0 and j == 0 and g:
                            pe.wait_ge(copied, GP * g)
                        pe.matmul(ps_acc[32 * j:32 * j + VW, :], v_sb[0:n, kt, GP * g + j, :],
                                  probs[0:n, (nth[u] - 1) % 3].rearrange("p a q -> p (a q)"),
                                  start=(kt == 0), stop=(kt == KT - 1)).then_inc(valued, 1)

                    def program(uneven_block):
                        if first is not None:
                            pe.wait_ge(qm_in, 32)
                        if second is not None:
                            pe.wait_ge(q_in, 32)
                        behind = []
                        for which, u in order:
                            if which == 1:
                                max_unit(u)
                                continue
                            if units2[u][0] != "exp":
                                while behind:
                                    values(behind.pop(0))
                            scores(u, uneven_block)
                            if units2[u][0] == "exp":
                                behind.append(u)
                                if len(behind) > 2:
                                    values(behind.pop(0))

                    by_flag(pe, program)

                @block.scalar
                def _(act):
                    def sum_fold(k):
                        n, o, w = FOLDS[k]
                        if masked:
                            act.wait_ge(apart_ready, k + 1)
                        else:
                            act.wait_ge(piece_in[n % 2], 16 * (n // 2 + 1))
                        after(act, folds, k - 1)
                        if masked:
                            act.activation(apart[:, k % 2, 0:w], apart[:, k % 2, 0:w], ACT.Square, scale=1.0 / NEG,
                                           accum_out=apart_sum[:, k:k + 1]).then_inc(folds, 1)
                        else:
                            act.activation(apart[:, k % 2, 0:w], piece[:, n % 2, o:o + w], ACT.Abs,
                                           accum_out=apart_sum[:, k:k + 1]).then_inc(folds, 1)

                    if second is None:
                        for k in range(NFOLDS):
                            sum_fold(k)
                        return
                    k = 0
                    for u, (kind, g, kt, j) in enumerate(units2):
                        if first is not None and k < NFOLDS and u == fold_after(k):
                            sum_fold(k)
                            k += 1
                        if kind == "exp":
                            n = P if kt < KT - 1 else T_LAST
                            act.wait_ge(scored2, u + 1)
                            after(act, valued, nth[u] - 3)
                            act.activation(probs[0:n, (nth[u] - 1) % 3].rearrange("p a q -> p (a q)"),
                                           ps_att[0:n, u % 3, :], ACT.Exp).then_inc(read2["exp"], 1)
                        elif kind == "turn":
                            act.wait_ge(scored2, u + 1)
                            act.activation(yT[:, kt, :], ps_att[:, u % 3, 0:P], ACT.Copy).then_inc(read2["turn"], 1)

                @block.gpsimd
                def _(pool):
                    def convert(ap):
                        return pool.tensor_scalar(ap, ap.bitcast(I32), 0, NEG, ALU.is_equal, ALU.mult)

                    def convert_piece(n):
                        pool.wait_ge(piece_in[n % 2], 16 * (n // 2 + 1))
                        convert(piece[:, n % 2, 0:PIECES[n % len(PIECES)][1]]).then_inc(piece_ready, 1)

                    def set_apart(k):
                        n, o, w = FOLDS[k]
                        if k == FOLD_END[n - 1] or k == 0:
                            pool.wait_ge(piece_ready, n + 1)
                        after(pool, folds, k - 1)
                        c = PIECES[n % len(PIECES)][0] + o
                        pool.tensor_tensor(apart[:, k % 2, 0:w], piece[:, n % 2, o:o + w], first_row[:, c:c + w],
                                           ALU.add).then_inc(apart_ready, 1)

                    def program(uneven_block):
                        k = 0
                        for s in range(STEPS if uneven_block else 0):
                            if first is not None and (s == 0 or (s % EVERY == 6 and s // EVERY + 1 < NPIECE)):
                                convert_piece(0 if s == 0 else s // EVERY + 1)
                            if first is not None and k < NFOLDS and s == fold_after(k) // GP - 1:
                                set_apart(k)
                                k += 1
                            n = P if s % KT < KT - 1 else T_LAST
                            pool.wait_ge(chunk_in[s % 3], 16 * QT * (s // 3 + 1))
                            convert(chunk[:, s % 3, :, 0:n]).then_inc(chunk_ready, 1)
                        if not uneven_block and first is not None:
                            for k, (n, o, w) in enumerate(FOLDS):
                                if o == 0:
                                    convert_piece(n)
                                set_apart(k)

                    if masked:
                        by_flag(pool, program)

                @block.vector
                def _(dve):
                    def max_unit(u):
                        dve.wait_ge(scored1, u + 1)
                        if u == n_u1 - 1:
                            dve.tensor_reduce(worst[:], ps_max[0:1, u % 2, 0:P], AX.X, ALU.max).then_inc(maxed, 1)
                            dve.wait_ge(maxed, u + 1)
                            if masked:
                                dve.tensor_scalar(uneven_f[:], worst[:], shut[:], 0.5, ALU.max,
                                                  ALU.is_gt).then_inc(judged, 1)
                            else:
                                dve.tensor_scalar(uneven_f[:], worst[:], 0.0, None, ALU.is_gt).then_inc(judged, 1)
                            dve.wait_ge(judged, 2)
                            dve.tensor_copy(uneven[:], uneven_f[:]).then_inc(judged, 1)
                            if masked:
                                dve.tensor_scalar(even_row[:], ones_sb[:], uneven_f[:], 0.0, ALU.mult,
                                                  ALU.is_equal).then_inc(judged, 1)
                            return
                        if u >= len(units1):
                            qt = u - len(units1)
                            src = ps_max[0:H, u % 2, 0:P]
                            k = 4 * qt
                            dve.tensor_copy(m_parts[:, 0, qt, :], src).then_inc(max_split, 1)
                            dve.wait_ge(max_split, k + 1)
                            dve.tensor_tensor(m_rest[:, qt, 0], src, m_parts[:, 0, qt, :], ALU.subtract).then_inc(maxed, 1)
                            dve.wait_ge(maxed, u + 1)
                            dve.tensor_copy(m_parts[:, 1, qt, :], m_rest[:, qt, 0]).then_inc(max_split, 1)
                            dve.wait_ge(max_split, k + 2)
                            dve.tensor_tensor(m_rest[:, qt, 1], m_rest[:, qt, 0], m_parts[:, 1, qt, :],
                                              ALU.subtract).then_inc(max_split, 1)
                            dve.wait_ge(max_split, k + 3)
                            dve.tensor_copy(m_parts[:, 2, qt, :], m_rest[:, qt, 1]).then_inc(max_split, 1)
                            return
                        qt, i, h, o, w = units1[u]
                        n = qt * len(PIECES) + i
                        if h == 0 and o == 0:
                            if masked:
                                dve.wait_ge(piece_ready, n + 1)
                            else:
                                dve.wait_ge(piece_in[n % 2], 16 * (n // 2 + 1))
                        slot = sum(map(len, OPS[:i])) + o // MAXW
                        dve.tensor_tensor_reduce(ps_max[:, u % 2, 0:w], ps_max[:, u % 2, 0:w], piece[:, n % 2, o:o + w], 1.0,
                                                 LOW, ALU.add, ALU.max, part_max[:, qt, h, slot:slot + 1]).then_inc(maxed, 1)
                        if u == len(units1) - 1:
                            dve.wait_ge(maxed, u + 1)
                            dve.tensor_reduce(neg_max[:], part_max[:], AX.X, ALU.max, negate=True).then_inc(reduced, 1)
                            dve.wait_ge(folds, NFOLDS)
                            dve.tensor_reduce(apart_max[:], apart_sum[:], AX.X, ALU.max).then_inc(judged, 1)

                    def copy_sums(g):
                        if g:
                            dve.wait_ge(scored2, sums_at[g - 1] + 1)
                        dve.wait_ge(valued, per_group * (g + 1))
                        for j in range(GP):
                            dve.tensor_copy(summed[32 * j:32 * j + VW].rearrange("p a t q -> p (a t q)"),
                                            ps_acc[32 * j:32 * j + VW, :]).then_inc(copied, 1)

                    def second_unit(u):
                        kind, g, kt, j = units2[u]
                        bank = ps_att[:, u % 3, :]
                        if u == per_group + 2:
                            copy_sums(0)
                        if kind == "sums":
                            if g == 1:
                                copy_sums(1)
                            dve.wait_ge(scored2, u + 1)
                            cols = bank.rearrange("p (a t j r) -> p a t j r", a=2, t=QT, j=GP)
                            dve.reciprocal(recip[:], cols[:, :, :, :, 2 * DH]).then_inc(y_recip, 1)
                            dve.wait_ge(y_recip, g + 1)
                            dve.tensor_tensor(y[:, :, GP * g:GP * g + GP, 0, :], cols[:, 0, :, :, 0:DH],
                                              recip[:, 0, :, :, None].to_broadcast([P, QT, GP, DH]),
                                              ALU.mult).then_inc(y_half, 1)
                            dve.wait_ge(y_half, g + 1)
                            dve.tensor_tensor(y[:, :, GP * g:GP * g + GP, 1, :], cols[:, 1, :, :, DH:2 * DH],
                                              recip[:, 1, :, :, None].to_broadcast([P, QT, GP, DH]),
                                              ALU.mult).then_inc(read2["sums"], 1)
                        if kind == "out":
                            dve.wait_ge(scored2, u + 1)
                            if isinstance(second, int):
                                xs = x_sb[:, QT * second + kt, :]
                            else:
                                xs = x_sb[:, bass.ds(QT * second + kt, 1), :].rearrange("p o d -> p (o d)")
                            dve.tensor_tensor(xs, xs, bank[:, 0:D], ALU.add).then_inc(read2["out"], 1)

                    for which, u in order:
                        max_unit(u) if which == 1 else second_unit(u)

        run_block(0, None)
        with nc.Fori(0, NB - 1) as b:
            clear(nc, block_sems)
            run_block(b + 1, b)
        clear(nc, block_sems)
        run_block(None, NB - 1)


PH = 8
NK = 32
NE = NK * NK
ET = NE // P
TOPK = 8
BN_EPS = 1e-5


def product_key_stage(nc, w_q, gamma, beta, keys, down, up, x_sb, xnT, ident):
    SIDE = 2
    F = SIDE * PH
    POOL_HEADS = 3
    with Stage(nc, "pk") as st:
        wq_sb = st.sb("wq_sb", [P, F * P])
        g_sb, b_sb = st.sb("g_sb", [P, F]), st.sb("b_sb", [P, F])
        keys_in = st.sb("keys_in", [P, 4, D])
        keys_T = st.sb("keys_T", [P, PH, NK, SIDE])
        down_in = st.sb("down_in", [P, ET, D])
        down_T = st.sb("down_T", [P, ET, P])
        up_sb = st.sb("up_sb", [P, ET, D])
        q_T = st.sb("q_T", [P, F, N])
        gelu_T = st.sb("gelu_T", [P, ET, N])
        stats, mv = st.sb("stats", [P, F, 2, 6]), st.sb("mv", [P, F, 2])
        bn = st.sb("bn", [P, F, 4])
        sim = st.sb("sim", [P, 2, SIDE, PH, NK])
        top = st.sb("top", [P, SIDE, PH, TOPK])
        pair = st.sb("pair", [P, PH, TOPK, TOPK])
        best = st.sb("best", [P, 2, PH, TOPK])
        neg = st.sb("neg", [P, 2, PH])
        ex, z = st.sb("ex", [P, PH, TOPK]), st.sb("z", [P, PH])
        rz = st.sb("rz", [P, 2, PH])
        total = st.sb("total", [P, 3, NK, NK])
        expo = st.sb("expo", [P, 2, NE])
        weight = st.sb("weight", [P, 2, NE])
        diag = st.sb("diag", [P, 2, P])
        act_T = st.sb("act_T", [P, ET, P])
        banks = st.ps("banks", [P, 8, 512])
        s = {n: st.sem(n) for n in (
            "w_in", "k_in", "d_in", "u_in", "gb_in", "turned", "turned_out", "q_ready", "q_stats", "var", "root",
            "rroot", "scale", "shift0", "shift", "q_used", "h_ready", "gelu", "sim_ready", "sim_out", "top", "pair",
            "best", "neg", "exd", "ex", "z", "rz", "total_d", "total_p", "expo", "weight", "diag", "wT", "act_T",
            "out", "added")}
        block = st.block()

        def store_q(act, f):
            act.wait_ge(s["shift"], f + 1)
            act.activation(q_T[:, f, :], banks[:, 2 * (f % 3):2 * (f % 3) + 2, :].rearrange("p b c -> p (b c)"),
                           ACT.Identity, scale=bn[:, f, 2:3], bias=bn[:, f, 3:4]).then_inc(s["q_used"], 1)

        def sim_copy(act, t):
            act.wait_ge(s["sim_ready"], t + 1)
            if t >= 2:
                act.wait_ge(s["weight"], PH * (t - 1))
            act.activation(sim[:, t % 2].rearrange("p s h k -> p (s h k)"), banks[:, t % 2, :], ACT.Copy).then_inc(s["sim_out"], 1)

        def total_sem(t, h):
            if h < POOL_HEADS:
                return s["total_p"], POOL_HEADS * t + h + 1
            return s["total_d"], (PH - POOL_HEADS) * t + h - POOL_HEADS + 1

        def form_total(eng, t, h):
            n = PH * t + h
            if n >= 3:
                eng.wait_ge(s["weight"], n - 2)
            return eng.tensor_tensor(total[:, n % 3], sim[:, t % 2, 0, h, :, None].to_broadcast([P, NK, NK]),
                                     sim[:, t % 2, 1, h, None, :].to_broadcast([P, NK, NK]), ALU.add)

        @block.sync
        def _(sp):
            sp.dma_start(wq_sb[:], w_q).then_inc(s["w_in"], 16)
            sp.dma_start(down_in[:], down.rearrange("(t p) d -> p t d", p=P)).then_inc(s["d_in"], 16)
            sp.dma_start(up_sb[:], up.rearrange("(t p) d -> p t d", p=P)).then_inc(s["u_in"], 16)

        @block.scalar
        def _(act):
            act.dma_start(keys_in[:], keys.rearrange("h k s d -> (h k s) d").rearrange("(t p) d -> p t d", p=P)
                          ).then_inc(s["k_in"], 16)
            with nc.allow_non_contiguous_dma(reason="4096 scale and shift values, once"):
                act.dma_start(g_sb[:], gamma.rearrange("(f p) -> p f", p=P)).then_inc(s["gb_in"], 16)
                act.dma_start(b_sb[:], beta.rearrange("(f p) -> p f", p=P)).then_inc(s["gb_in"], 16)
            act.wait_ge(s["turned"], 1)
            act.activation(keys_T[:].rearrange("p h k s -> p (h k s)"), banks[:, 6, :], ACT.Copy).then_inc(s["turned_out"], 1)
            for i in range(2):
                act.wait_ge(s["turned"], 2 + i)
                act.activation(down_T[:, 4 * i:4 * i + 4, :].rearrange("p t e -> p (t e)"), banks[:, 7 - i, :],
                               ACT.Copy).then_inc(s["turned_out"], 1)
            for f in range(F):
                act.wait_ge(s["var"], f + 1)
                act.activation(bn[:, f, 1:2], bn[:, f, 0:1], ACT.Sqrt).then_inc(s["root"], 1)
                if f >= 1:
                    store_q(act, f - 1)
            store_q(act, F - 1)
            for i in range(2 * ET):
                act.wait_ge(s["h_ready"], i + 1)
                act.activation(gelu_T[:, i // 2, (i % 2) * 512:(i % 2) * 512 + 512], banks[:, i % 4, :],
                               ACT.Gelu_apprx_tanh).then_inc(s["gelu"], 1)
            for t in range(NT):
                if t == 0:
                    sim_copy(act, 0)
                if t + 1 < NT:
                    sim_copy(act, t + 1)
                act.wait_ge(s["exd"], t + 1)
                if t >= 1:
                    act.wait_ge(s["z"], t)
                act.activation(ex[:], ex[:], ACT.Exp).then_inc(s["ex"], 1)
                for h in range(PH):
                    n = PH * t + h
                    act.wait_ge(*total_sem(t, h))
                    if n >= 2:
                        act.wait_ge(s["weight"], n - 1)
                    act.activation(expo[:, n % 2, :], total[:, n % 3].rearrange("p i j -> p (i j)"), ACT.Exp,
                                   bias=neg[:, t % 2, h:h + 1]).then_inc(s["expo"], 1)

        @block.gpsimd
        def _(pool):
            for t in range(NT):
                pool.wait_ge(s["sim_out"], t + 1)
                for h in range(PH):
                    n = PH * t + h
                    if h < POOL_HEADS:
                        form_total(pool, t, h).then_inc(s["total_p"], 1)
                    if h == 0:
                        pool.wait_ge(s["rz"], t + 1)
                    if n >= 2:
                        pool.wait_ge(s["wT"], n - 1)
                    pool.tensor_scalar(diag[:, n % 2, :], ident[:], rz[:, t % 2, h:h + 1], None, ALU.mult).then_inc(s["diag"], 1)

        @block.tensor
        def _(pe):
            pe.wait_ge(s["k_in"], 16)
            for i in range(4):
                mm = pe.transpose(banks[:, 6, i * P:(i + 1) * P], keys_in[:, i, :], ident[:])
            mm.then_inc(s["turned"], 1)
            pe.wait_ge(s["d_in"], 16)
            for i in range(ET):
                if i == 4:
                    pe.wait_ge(s["turned_out"], 1)
                mm = pe.transpose(banks[:, 7 - i // 4, (i % 4) * P:(i % 4 + 1) * P], down_in[:, i, :], ident[:])
                if i % 4 == 3:
                    mm.then_inc(s["turned"], 1)
            pe.wait_ge(s["w_in"], 16)
            for f in range(F):
                if f >= 3:
                    pe.wait_ge(s["q_used"], f - 2)
                for c in range(2):
                    mm = pe.matmul(banks[:, 2 * (f % 3) + c, :], wq_sb[:, f * P:(f + 1) * P],
                                   xnT[:, 512 * c:512 * c + 512], start=True, stop=True)
                mm.then_inc(s["q_ready"], 1)
            pe.wait_ge(s["q_used"], F)
            pe.wait_ge(s["turned_out"], 3)
            for i in range(2 * ET):
                if i >= 4:
                    pe.wait_ge(s["gelu"], i - 3)
                pe.matmul(banks[:, i % 4, :], down_T[:, i // 2, :], xnT[:, (i % 2) * 512:(i % 2) * 512 + 512],
                          start=True, stop=True).then_inc(s["h_ready"], 1)
            pe.wait_ge(s["gelu"], 2 * ET)

            def similarities(t):
                if t >= 2:
                    pe.wait_ge(s["sim_out"], t - 1)
                for side in range(SIDE):
                    for h in range(PH):
                        c = (side * PH + h) * NK
                        mm = pe.matmul(banks[:, t % 2, c:c + NK], q_T[:, side * PH + h, t * P:(t + 1) * P],
                                       keys_T[:, h, :, side], start=True, stop=True)
                mm.then_inc(s["sim_ready"], 1)

            def up_product(t):
                pe.wait_ge(s["act_T"], t + 1)
                if t >= 1:
                    pe.wait_ge(s["added"], t)
                for i in range(ET):
                    mm = pe.matmul(banks[:, 6, 0:D], act_T[:, i, :], up_sb[:, i, :], start=(i == 0), stop=(i == ET - 1))
                mm.then_inc(s["out"], 1)

            similarities(0)
            pe.wait_ge(s["u_in"], 16)
            for t in range(NT):
                if t + 1 < NT:
                    similarities(t + 1)
                for h in range(PH):
                    n = PH * t + h
                    pe.wait_ge(s["weight"], n + 1)
                    pe.wait_ge(s["diag"], n + 1)
                    if h == 0 and t >= 2:
                        pe.wait_ge(s["act_T"], t - 1)
                    for i in range(ET):
                        mm = pe.matmul(banks[:, 2 + 2 * (t % 2) + i // 4, (i % 4) * P:(i % 4 + 1) * P],
                                       weight[:, n % 2, i * P:(i + 1) * P], diag[:, n % 2, :],
                                       start=(h == 0 and i % 4 == 0), stop=(h == PH - 1), skip_group_check=True)
                    mm.then_inc(s["wT"], 1)
                if t >= 1:
                    up_product(t - 1)
            up_product(NT - 1)

        @block.vector
        def _(dve):
            for f in range(F):
                dve.wait_ge(s["q_ready"], f + 1)
                for c in range(2):
                    dve.bn_stats(stats[:, f, c, :], banks[:, 2 * (f % 3) + c, :]).then_inc(s["q_stats"], 1)
                dve.wait_ge(s["q_stats"], 3 * f + 2)
                dve.bn_aggr(mv[:, f, :], stats[:, f].rearrange("p c k -> p (c k)")).then_inc(s["q_stats"], 1)
                dve.wait_ge(s["q_stats"], 3 * f + 3)
                dve.tensor_scalar(bn[:, f, 0:1], mv[:, f, 1:2], BN_EPS, None, ALU.add).then_inc(s["var"], 1)
                if f == 0:
                    dve.wait_ge(s["gb_in"], 32)
                dve.wait_ge(s["root"], f + 1)
                dve.reciprocal(bn[:, f, 1:2], bn[:, f, 1:2]).then_inc(s["rroot"], 1)
                dve.wait_ge(s["rroot"], f + 1)
                dve.tensor_tensor(bn[:, f, 2:3], bn[:, f, 1:2], g_sb[:, f:f + 1], ALU.mult).then_inc(s["scale"], 1)
                dve.wait_ge(s["scale"], f + 1)
                dve.tensor_tensor(bn[:, f, 3:4], mv[:, f, 0:1], bn[:, f, 2:3], ALU.mult).then_inc(s["shift0"], 1)
                dve.wait_ge(s["shift0"], f + 1)
                dve.tensor_tensor(bn[:, f, 3:4], b_sb[:, f:f + 1], bn[:, f, 3:4], ALU.subtract).then_inc(s["shift"], 1)

            def select(t):
                dve.wait_ge(s["sim_out"], t + 1)
                for side in range(SIDE):
                    for h in range(PH):
                        dve.max(top[:, side, h, :], sim[:, t % 2, side, h, :]).then_inc(s["top"], 1)
                dve.wait_ge(s["top"], F * (t + 1))
                dve.tensor_tensor(pair[:], top[:, 0, :, :, None].to_broadcast([P, PH, TOPK, TOPK]),
                                  top[:, 1, :, None, :].to_broadcast([P, PH, TOPK, TOPK]), ALU.add).then_inc(s["pair"], 1)
                dve.wait_ge(s["pair"], t + 1)
                if t >= 2:
                    dve.wait_ge(s["weight"], PH * (t - 1))
                for h in range(PH):
                    dve.max(best[:, t % 2, h, :], pair[:, h].rearrange("p a b -> p (a b)")).then_inc(s["best"], 1)
                dve.wait_ge(s["best"], PH * (t + 1))
                if t >= 2:
                    dve.wait_ge(s["expo"], PH * (t - 1))
                dve.tensor_scalar(neg[:, t % 2, :], best[:, t % 2, :, 0], -1.0, None, ALU.mult).then_inc(s["neg"], 1)
                dve.wait_ge(s["neg"], t + 1)
                dve.tensor_tensor(ex[:], best[:, t % 2], neg[:, t % 2, :, None].to_broadcast([P, PH, TOPK]),
                                  ALU.add).then_inc(s["exd"], 1)
                dve.wait_ge(s["ex"], t + 1)
                dve.tensor_reduce(z[:], ex[:], AX.X, ALU.add).then_inc(s["z"], 1)
                dve.wait_ge(s["z"], t + 1)
                if t >= 2:
                    dve.wait_ge(s["diag"], PH * (t - 1))
                dve.reciprocal(rz[:, t % 2, :], z[:]).then_inc(s["rz"], 1)

            def activate(t):
                dve.wait_ge(s["wT"], PH * (t + 1))
                if t >= 1:
                    dve.wait_ge(s["out"], t)
                dve.tensor_tensor(act_T[:], banks[:, 2 + 2 * (t % 2):4 + 2 * (t % 2), :]
                                  .rearrange("p b (i n) -> p (b i) n", i=4), gelu_T[:, :, t * P:(t + 1) * P],
                                  ALU.mult).then_inc(s["act_T"], 1)

            def add(t):
                dve.wait_ge(s["out"], t + 1)
                dve.tensor_tensor(x_sb[:, t, :], x_sb[:, t, :], banks[:, 6, 0:D], ALU.add).then_inc(s["added"], 1)

            def mask(t, h):
                n = PH * t + h
                dve.wait_ge(s["expo"], n + 1)
                if n >= 2:
                    dve.wait_ge(s["wT"], n - 1)
                dve.scalar_tensor_tensor(weight[:, n % 2, :], total[:, n % 3].rearrange("p i j -> p (i j)"),
                                         best[:, t % 2, h, TOPK - 1:TOPK], expo[:, n % 2, :], ALU.is_ge,
                                         ALU.mult).then_inc(s["weight"], 1)

            for t in range(NT):
                select(t)
                if t >= 1:
                    activate(t - 1)
                for h in range(PH):
                    if h >= POOL_HEADS:
                        form_total(dve, t, h).then_inc(s["total_d"], 1)
                        if h - 1 >= POOL_HEADS:
                            mask(t, h - 1)
                    else:
                        mask(t, h) if h < POOL_HEADS - 1 else None
                    if h == POOL_HEADS:
                        mask(t, POOL_HEADS - 1)
                mask(t, PH - 1)
                if t >= 1:
                    add(t - 1)
            activate(NT - 1)
            add(NT - 1)


DI = 256
CT = DI // P
NS = 16
TAPS = 4


def state_space_stage(nc, w_in, conv_w, conv_b, w_x, w_dt, b_dt, a_log, d_par, w_out, x_sb, xnT, ident, ssm_scr):
    R = 1 + 2 * NS
    with Stage(nc, "ssm") as st:
        w_sb = st.sb("w_sb", [P, 2 * DI])
        wx_sb, wo_sb = st.sb("wx_sb", [P, CT, R]), st.sb("wo_sb", [P, CT, D])
        cw, cb = st.sb("cw", [P, CT, TAPS]), st.sb("cb", [P, CT])
        wdt, bdt, dpar = st.sb("wdt", [P, CT]), st.sb("bdt", [P, CT]), st.sb("dpar", [P, CT])
        a_sb = st.sb("a_sb", [P, CT, NS])
        x_in = st.sb("x_in", [P, CT, TAPS - 1 + N])
        conv = st.sb("conv", [P, 2, N])
        xc, gate = st.sb("xc", [P, CT, N]), st.sb("gate", [P, CT, N])
        ssm_T = st.sb("ssm_T", [R, N])
        row_b = st.sb("row_b", [P, N])
        v, soft = st.sb("v", [P, N]), st.sb("soft", [P, N])
        delta, u = st.sb("delta", [P, CT, N]), st.sb("u", [P, CT, N])
        bc = st.sb("bc", [P, 2, 2, N])
        decay, drive = st.sb("decay", [P, 3, N]), st.sb("drive", [P, 3, N])
        state, read = st.sb("state", [P, 2, N]), st.sb("read", [P, 2, N])
        y = st.sb("y", [P, CT, N])
        banks = st.ps("banks", [P, 8, 512])
        s = {n: st.sem(n) for n in (
            "w_in", "p_in", "xz", "zeros", "xz_used", "conv", "xc", "gate", "x_ssm", "ssm_T", "ssm_out", "row", "v",
            "dv", "e1", "e2", "max0", "delta", "u", "a_exp", "a_neg", "decay", "drive", "state", "read", "summed",
            "skip", "y", "out", "added")}
        bc_in = [st.sem(f"bc_in{i}") for i in range(2)]
        block = st.block()
        N_PAR = 9

        @block.sync
        def _(sp):
            sp.dma_start(w_sb[:], w_in).then_inc(s["w_in"], 16)
            with nc.allow_non_contiguous_dma(reason="a few values per channel, once"):
                sp.dma_start(wx_sb[:], w_x.rearrange("(c p) r -> p c r", p=P)).then_inc(s["p_in"], 16)
                sp.dma_start(wo_sb[:], w_out.rearrange("(c p) r -> p c r", p=P)).then_inc(s["p_in"], 16)
                sp.dma_start(cw[:], conv_w.rearrange("(c p) a k -> p c (a k)", p=P)).then_inc(s["p_in"], 16)
                sp.dma_start(a_sb[:], a_log.rearrange("(c p) s -> p c s", p=P)).then_inc(s["p_in"], 16)
                for dst, src in ((cb, conv_b), (wdt, w_dt), (bdt, b_dt), (dpar, d_par)):
                    sp.dma_start(dst[:], src.rearrange("(c p) -> p c", p=P)).then_inc(s["p_in"], 16)
            sp.wait_ge(s["ssm_T"], 2)
            sp.dma_start(ssm_scr, ssm_T[:]).then_inc(s["ssm_out"], 16)
            sp.wait_ge(s["ssm_out"], 16)
            sp.dma_start(row_b[:], ssm_scr[0:1, :].partition_broadcast(P)).then_inc(s["row"], 16)
            for i in range(NS):
                if i >= 2:
                    sp.wait_ge(s["drive"], CT * (i - 1))
                    sp.wait_ge(s["read"], CT * (i - 1))
                sp.dma_start(bc[:, i % 2, 0, :], ssm_scr[1 + i:2 + i, :].partition_broadcast(P)).then_inc(bc_in[i % 2], 16)
                sp.dma_start(bc[:, i % 2, 1, :], ssm_scr[1 + NS + i:2 + NS + i, :].partition_broadcast(P)).then_inc(bc_in[i % 2], 16)

        @block.tensor
        def _(pe):
            pe.wait_ge(s["w_in"], 16)
            for f in range(2 * CT):
                for c in range(2):
                    mm = pe.matmul(banks[:, 2 * f + c, :], w_sb[:, f * P:(f + 1) * P], xnT[:, 512 * c:512 * c + 512],
                                   start=True, stop=True)
                mm.then_inc(s["xz"], 1)
            pe.wait_ge(s["p_in"], 16 * (N_PAR - 1))
            pe.wait_ge(s["xc"], CT)
            pe.wait_ge(s["xz_used"], CT)
            for c in range(2):
                for ct in range(CT):
                    mm = pe.matmul(banks[0:R, c, :], wx_sb[:, ct, :], xc[:, ct, 512 * c:512 * c + 512],
                                   start=(ct == 0), stop=(ct == CT - 1))
                mm.then_inc(s["x_ssm"], 1)
            pe.wait_ge(s["gate"], CT)
            pe.wait_ge(s["ssm_T"], 2)
            for i in range(NS):
                for ct in range(CT):
                    k = CT * i + ct
                    pe.wait_ge(s["read"], k + 1)
                    for c in range(2):
                        mm = pe.matmul(banks[:, 4 + 2 * ct + c, :], ident[:], read[:, k % 2, 512 * c:512 * c + 512],
                                       start=(i == 0), stop=(i == NS - 1), skip_group_check=True)
                    mm.then_inc(s["summed"], 1)
            pe.wait_ge(s["y"], CT)
            for t in range(NT):
                for ct in range(CT):
                    mm = pe.matmul(banks[:, t // 4, (t % 4) * D:(t % 4 + 1) * D], y[:, ct, t * P:(t + 1) * P],
                                   wo_sb[:, ct, :], start=(ct == 0), stop=(ct == CT - 1))
                mm.then_inc(s["out"], 1)

        @block.scalar
        def _(act):
            act.wait_ge(s["p_in"], 16 * (N_PAR - 1))
            for ct in range(CT):
                act.wait_ge(s["xz"], ct + 1)
                act.activation(x_in[:, ct, TAPS - 1:], banks[:, 2 * ct:2 * ct + 2, :].rearrange("p b n -> p (b n)"),
                               ACT.Copy).then_inc(s["xz_used"], 1)
            for ct in range(CT):
                act.wait_ge(s["xz"], CT + ct + 1)
                act.activation(gate[:, ct, :], banks[:, 2 * (CT + ct):2 * (CT + ct) + 2, :].rearrange("p b n -> p (b n)"),
                               ACT.Silu).then_inc(s["gate"], 1)
            for ct in range(CT):
                act.wait_ge(s["conv"], TAPS * (ct + 1))
                act.activation(xc[:, ct, :], conv[:, ct, :], ACT.Silu).then_inc(s["xc"], 1)
            for c in range(2):
                act.wait_ge(s["x_ssm"], c + 1)
                act.activation(ssm_T[:, 512 * c:512 * c + 512], banks[0:R, c, :], ACT.Copy).then_inc(s["ssm_T"], 1)
            act.activation(a_sb[:], a_sb[:], ACT.Exp).then_inc(s["a_exp"], 1)
            for ct in range(CT):
                act.wait_ge(s["dv"], 2 * ct + 2)
                act.activation(soft[:], soft[:], ACT.Exp, scale=-1.0).then_inc(s["e1"], 1)
                act.wait_ge(s["e1"], ct + 1)
                act.activation(soft[:], soft[:], ACT.Ln, bias=1.0).then_inc(s["e2"], 1)
            act.wait_ge(s["a_neg"], 1)
            for i in range(NS):
                for ct in range(CT):
                    k = CT * i + ct
                    if k >= 3:
                        act.wait_ge(s["state"], k - 2)
                    act.wait_ge(s["delta"], ct + 1)
                    act.activation(decay[:, k % 3, :], delta[:, ct, :], ACT.Exp, scale=a_sb[:, ct, i:i + 1]).then_inc(s["decay"], 1)

        @block.gpsimd
        def _(pool):
            pool.memset(x_in[:, :, 0:TAPS - 1], 0.0).then_inc(s["zeros"], 1)
            for i in range(NS):
                for ct in range(CT):
                    k = CT * i + ct
                    if k >= 3:
                        pool.wait_ge(s["state"], k - 2)
                    if ct == 0:
                        pool.wait_ge(bc_in[i % 2], 32 * (i // 2 + 1))
                    pool.wait_ge(s["u"], ct + 1)
                    pool.tensor_tensor(drive[:, k % 3, :], u[:, ct, :], bc[:, i % 2, 0, :], ALU.mult).then_inc(s["drive"], 1)

        @block.vector
        def _(dve):
            dve.wait_ge(s["p_in"], 16 * (N_PAR - 1))
            dve.wait_ge(s["zeros"], 1)
            for ct in range(CT):
                dve.wait_ge(s["xz_used"], ct + 1)
                dve.tensor_scalar(conv[:, ct, :], x_in[:, ct, 0:N], cw[:, ct, 0:1], cb[:, ct:ct + 1], ALU.mult,
                                  ALU.add).then_inc(s["conv"], 1)
                for k in range(1, TAPS):
                    dve.wait_ge(s["conv"], TAPS * ct + k)
                    dve.scalar_tensor_tensor(conv[:, ct, :], x_in[:, ct, k:k + N], cw[:, ct, k:k + 1], conv[:, ct, :],
                                             ALU.mult, ALU.add).then_inc(s["conv"], 1)
            dve.wait_ge(s["a_exp"], 1)
            dve.tensor_scalar(a_sb[:], a_sb[:], -1.0, None, ALU.mult).then_inc(s["a_neg"], 1)
            dve.wait_ge(s["row"], 16)
            for ct in range(CT):
                if ct >= 1:
                    dve.wait_ge(s["delta"], ct)
                dve.tensor_scalar(v[:], row_b[:], wdt[:, ct:ct + 1], bdt[:, ct:ct + 1], ALU.mult, ALU.add).then_inc(s["dv"], 1)
                dve.wait_ge(s["dv"], 2 * ct + 1)
                dve.scalar_tensor_tensor(soft[:], v[:], -1.0, v[:], ALU.mult, ALU.max).then_inc(s["dv"], 1)
                dve.wait_ge(s["e2"], ct + 1)
                dve.scalar_tensor_tensor(delta[:, ct, :], v[:], 0.0, soft[:], ALU.max, ALU.add).then_inc(s["delta"], 1)
                dve.wait_ge(s["delta"], ct + 1)
                dve.wait_ge(s["xc"], ct + 1)
                dve.tensor_tensor(u[:, ct, :], delta[:, ct, :], xc[:, ct, :], ALU.mult).then_inc(s["u"], 1)
            for i in range(NS):
                for ct in range(CT):
                    k = CT * i + ct
                    dve.wait_ge(s["decay"], k + 1)
                    dve.wait_ge(s["drive"], k + 1)
                    if k >= 2:
                        dve.wait_ge(s["read"], k - 1)
                    dve.tensor_tensor_scan(state[:, k % 2, :], decay[:, k % 3, :], drive[:, k % 3, :], 0.0,
                                           ALU.mult, ALU.add).then_inc(s["state"], 1)
                    dve.wait_ge(bc_in[i % 2], 32 * (i // 2 + 1))
                    dve.wait_ge(s["state"], k + 1)
                    if k >= 2:
                        dve.wait_ge(s["summed"], k - 1)
                    dve.tensor_tensor(read[:, k % 2, :], state[:, k % 2, :], bc[:, i % 2, 1, :], ALU.mult).then_inc(s["read"], 1)
            for ct in range(CT):
                dve.wait_ge(s["summed"], CT * NS)
                dve.scalar_tensor_tensor(y[:, ct, :], xc[:, ct, :], dpar[:, ct:ct + 1],
                                         banks[:, 4 + 2 * ct:6 + 2 * ct, :].rearrange("p b n -> p (b n)"), ALU.mult,
                                         ALU.add).then_inc(s["skip"], 1)
                dve.wait_ge(s["skip"], ct + 1)
                dve.wait_ge(s["gate"], ct + 1)
                dve.tensor_tensor(y[:, ct, :], y[:, ct, :], gate[:, ct, :], ALU.mult).then_inc(s["y"], 1)
            for g in range(2):
                dve.wait_ge(s["out"], 4 * (g + 1))
                xs = x_sb[:, 4 * g:4 * g + 4, :]
                dve.tensor_tensor(xs, xs, banks[:, g, :].rearrange("p (t d) -> p t d", t=4), ALU.add).then_inc(s["added"], 1)


EX = 8
FF = 512
FT = FF // P
CAP = N // EX


def expert_choice_stage(nc, ws, bs, w1, b1, w2, b2, x_sb, xnT, ident):
    TAKEN = -1.0
    with Stage(nc, "moe") as st:
        ws_sb, bs_sb = st.sb("ws_sb", [P, EX]), st.sb("bs_sb", [P, EX])
        w1_sb, w2_sb = st.sb("w1_sb", [P, 2, FF]), st.sb("w2_sb", [P, 2, FT, D])
        b1_sb, b2_sb = st.sb("b1_sb", [P, EX, FT]), st.sb("b2_sb", [EX, D])
        logit = st.sb("logit", [P, NT, EX])
        top, total, rtotal = st.sb("top", [P, NT]), st.sb("total", [P, NT]), st.sb("rtotal", [P, NT])
        prob_T, left = st.sb("prob_T", [EX, N]), st.sb("left", [EX, N])
        eight = st.sb("eight", [EX, CAP // 8, 8])
        gate_T = st.sb("gate_T", [EX, N])
        gate = st.sb("gate", [P, NT, EX])
        hid = st.sb("hid", [P, 2, FT, N])
        banks = st.ps("banks", [P, 8, 512])
        s = {n: st.sem(n) for n in (
            "s_in", "bs_in", "b_in", "logits", "step", "exp", "prob", "probT", "probT_out", "left", "gateT", "gate",
            "gate_out", "hid_ps", "hid", "out", "added")}
        w_in = [st.sem(f"w_in{i}") for i in range(2)]
        block = st.block()

        @block.sync
        def _(sp):
            sp.dma_start(ws_sb[:], ws).then_inc(s["s_in"], 16)
            sp.dma_start(bs_sb[:], row(bs, EX).partition_broadcast(P)).then_inc(s["bs_in"], 16)
            with nc.allow_non_contiguous_dma(reason="4096 bias values, once"):
                sp.dma_start(b1_sb[:], b1.rearrange("e (f p) -> p e f", p=P)).then_inc(s["b_in"], 16)
            sp.dma_start(b2_sb[:], b2).then_inc(s["b_in"], 16)
            for e in range(EX):
                if e >= 2:
                    sp.wait_ge(s["out"], 2 * (e - 1))
                sp.dma_start(w1_sb[:, e % 2, :], w1[e]).then_inc(w_in[e % 2], 16)
                sp.dma_start(w2_sb[:, e % 2], w2[e].rearrange("(f p) d -> p f d", p=P)).then_inc(w_in[e % 2], 16)

        @block.tensor
        def _(pe):
            pe.wait_ge(s["s_in"], 16)
            for t in range(NT):
                mm = pe.matmul(banks[:, 0, t * EX:(t + 1) * EX], xnT[:, t * P:(t + 1) * P], ws_sb[:], start=True, stop=True)
            mm.then_inc(s["logits"], 1)
            pe.wait_ge(s["prob"], 1)
            for t in range(NT):
                mm = pe.transpose(banks[0:EX, 1 + t // 4, (t % 4) * P:(t % 4 + 1) * P], logit[:, t, :], ident[:])
            mm.then_inc(s["probT"], 1)

            def hidden(e, k):
                n = 2 * FT * e + k
                f, c = k // 2, k % 2
                if n >= 3:
                    pe.wait_ge(s["hid"], n - 2)
                else:
                    pe.wait_ge(s["probT_out"], 1)
                pe.matmul(banks[:, 1 + n % 3, :], w1_sb[:, e % 2, f * P:(f + 1) * P], xnT[:, 512 * c:512 * c + 512],
                          start=True, stop=True).then_inc(s["hid_ps"], 1)

            def output(e, half):
                n = 2 * e + half
                if n >= 2:
                    pe.wait_ge(s["added"], 4 * (n - 1))
                pe.wait_ge(s["hid"], 2 * FT * (e + 1))
                for t in range(4 * half, 4 * half + 4):
                    for f in range(FT):
                        mm = pe.matmul(banks[:, 4 + n % 2, (t % 4) * D:(t % 4 + 1) * D], hid[:, e % 2, f, t * P:(t + 1) * P],
                                       w2_sb[:, e % 2, f, :], start=(f == 0), stop=(f == FT - 1))
                mm.then_inc(s["out"], 1)

            for e in range(EX):
                pe.wait_ge(w_in[e % 2], 32 * (e // 2 + 1))
                for k in range(2 * FT):
                    hidden(e, k)
                if e == 0:
                    pe.wait_ge(s["gateT"], 1)
                    for t in range(NT):
                        mm = pe.transpose(banks[:, 6, t * EX:(t + 1) * EX], gate_T[:, t * P:(t + 1) * P], ident[0:EX, 0:EX])
                    mm.then_inc(s["gate"], 1)
                output(e, 0)
                output(e, 1)
            pe.wait_ge(s["b_in"], 32)
            for g in range(2):
                pe.wait_ge(s["added"], 4 * (2 * EX - 1 + g))
                for t in range(4 * g, 4 * g + 4):
                    mm = pe.matmul(banks[:, 4 + g, (t % 4) * D:(t % 4 + 1) * D], gate_T[:, t * P:(t + 1) * P], b2_sb[:],
                                   start=True, stop=True)
                mm.then_inc(s["out"], 1)

        @block.scalar
        def _(act):
            act.wait_ge(s["step"], 3)
            act.activation(logit[:], logit[:], ACT.Exp).then_inc(s["exp"], 1)
            act.wait_ge(s["probT"], 1)
            act.activation(prob_T[:], banks[0:EX, 1:3, :].rearrange("p b n -> p (b n)"), ACT.Copy).then_inc(s["probT_out"], 1)
            act.wait_ge(s["b_in"], 32)
            for e in range(EX):
                for k in range(2 * FT):
                    n = 2 * FT * e + k
                    f, c = k // 2, k % 2
                    act.wait_ge(s["hid_ps"], n + 1)
                    if e >= 2 and k == 0:
                        act.wait_ge(s["out"], 2 * (e - 1))
                    act.activation(hid[:, e % 2, f, 512 * c:512 * c + 512], banks[:, 1 + n % 3, :], ACT.Gelu_apprx_tanh,
                                   bias=b1_sb[:, e, f:f + 1]).then_inc(s["hid"], 1)

        @block.vector
        def _(dve):
            chain = Chain(dve, s["step"])
            wide = [P, NT, EX]
            dve.wait_ge(s["logits"], 1)
            dve.wait_ge(s["bs_in"], 16)
            chain(dve.tensor_tensor(logit[:], banks[:, 0, 0:NT * EX].rearrange("p (t e) -> p t e", t=NT),
                                    bs_sb[:, None, :].to_broadcast(wide), ALU.add))
            chain(dve.tensor_reduce(top[:], logit[:], AX.X, ALU.max))
            chain(dve.tensor_tensor(logit[:], logit[:], top[:, :, None].to_broadcast(wide), ALU.subtract))
            dve.wait_ge(s["exp"], 1)
            chain(dve.tensor_reduce(total[:], logit[:], AX.X, ALU.add))
            chain(dve.reciprocal(rtotal[:], total[:]))
            dve.tensor_tensor(logit[:], logit[:], rtotal[:, :, None].to_broadcast(wide), ALU.mult).then_inc(s["prob"], 1)
            dve.wait_ge(s["probT_out"], 1)
            for r in range(CAP // 8):
                src = prob_T if r == 0 else left
                dve.max(eight[:, r, :], src[:]).then_inc(s["left"], 1)
                dve.wait_ge(s["left"], 2 * r + 1)
                dve.match_replace(left[:], eight[:, r, :], src[:], TAKEN).then_inc(s["left"], 1)
                dve.wait_ge(s["left"], 2 * r + 2)
            dve.scalar_tensor_tensor(gate_T[:], left[:], TAKEN, prob_T[:], ALU.is_equal, ALU.mult).then_inc(s["gateT"], 1)
            dve.wait_ge(s["gate"], 1)
            dve.tensor_copy(gate[:].rearrange("p t e -> p (t e)"), banks[:, 6, 0:NT * EX]).then_inc(s["gate_out"], 1)
            dve.wait_ge(s["gate_out"], 1)
            for e in range(EX):
                for half in range(2):
                    n = 2 * e + half
                    dve.wait_ge(s["out"], n + 1)
                    if n >= 2:
                        dve.wait_ge(s["added"], 4 * (n - 1))
                    for t in range(4 * half, 4 * half + 4):
                        dve.scalar_tensor_tensor(x_sb[:, t, :], banks[:, 4 + n % 2, (t % 4) * D:(t % 4 + 1) * D],
                                                 gate[:, t, e:e + 1], x_sb[:, t, :], ALU.mult, ALU.add).then_inc(s["added"], 1)
            for g in range(2):
                dve.wait_ge(s["out"], 2 * EX + g + 1)
                dve.wait_ge(s["added"], 4 * (2 * EX - 1 + g))
                xs = x_sb[:, 4 * g:4 * g + 4, :]
                dve.tensor_tensor(xs, xs, banks[:, 4 + g, :].rearrange("p (t d) -> p t d", t=4), ALU.add).then_inc(s["added"], 4)



def decoder_program(nc, out, **a):
    x_sb = nc.alloc_sbuf_tensor("x_sb", [P, NT, D], F32)
    ident = nc.alloc_sbuf_tensor("ident", [P, P], F32)
    xnT = nc.alloc_sbuf_tensor("xnT", [P, N], F32)
    k_scr = [nc.dram_tensor(f"k_scr{l}", [3, P, T], BF16).ap() for l in range(2)]
    v_scr = [nc.dram_tensor(f"v_scr{l}", [P, KT, PAIRS, VW], F32).ap() for l in range(2)]
    q_scr = [nc.dram_tensor(f"q_scr{l}", [2, ROW_M + 6, PAIRS, N], BF16).ap() for l in range(2)]
    bias_scr = [nc.dram_tensor(f"bias_scr{l}", [QB, T], F32 if l == 0 else I32).ap() for l in range(2)]
    rows_scr = nc.dram_tensor("rows_scr", [5, T], BF16).ap()
    ssm_scr = nc.dram_tensor("ssm_scr", [1 + 2 * NS, N], F32).ap()

    def flat_heads(w):
        return w.rearrange("a h e -> a (h e)")

    constants_stage(nc, a["x"], x_sb, ident)
    kv_stage(nc, a["ctx_1024"][0], [flat_heads(a["L0_xattn_wk"]), a["L1_xattn_Wk"]],
             [flat_heads(a["L0_xattn_wv"]), a["L1_xattn_Wv"]], a["L1_xattn_bk"], a["L1_xattn_bv"], ident, k_scr, v_scr)

    even_rows_stage(nc, a["mask_1x1xSxS2_ik0"][0, 0, 0:1, :], rows_scr)

    layernorm_stage(nc, "ln0", x_sb, xnT, ident)
    linear_attention_stage(nc, a["L0_attn_wqkv"], a["L0_attn_wo"], x_sb, xnT, ident)
    layernorm_stage(nc, "ln1", x_sb, xnT, ident)
    q_stage(nc, "q0", flat_heads(a["L0_xattn_wq"]), None, DH ** -0.5, xnT, ident, q_scr[0])
    cross_attention_stage(nc, "xa0", a["mask_Bx1xSxS2_ff0"][0, 0], False,
                          a["L0_xattn_wo"].rearrange("h e d -> (h e) d"), None, x_sb, ident, q_scr[0], k_scr[0],
                          v_scr[0], bias_scr[0], rows_scr)
    layernorm_stage(nc, "ln2", x_sb, xnT, ident)
    product_key_stage(nc, a["L0_ffn_w_q"], a["L0_ffn_bn_gamma"], a["L0_ffn_bn_beta"], a["L0_ffn_keys"],
                      a["L0_ffn_down_embed"], a["L0_ffn_up_embed"], x_sb, xnT, ident)

    layernorm_stage(nc, "ln3", x_sb, xnT, ident)
    state_space_stage(nc, *[a["L1_attn_" + n] for n in ("W_in", "conv_w", "conv_b", "W_xproj", "w_dt", "b_dt",
                                                        "A_log", "D_param", "W_out")], x_sb, xnT, ident, ssm_scr)
    layernorm_stage(nc, "ln4", x_sb, xnT, ident)
    q_stage(nc, "q1", a["L1_xattn_Wq"], a["L1_xattn_bq"], DH ** -0.5, xnT, ident, q_scr[1])
    cross_attention_stage(nc, "xa1", a["mask_1x1xSxS2_ik0"][0, 0], True, a["L1_xattn_Wo"], a["L1_xattn_bo"], x_sb,
                          ident, q_scr[1], k_scr[1], v_scr[1], bias_scr[1], rows_scr)
    layernorm_stage(nc, "ln5", x_sb, xnT, ident)
    expert_choice_stage(nc, *[a["L1_ffn_" + n] for n in ("Ws", "bs", "W1", "b1", "W2", "b2")], x_sb, xnT, ident)

    with Stage(nc, "store") as st:
        stored = st.sem("stored")
        block = st.block()

        @block.sync
        def _(sp):
            sp.dma_start(out[0].rearrange("(t p) d -> p t d", p=P), x_sb[:]).then_inc(stored, 16)
            sp.wait_ge(stored, 16)


INPUTS = (["x", "ctx_1024", "mask_Bx1xSxS2_ff0", "mask_1x1xSxS2_ik0", "L0_attn_wqkv", "L0_attn_wo"]
          + ["L0_xattn_" + n for n in ("wq", "wk", "wv", "wo")]
          + ["L0_ffn_" + n for n in ("w_q", "bn_gamma", "bn_beta", "keys", "down_embed", "up_embed")]
          + ["L1_attn_" + n for n in ("W_in", "conv_w", "conv_b", "W_xproj", "w_dt", "b_dt", "A_log", "D_param", "W_out")]
          + ["L1_xattn_" + n for n in ("Wq", "bq", "Wk", "bk", "Wv", "bv", "Wo", "bo")]
          + ["L1_ffn_" + n for n in ("Ws", "bs", "W1", "b1", "W2", "b2")])


def kernel(**inputs):
    import numpy as np
    import concourse.bacc as bacc
    from concourse.bass_utils import run_bass_kernel_spmd

    nc = bacc.Bacc("TRN2", target_bir_lowering=False, num_devices=1)
    arrays, aps = {}, {}
    for name in INPUTS:
        a = np.ascontiguousarray(inputs[name])
        arrays["in_" + name] = a
        aps[name] = nc.dram_tensor("in_" + name, a.shape, mybir.dt.from_np(a.dtype), kind="ExternalInput").ap()
    out = nc.dram_tensor("out", [1, N, D], F32, kind="ExternalOutput").ap()
    decoder_program(nc, out, **aps)
    r = run_bass_kernel_spmd(nc, [arrays], core_ids=[0])
    return r.results[0]["out"]
```

```python
from contextlib import ExitStack

import concourse.bass as bass
from concourse import mybir

ALU = mybir.AluOpType
ACT = mybir.ActivationFunctionType
AX = mybir.AxisListType
F32 = mybir.dt.float32
BF16 = mybir.dt.bfloat16
I32 = mybir.dt.int32
U32 = mybir.dt.uint32

P = 128
N = 1024
D = 128
NT = N // P
H = 16
DH = D // H
T = 6404
LN_EPS = 1e-5
NEG = -1e9


def clear(nc, sems):
    with nc.Block() as between:
        @between.gpsimd
        def _(pool):
            for sem in sems[0::3]:
                pool.sem_clear(sem)

        @between.vector
        def _(dve):
            for sem in sems[1::3]:
                dve.sem_clear(sem)

        @between.scalar
        def _(act):
            for sem in sems[2::3]:
                act.sem_clear(sem)


class Stage:

    def __init__(self, nc, tag):
        self.nc, self.tag, self.memory, self.work, self.sems = nc, tag, ExitStack(), ExitStack(), []

    def __enter__(self):
        return self

    def __exit__(self, *e):
        self.work.close()
        if e[0] is None:
            clear(self.nc, self.sems)
        self.memory.close()

    def sb(self, name, shape, dt=F32):
        return self.memory.enter_context(self.nc.sbuf_tensor(f"{self.tag}_{name}", shape, dt))

    def ps(self, name, shape, dt=F32):
        return self.memory.enter_context(self.nc.psum_tensor(f"{self.tag}_{name}", shape, dt))

    def sem(self, name):
        self.sems.append(self.memory.enter_context(self.nc.semaphore(f"{self.tag}_{name}")))
        return self.sems[-1]

    def block(self):
        return self.work.enter_context(self.nc.Block())


class Chain:

    def __init__(self, eng, sem):
        self.eng, self.sem, self.n = eng, sem, 0

    def __call__(self, ins):
        self.n += 1
        ins.then_inc(self.sem, 1)
        self.eng.wait_ge(self.sem, self.n)


def row(ap, n):
    return ap.rearrange("(a n) -> a n", a=1)


def spread(ap, n):
    return row(ap, n).partition_broadcast(n)


def constants_stage(nc, x, x_sb, ident):
    with Stage(nc, "const") as st:
        x_loaded, ident_step = st.sem("x_loaded"), st.sem("ident_step")
        block = st.block()

        @block.sync
        def _(sp):
            sp.dma_start(x_sb[:], x[0].rearrange("(t p) d -> p t d", p=P)).then_inc(x_loaded, 16)
            sp.wait_ge(x_loaded, 16)

        @block.gpsimd
        def _(pool):
            pool.memset(ident[:], 0.0).then_inc(ident_step, 1)
            pool.wait_ge(ident_step, 1)
            pool.affine_select(out=ident[:], in_=ident[:], compare_op=ALU.not_equal, fill=1.0,
                               base=0, pattern=[[-1, P]], channel_multiplier=1).then_inc(ident_step, 1)
            pool.wait_ge(ident_step, 2)


def layernorm_stage(nc, tag, x_sb, xnT, ident, beside=None):
    with Stage(nc, tag) as st:
        xn = st.sb("xn", [P, NT, D])
        stats = st.sb("stats", [P, NT, 6])
        mv = st.sb("mv", [P, NT, 2])
        var_eps = st.sb("var_eps", [P, NT])
        std = st.sb("std", [P, NT])
        rstd = st.sb("rstd", [P, NT])
        turned = st.ps("turned", [P, 2, 512])
        stats_done, moments_done = st.sem("stats_done"), st.sem("moments_done")
        var_ready, std_ready, rstd_ready = st.sem("var_ready"), st.sem("std_ready"), st.sem("rstd_ready")
        xn_ready, turned_ready, xnT_ready = st.sem("xn_ready"), st.sem("turned_ready"), st.sem("xnT_ready")
        block = st.block()

        @block.vector
        def _(dve):
            for t in range(NT):
                dve.bn_stats(stats[:, t, :], x_sb[:, t, :]).then_inc(stats_done, 1)
            for t in range(NT):
                dve.wait_ge(stats_done, t + 1)
                dve.bn_aggr(mv[:, t, :], stats[:, t, :]).then_inc(moments_done, 1)
            dve.wait_ge(moments_done, NT)
            dve.tensor_scalar(var_eps[:], mv[:, :, 1], LN_EPS, None, ALU.add).then_inc(var_ready, 1)
            dve.wait_ge(std_ready, 1)
            dve.reciprocal(rstd[:], std[:]).then_inc(rstd_ready, 1)
            dve.wait_ge(rstd_ready, 1)
            for t in range(NT):
                dve.tensor_scalar(xn[:, t, :], x_sb[:, t, :], mv[:, t, 0:1], rstd[:, t:t + 1],
                                  ALU.subtract, ALU.mult).then_inc(xn_ready, 1)

        @block.scalar
        def _(act):
            act.wait_ge(var_ready, 1)
            act.activation(std[:], var_eps[:], ACT.Sqrt).then_inc(std_ready, 1)
            for h in range(2):
                act.wait_ge(turned_ready, 4 * h + 4)
                act.activation(xnT[:, 512 * h:512 * h + 512], turned[:, h, :], ACT.Copy).then_inc(xnT_ready, 1)
            act.wait_ge(xnT_ready, 2)

        @block.sync
        def _(sp):
            if beside is not None:
                beside(sp)

        @block.tensor
        def _(pe):
            for t in range(NT):
                pe.wait_ge(xn_ready, t + 1)
                pe.transpose(turned[:, t // 4, (t % 4) * P:(t % 4 + 1) * P], xn[:, t, :],
                             ident[:]).then_inc(turned_ready, 1)


def linear_attention_stage(nc, wqkv, wo, x_sb, xnT, ident, beside):
    C = P
    E = DH + 1
    with Stage(nc, "lin") as st:
        w_sb = st.sb("w_sb", [P, 3 * D])
        wo_sb = st.sb("wo_sb", [P, D])
        head_mask = st.sb("head_mask", [P, H])
        block_mask = st.sb("block_mask", [P, H, E])
        causal = st.sb("causal", [P, C])
        qT = st.sb("qT", [P, N])
        kT = st.sb("kT", [P, N])
        k_tok = st.sb("k_tok", [P, NT, D])
        v_tok = st.sb("v_tok", [P, NT, H, E])
        q_heads = st.sb("q_heads", [P, 2, H, C])
        scores = st.sb("scores", [P, H, C])
        state = st.sb("state", [P, H, E])
        fresh = st.sb("fresh", [P, H, E])
        den = st.sb("den", [P, H])
        rden = st.sb("rden", [P, H])
        y = st.sb("y", [P, D])
        yT = st.sb("yT", [P, D])
        ps_a = st.ps("ps_a", [P, 4, 512])
        ps_n = st.ps("ps_n", [P, 512])
        ps_s = st.ps("ps_s", [P, 512])
        ps_y = st.ps("ps_y", [P, 512])
        ps_o = st.ps("ps_o", [P, 512])
        w_loaded, wo_loaded, masks, ones_set = st.sem("w_loaded"), st.sem("wo_loaded"), st.sem("masks"), st.sem("ones_set")
        proj_ready, proj_used = st.sem("proj_ready"), st.sem("proj_used")
        q_split = st.sem("q_split")
        scores_ready, scores_masked = st.sem("scores_ready"), st.sem("scores_masked")
        sum_ready, num_ready = st.sem("sum_ready"), st.sem("num_ready")
        y_ready, yT_psum, yT_ready, out_ready = st.sem("y_ready"), st.sem("yT_psum"), st.sem("yT_ready"), st.sem("out_ready")
        state_ready, dve_step, out_added = st.sem("state_ready"), st.sem("dve_step"), st.sem("out_added")
        block = st.block()

        @block.sync
        def _(sp):
            sp.dma_start(w_sb[:], wqkv).then_inc(w_loaded, 16)
            sp.dma_start(wo_sb[:], wo).then_inc(wo_loaded, 16)
            beside(sp)

        @block.gpsimd
        def _(pool):
            pool.memset(head_mask[:], 1.0).then_inc(masks, 1)
            pool.memset(block_mask[:], 1.0).then_inc(masks, 1)
            pool.memset(causal[:], 1.0).then_inc(masks, 1)
            pool.memset(v_tok[:], 1.0).then_inc(ones_set, 1)
            pool.wait_ge(masks, 3)
            pool.affine_select(out=head_mask[:], in_=head_mask[:], compare_op=ALU.is_ge, fill=0.0, base=0,
                               pattern=[[-DH, H]], channel_multiplier=1).then_inc(masks, 1)
            pool.affine_select(out=block_mask[:], in_=block_mask[:], compare_op=ALU.is_ge, fill=0.0, base=0,
                               pattern=[[-DH, H], [0, E]], channel_multiplier=1).then_inc(masks, 1)
            pool.affine_select(out=causal[:], in_=causal[:], compare_op=ALU.is_ge, fill=0.0, base=0,
                               pattern=[[1, C]], channel_multiplier=-1).then_inc(masks, 1)
            pool.wait_ge(masks, 6)
            pool.affine_select(out=head_mask[:], in_=head_mask[:], compare_op=ALU.is_ge, fill=0.0,
                               base=DH - 1, pattern=[[DH, H]], channel_multiplier=-1).then_inc(masks, 1)
            pool.affine_select(out=block_mask[:], in_=block_mask[:], compare_op=ALU.is_ge, fill=0.0,
                               base=DH - 1, pattern=[[DH, H], [0, E]], channel_multiplier=-1).then_inc(masks, 1)
            pool.wait_ge(masks, 8)
            for c in range(NT):
                pool.wait_ge(proj_used, 4)
                if c >= 2:
                    pool.wait_ge(scores_ready, 4 * (c - 1))
                pool.tensor_tensor(q_heads[:, c % 2], qT[:, None, c * C:(c + 1) * C].to_broadcast([P, H, C]),
                                   head_mask[:, :, None].to_broadcast([P, H, C]), ALU.mult).then_inc(q_split, 1)

        @block.tensor
        def _(pe):
            pe.wait_ge(w_loaded, 16)
            for i in range(4):
                pe.matmul(ps_a[:, i, :], w_sb[:, (i // 2) * D:(i // 2 + 1) * D],
                          xnT[:, (i % 2) * 512:(i % 2) * 512 + 512], start=True, stop=True).then_inc(proj_ready, 1)
            for t in range(NT):
                if t % 2 == 0:
                    pe.wait_ge(proj_used, t // 2 + 1)
                pe.matmul(ps_a[:, t // 2, (t % 2) * 256:(t % 2) * 256 + 256], xnT[:, t * P:(t + 1) * P],
                          w_sb[:, D:3 * D], start=True, stop=True).then_inc(proj_ready, 1)
            pe.wait_ge(proj_used, 4 + 2 * NT)

            def output(c):
                pe.wait_ge(y_ready, c + 1)
                pe.transpose(ps_y[:, 0:P], y[:], ident[:]).then_inc(yT_psum, 1)
                pe.wait_ge(yT_ready, c + 1)
                if c == 0:
                    pe.wait_ge(wo_loaded, 16)
                if c >= 1:
                    pe.wait_ge(out_added, c)
                pe.matmul(ps_o[:, 0:D], yT[:], wo_sb[:], start=True, stop=True).then_inc(out_ready, 1)

            for c in range(NT):
                pe.wait_ge(q_split, c + 1)
                if c >= 1:
                    pe.wait_ge(scores_masked, 4 * c)
                for g in range(4):
                    mm = pe.matmul(ps_a[:, g, :], kT[:, c * C:(c + 1) * C], q_heads[:, c % 2, 4 * g:4 * g + 4, :],
                                   start=True, stop=True)
                    mm.then_inc(scores_ready, 1)
                if c >= 1:
                    output(c - 1)
                pe.matmul(ps_s[:, 0:H * E], k_tok[:, c, :], v_tok[:, c, :, :], start=True,
                          stop=True).then_inc(sum_ready, 1)
                if c >= 1:
                    pe.wait_ge(y_ready, c)
                for h in range(H):
                    if h % 4 == 0:
                        pe.wait_ge(scores_masked, 4 * c + h // 4 + 1)
                    pe.matmul(ps_n[:, h * E:(h + 1) * E], scores[:, h, :], v_tok[:, c, h, :],
                              start=(h == 0), stop=False, skip_group_check=True)
                pe.wait_ge(state_ready, c + 1)
                pe.matmul(ps_n[:, 0:H * E], qT[:, c * C:(c + 1) * C], state[:], start=False,
                          stop=True, skip_group_check=True).then_inc(num_ready, 1)
            output(NT - 1)

        @block.scalar
        def _(act):
            for i in range(4):
                act.wait_ge(proj_ready, i + 1)
                dst = qT if i < 2 else kT
                act.activation(dst[:, (i % 2) * 512:(i % 2) * 512 + 512], ps_a[:, i, :],
                               ACT.Relu).then_inc(proj_used, 1)
            act.wait_ge(ones_set, 1)
            for t in range(NT):
                act.wait_ge(proj_ready, 4 + 2 * (t // 2) + 2)
                bank = ps_a[:, t // 2, (t % 2) * 256:(t % 2) * 256 + 256]
                act.activation(k_tok[:, t, :], bank[:, 0:D], ACT.Relu).then_inc(proj_used, 1)
                act.activation(v_tok[:, t, :, 0:DH], bank[:, D:2 * D].rearrange("p (h e) -> p h e", h=H),
                               ACT.Copy).then_inc(proj_used, 1)
            for c in range(NT):
                act.wait_ge(yT_psum, c + 1)
                if c >= 1:
                    act.wait_ge(out_ready, c)
                act.activation(yT[:], ps_y[:, 0:P], ACT.Copy).then_inc(yT_ready, 1)

        @block.vector
        def _(dve):
            chain = Chain(dve, dve_step)

            def add(c):
                dve.wait_ge(out_ready, c + 1)
                dve.tensor_tensor(x_sb[:, c, :], x_sb[:, c, :], ps_o[:, 0:D], ALU.add).then_inc(out_added, 1)

            dve.memset(state[:], 0.0).then_inc(state_ready, 1)
            dve.wait_ge(state_ready, 1)
            dve.wait_ge(masks, 8)
            for c in range(NT):
                for g in range(4):
                    dve.wait_ge(scores_ready, 4 * c + g + 1)
                    if c >= 1:
                        dve.wait_ge(num_ready, c)
                    dve.tensor_tensor(scores[:, 4 * g:4 * g + 4, :],
                                      ps_a[:, g, :].rearrange("p (h i) -> p h i", h=4),
                                      causal[:, None, :].to_broadcast([P, 4, C]), ALU.mult).then_inc(scores_masked, 1)
                if c >= 1:
                    add(c - 1)
                dve.wait_ge(sum_ready, c + 1)
                sums = ps_s[:, 0:H * E].rearrange("p (h e) -> p h e", h=H)
                chain(dve.tensor_tensor(fresh[:], sums, block_mask[:], ALU.mult))
                dve.wait_ge(num_ready, c + 1)
                dve.tensor_tensor(state[:], state[:], fresh[:], ALU.add).then_inc(state_ready, 1)
                num = ps_n[:, 0:H * E].rearrange("p (h e) -> p h e", h=H)
                chain(dve.tensor_scalar(den[:], num[:, :, DH], LN_EPS, None, ALU.add))
                chain(dve.reciprocal(rden[:], den[:]))
                if c >= 1:
                    dve.wait_ge(yT_psum, c)
                dve.tensor_tensor(y[:].rearrange("p (h e) -> p h e", h=H), num[:, :, 0:DH],
                                  rden[:, :, None].to_broadcast([P, H, DH]), ALU.mult).then_inc(y_ready, 1)
            add(NT - 1)
            dve.wait_ge(out_added, NT)




PAIRS = H // 2
KT = -(-T // P)
T_LAST = T - (KT - 1) * P
VW = 2 * DH + 1
Q_PART = [0, 0, 1, 1, 0, 2]
K_PART = [0, 1, 0, 1, 2, 0]
NPROD = len(Q_PART)
ROW_M = NPROD * DH
HALF = 64




def kv_stage(nc, ctx, k_weights, v_weights, k_bias, v_bias, ident, k_scr, v_scr):
    CH = 512
    NC = -(-T // CH)
    W = [min(CH, T - c * CH) for c in range(NC)]
    L = 2
    IN = 4
    with Stage(nc, "kv") as st:
        wk = [st.sb(f"wk{l}", [P, D]) for l in range(L)]
        wv = [st.sb(f"wv{l}", [P, D]) for l in range(L)]
        raw_k, raw_v = st.sb("raw_k", [P, D]), st.sb("raw_v", [P, D])
        bk = st.sb("bk", [P, 1])
        bv = st.sb("bv", [P, D])
        c_in = st.sb("c_in", [P, IN, 4, D])
        c_T = st.sb("c_T", [P, 2, CH])
        k_f = st.sb("k_f", [P, 2, L, CH])
        k_r = st.sb("k_r", [P, 2, L, CH])
        k_p = st.sb("k_p", [P, 2, L, 3, CH], BF16)
        v_o = st.sb("v_o", [P, 2, L, 4, PAIRS, VW])
        ps_t = st.ps("ps_t", [P, 2, 512])
        ps_k = st.ps("ps_k", [P, L, 512])
        ps_v = st.ps("ps_v", [P, L, 512])
        ps_w = st.ps("ps_w", [P, 512])
        w_loaded, w_turned, w_ready = st.sem("w_loaded"), st.sem("w_turned"), st.sem("w_ready")
        c_loaded = [st.sem(f"c_loaded{i}") for i in range(IN)]
        c_turned, cT_ready = st.sem("c_turned"), st.sem("cT_ready")
        k_ready, v_ready = st.sem("k_ready"), st.sem("v_ready")
        kf_ready, k1_ready, k2_ready, k3_ready = st.sem("kf_ready"), st.sem("k1_ready"), st.sem("k2_ready"), st.sem("k3_ready")
        r_ready, vo_ready, ones_set = st.sem("r_ready"), st.sem("vo_ready"), st.sem("ones_set")
        k_stored = [st.sem(f"k_stored{i}") for i in range(2)]
        v_stored = [st.sem(f"v_stored{i}") for i in range(2)]
        block = st.block()

        def tiles(c):
            return [(j, min(P, W[c] - j * P)) for j in range(-(-W[c] // P))]

        n_loads = [0] * IN
        loads_after = []
        for c in range(NC):
            n_loads[c % IN] += 1 if W[c] % P == 0 else 2
            loads_after.append(16 * n_loads[c % IN])
        stores_after, n_st = [], [0, 0]
        for c in range(NC):
            n_st[c % 2] += L * (1 if W[c] % P == 0 else 2)
            stores_after.append(16 * n_st[c % 2])

        def store_k(sp, c):
            for l in range(L):
                sp.wait_ge(k3_ready, L * c + l + 1)
                sp.wait_ge(k1_ready, L * c + l + 1)
                sp.wait_ge(k2_ready, L * c + l + 1)
                sp.dma_start(k_scr[l][:, :, c * CH:c * CH + W[c]].rearrange("a p t -> p a t"),
                             k_p[:, c % 2, l, :, 0:W[c]]).then_inc(k_stored[c % 2], 16)

        def store_v(act, c):
            full = W[c] // P
            for l in range(L):
                act.wait_ge(vo_ready, L * c + l + 1)
                act.dma_start(v_scr[l][:, 4 * c:4 * c + full, :, :], v_o[:, c % 2, l, 0:full]).then_inc(v_stored[c % 2], 16)
                if W[c] % P:
                    act.dma_start(v_scr[l][0:T_LAST, KT - 1, :, :], v_o[0:T_LAST, c % 2, l, full]).then_inc(v_stored[c % 2], 16)

        @block.sync
        def _(sp):
            sp.dma_start(wk[0][:], k_weights[0]).then_inc(w_loaded, 16)
            sp.dma_start(wv[0][:], v_weights[0]).then_inc(w_loaded, 16)
            sp.dma_start(raw_k[:], k_weights[1]).then_inc(w_loaded, 16)
            sp.dma_start(raw_v[:], v_weights[1]).then_inc(w_loaded, 16)
            sp.dma_start(bk[:], k_bias.rearrange("(p a) -> p a", a=1)).then_inc(w_loaded, 16)
            sp.dma_start(bv[:], row(v_bias, D).partition_broadcast(P)).then_inc(w_loaded, 16)
            def load(c):
                if c >= IN:
                    sp.wait_ge(c_turned, c - IN + 1)
                full = W[c] // P
                sp.dma_start(c_in[:, c % IN, 0:full, :],
                             ctx[c * CH:c * CH + full * P, :].rearrange("(j p) d -> p j d", p=P)
                             ).then_inc(c_loaded[c % IN], 16)
                if W[c] % P:
                    sp.dma_start(c_in[0:T_LAST, c % IN, full, :], ctx[T - T_LAST:T, :]).then_inc(c_loaded[c % IN], 16)

            for c in range(IN - 1):
                load(c)
            for c in range(NC):
                if c + IN - 1 < NC:
                    load(c + IN - 1)
                store_k(sp, c)
            for i in range(2):
                sp.wait_ge(k_stored[i], 16 * L * len(range(i, NC, 2)))

        @block.tensor
        def _(pe):
            pe.wait_ge(w_loaded, 16 * 6)
            pe.transpose(ps_w[:, 0:P], raw_k[:], ident[:])
            pe.transpose(ps_w[:, P:2 * P], raw_v[:], ident[:]).then_inc(w_turned, 1)

            def turn(c):
                pe.wait_ge(c_loaded[c % IN], loads_after[c])
                if c >= 2:
                    pe.wait_ge(cT_ready, c - 1)
                for j, n in tiles(c):
                    mm = pe.transpose(ps_t[:, c % 2, j * P:j * P + n], c_in[0:n, c % IN, j, :], ident[0:n, 0:n])
                mm.then_inc(c_turned, 1)

            turn(0)
            pe.wait_ge(w_ready, 2)
            for c in range(NC):
                if c + 1 < NC:
                    turn(c + 1)
                pe.wait_ge(cT_ready, c + 1)
                for l in range(L):
                    if c >= 1:
                        pe.wait_ge(kf_ready, L * (c - 1) + l + 1)
                        pe.wait_ge(k1_ready, L * (c - 1) + l + 1)
                    pe.matmul(ps_k[:, l, 0:W[c]], wk[l][:], c_T[:, c % 2, 0:W[c]], start=True,
                              stop=True).then_inc(k_ready, 1)
                for l in range(L):
                    if c >= 1:
                        pe.wait_ge(vo_ready, L * (c - 1) + l + 1)
                    for j, n in tiles(c):
                        mm = pe.matmul(ps_v[0:n, l, j * D:(j + 1) * D], c_T[:, c % 2, j * P:j * P + n], wv[l][:],
                                       start=True, stop=True)
                    mm.then_inc(v_ready, 1)

        @block.scalar
        def _(act):
            act.wait_ge(w_turned, 1)
            act.activation(wk[1][:], ps_w[:, 0:P], ACT.Copy).then_inc(w_ready, 1)
            act.activation(wv[1][:], ps_w[:, P:2 * P], ACT.Copy).then_inc(w_ready, 1)
            for c in range(NC):
                w = W[c]
                act.wait_ge(c_turned, c + 1)
                if c >= 2:
                    act.wait_ge(v_ready, L * (c - 1))
                act.activation(c_T[:, c % 2, 0:w], ps_t[:, c % 2, 0:w], ACT.Copy).then_inc(cT_ready, 1)
                for l in range(L):
                    act.wait_ge(k_ready, L * c + l + 1)
                    if c >= 2:
                        act.wait_ge(k3_ready, L * (c - 2) + l + 1)
                        act.wait_ge(k_stored[c % 2], 16 * L * (c // 2))
                    bias = 0.0 if l == 0 else bk[:, 0:1]
                    act.activation(k_f[:, c % 2, l, 0:w], ps_k[:, l, 0:w], ACT.Identity,
                                   bias=bias).then_inc(kf_ready, 1)
                    act.activation(k_p[:, c % 2, l, 0, 0:w], ps_k[:, l, 0:w], ACT.Identity,
                                   bias=bias).then_inc(k1_ready, 1)
                if c >= 1:
                    store_v(act, c - 1)
            store_v(act, NC - 1)
            for i in range(2):
                act.wait_ge(v_stored[i], 16 * n_st[i])

        @block.gpsimd
        def _(pool):
            pool.memset(v_o[:], 1.0).then_inc(ones_set, 1)
            for c in range(NC):
                for l in range(L):
                    pool.wait_ge(r_ready, L * c + l + 1)
                    if c >= 2:
                        pool.wait_ge(k_stored[c % 2], 16 * L * (c // 2))
                    pool.tensor_copy(k_p[:, c % 2, l, 1, 0:W[c]], k_r[:, c % 2, l, 0:W[c]]).then_inc(k2_ready, 1)

        @block.vector
        def _(dve):
            dve.wait_ge(w_loaded, 16 * 6)
            dve.wait_ge(ones_set, 1)
            for c in range(NC):
                w = W[c]
                for l in range(L):
                    dve.wait_ge(kf_ready, L * c + l + 1)
                    dve.wait_ge(k1_ready, L * c + l + 1)
                    if c >= 2:
                        dve.wait_ge(k3_ready, L * (c - 2) + l + 1)
                        dve.wait_ge(k2_ready, L * (c - 2) + l + 1)
                    dve.tensor_tensor(k_r[:, c % 2, l, 0:w], k_f[:, c % 2, l, 0:w], k_p[:, c % 2, l, 0, 0:w],
                                      ALU.subtract).then_inc(r_ready, 1)
                for l in range(L):
                    dve.wait_ge(v_ready, L * c + l + 1)
                    if c >= 2:
                        dve.wait_ge(v_stored[c % 2], stores_after[c - 2])
                    whole = [(0, P, sum(n == P for _, n in tiles(c)))] + [(j, n, 1) for j, n in tiles(c) if n < P]
                    for k, (j, n, m) in enumerate(whole):
                        out = v_o[0:n, c % 2, l, j:j + m, :, 0:2 * DH]
                        src = ps_v[0:n, l, j * D:(j + m) * D].rearrange("p (m a e) -> p m a e", m=m, a=PAIRS)
                        if l == 0:
                            ins = dve.tensor_copy(out, src)
                        else:
                            ins = dve.tensor_tensor(out, src,
                                                    bv[0:n].rearrange("p (a e) -> p a e", a=PAIRS)[:, None]
                                                    .to_broadcast([n, m, PAIRS, 2 * DH]), ALU.add)
                        if k == len(whole) - 1:
                            ins.then_inc(vo_ready, 1)
                for l in range(L):
                    dve.wait_ge(k2_ready, L * c + l + 1)
                    dve.tensor_tensor(k_p[:, c % 2, l, 2, 0:w], k_r[:, c % 2, l, 0:w], k_p[:, c % 2, l, 1, 0:w],
                                      ALU.subtract).then_inc(k3_ready, 1)


import numpy as np

QB = P
NB = N // QB
COLS = 2 * 2 * QB
GP = PAIRS // 2
MAXW = 1024
OPW = -(-T // 7)
PIECES = [(o, min(2 * OPW, T - o)) for o in range(0, T, 2 * OPW)]
OPS = [[(o, min(OPW, w - o)) for o in range(0, w, OPW)] for _, w in PIECES]
NOPS = sum(map(len, OPS))
PIECE_W = max(w for _, w in PIECES)
AHEAD = 3
LEAD = 8
NPIECE = len(PIECES)
LOW = -3.0e38
FOLD = 1024
FOLDS = [(i, o, min(FOLD, w - o)) for i, (_, w) in enumerate(PIECES) for o in range(0, w, FOLD)]
NFOLDS = len(FOLDS)
FOLD_END = [sum(f[0] <= n for f in FOLDS) for n in range(NPIECE)]


def after(eng, sem, k):
    if k > 0:
        eng.wait_ge(sem, k)


def span(b, start, width):
    if isinstance(b, int):
        return slice(b * QB + start, b * QB + start + width)
    return bass.ds(b * QB + start, width)


class Sides(Stage):

    def __init__(self, nc, tag, masked, wq, bq, k_scr, v_scr, rows_scr):
        super().__init__(nc, tag)
        self.masked, self.wq, self.bq, self.k_scr, self.v_scr, self.rows_scr = masked, wq, bq, k_scr, v_scr, rows_scr
        self.w_sb = self.sb("w_sb", [P, D])
        self.raw = self.sb("raw", [P, D])
        self.b_sb = self.sb("b_sb", [P, 1])
        self.v_sb = self.sb("v_sb", [P, KT, PAIRS, VW])
        self.q_max = self.sb("q_max", [P, PAIRS, 2, QB], BF16)
        self.q_att = self.sb("q_att", [P, PAIRS, 2, QB], BF16)
        self.summed = self.sb("summed", [P, 2, 2, P])
        if masked:
            self.first_row = self.sb("first_row", [P, T], BF16)
        self.k_side = None
        self.q_loaded, self.loaded = self.sem("q_loaded"), self.sem("loaded")
        self.n_q = 1 if bq is None else 2
        self.n_loads = 2 * (NPROD + (3 if masked else 1)) + 2 + (1 if masked else 0)

    def make_keys(self):
        self.k_side = self.sb("k_side", [P, PAIRS, T], BF16)

    def load_values(self, eng):
        eng.dma_start(self.w_sb[:] if self.bq is None else self.raw[:], self.wq).then_inc(self.q_loaded, 16)
        if self.bq is not None:
            eng.dma_start(self.b_sb[:], self.bq.rearrange("(p a) -> p a", a=1)).then_inc(self.q_loaded, 16)
        eng.dma_start(self.v_sb[:, 0:KT - 1], self.v_scr[:, 0:KT - 1]).then_inc(self.loaded, 16)
        eng.dma_start(self.v_sb[0:T_LAST, KT - 1], self.v_scr[0:T_LAST, KT - 1]).then_inc(self.loaded, 16)
        if self.masked:
            eng.dma_start(self.first_row[:], self.rows_scr[4:5, :].to_broadcast([P, T])).then_inc(self.loaded, 16)

    def load_keys(self, eng):
        for a in range(2):
            for j in range(NPROD):
                rows = slice(HALF * a + DH * j, HALF * a + DH * (j + 1))
                src = self.k_scr[K_PART[j]].rearrange("(p a d) t -> a d p t", a=2, d=DH)[a]
                eng.dma_start(self.k_side[rows, :, :], src).then_inc(self.loaded, 16)
            r = HALF * a + ROW_M
            if self.masked:
                eng.dma_start(self.k_side[r:r + 3, :, :],
                              self.rows_scr[0:1, None, :].to_broadcast([3, PAIRS, T])).then_inc(self.loaded, 16)
                eng.dma_start(self.k_side[r + 3:r + 6, :, :],
                              self.rows_scr[1:4, None, :].to_broadcast([3, PAIRS, T])).then_inc(self.loaded, 16)
                r += 6
            rest = HALF * (a + 1) - r
            eng.dma_start(self.k_side[r:r + rest, :, :],
                          self.rows_scr[0:1, None, :].to_broadcast([rest, PAIRS, T])).then_inc(self.loaded, 16)

    def load(self, eng):
        self.load_values(eng)
        self.load_keys(eng)


def q_stage(nc, tag, sides, scale, xnT, ident, q_nat, q_scr):
    bq = sides.bq
    w_sb, raw, b_sb = sides.w_sb, sides.raw, sides.b_sb
    with Stage(nc, tag) as st:
        q_f = st.sb("q_f", [P, N])
        q_r = st.sb("q_r", [P, N])
        q_p = st.sb("q_p", [P, 3, N], BF16)
        ps = st.ps("ps", [P, 2, 512])
        ps_w = st.ps("ps_w", [P, 512])
        turned, w_ready, q_ready = st.sem("turned"), st.sem("w_ready"), st.sem("q_ready")
        f_ready, split, stored, b_ready = st.sem("f_ready"), st.sem("split"), st.sem("stored"), st.sem("b_ready")
        moved, filled = [st.sem(f"moved{a}") for a in range(2)], st.sem("filled")
        block = st.block()

        def move_rows(eng, a):
            eng.wait_ge(stored, 16)
            for j in range(NPROD):
                src = q_nat[Q_PART[j]].rearrange("(p a d) n -> a d p n", a=2, d=DH)[a]
                eng.dma_start(q_scr[a, DH * j:DH * j + DH, :, :], src).then_inc(moved[a], 16)
            eng.wait_ge(moved[a], 16 * NPROD)

        @block.sync
        def _(sp):
            sp.wait_ge(split, 5)
            sp.dma_start(q_nat.rearrange("j p n -> p j n"), q_p[:]).then_inc(stored, 16)
            move_rows(sp, 0)

        @block.gpsimd
        def _(pool):
            pool.memset(sides.q_max[:], 0.0).then_inc(filled, 1)
            pool.memset(sides.q_att[:], 0.0).then_inc(filled, 1)
            pool.memset(sides.summed[:], 0.0).then_inc(filled, 1)

        @block.tensor
        def _(pe):
            pe.wait_ge(sides.q_loaded, 16 * sides.n_q)
            if bq is not None:
                pe.transpose(ps_w[:, 0:P], raw[:], ident[:]).then_inc(turned, 1)
                pe.wait_ge(w_ready, 1)
            for i in range(2):
                pe.matmul(ps[:, i, :], w_sb[:], xnT[:, 512 * i:512 * i + 512], start=True,
                          stop=True).then_inc(q_ready, 1)

        @block.scalar
        def _(act):
            if bq is not None:
                act.wait_ge(turned, 1)
                act.activation(w_sb[:], ps_w[:, 0:P], ACT.Copy).then_inc(w_ready, 1)
                act.wait_ge(b_ready, 1)
            for i in range(2):
                act.wait_ge(q_ready, i + 1)
                act.activation(q_f[:, 512 * i:512 * i + 512], ps[:, i, :], ACT.Identity, scale=scale,
                               bias=0.0 if bq is None else b_sb[:, 0:1]).then_inc(f_ready, 1)
            move_rows(act, 1)

        @block.vector
        def _(dve):
            if bq is not None:
                dve.wait_ge(sides.q_loaded, 16 * sides.n_q)
                dve.tensor_scalar(b_sb[:], b_sb[:], scale, None, ALU.mult).then_inc(b_ready, 1)
            chain = Chain(dve, split)
            dve.wait_ge(f_ready, 2)
            chain(dve.tensor_copy(q_p[:, 0, :], q_f[:]))
            chain(dve.tensor_tensor(q_r[:], q_f[:], q_p[:, 0, :], ALU.subtract))
            chain(dve.tensor_copy(q_p[:, 1, :], q_r[:]))
            chain(dve.tensor_tensor(q_f[:], q_r[:], q_p[:, 1, :], ALU.subtract))
            chain(dve.tensor_copy(q_p[:, 2, :], q_f[:]))


def even_rows_stage(nc, first_mask, rows_scr):
    F = 4
    hi, parts = NEG, []
    for _ in range(3):
        bits = int(np.float32(hi).view(np.uint32)) & 0xFFFF0000
        parts.append(float(np.uint32(bits).view(np.float32)))
        hi -= parts[-1]
    assert hi == 0.0
    with Stage(nc, "even") as st:
        mask = st.sb("mask", [F, T // F], I32)
        rows = st.sb("rows", [F, 5, T // F], BF16)
        loaded, made, stored = st.sem("loaded"), st.sem("made"), st.sem("stored")
        block = st.block()

        @block.sync
        def _(sp):
            sp.dma_start(mask[:], first_mask.rearrange("a (f t) -> (a f) t", f=F)).then_inc(loaded, 16)
            sp.wait_ge(made, 5)
            sp.dma_start(rows_scr.rearrange("r (f t) -> f r t", f=F), rows[:]).then_inc(stored, 16)
            sp.wait_ge(stored, 16)

        @block.vector
        def _(dve):
            dve.memset(rows[:, 0, :], 1.0).then_inc(made, 1)
            dve.wait_ge(loaded, 16)
            for i, part in enumerate(parts + [-parts[0]]):
                dve.tensor_scalar(rows[:, 1 + i, :], mask[:], 0, part, ALU.is_equal, ALU.mult).then_inc(made, 1)


def cross_attention_stage(nc, tag, sides, bias, wo, bo, x_sb, ident, q_scr, bias_scr):
    with Stage(nc, tag) as st:
        masked, k_side, v_sb, q_max, q_att, summed = (sides.masked, sides.k_side, sides.v_sb, sides.q_max,
                                                      sides.q_att, sides.summed)
        piece = st.sb("piece", [P, 2, PIECE_W])
        chunk = st.sb("chunk", [P, 3, P])
        probs = st.sb("probs", [P, 3, COLS])
        part_max = st.sb("part_max", [P, H, NOPS])
        neg_max = st.sb("neg_max", [P, H])
        m_rest = st.sb("m_rest", [H, 2, P])
        m_parts = st.sb("m_parts", [H, 3, P], BF16)
        apart = st.sb("apart", [P, 2, FOLD], BF16)
        apart_sum = st.sb("apart_sum", [P, NFOLDS])
        apart_max = st.sb("apart_max", [P, 1])
        worst = st.sb("worst", [1, 1])
        uneven_f = st.sb("uneven_f", [1, 1])
        uneven = st.sb("uneven", [1, 1], I32)
        if masked:
            first_row = sides.first_row
            shut = st.sb("shut", [1, 1])
            ones_sb = st.sb("ones_sb", [1, QB])
            even_row = st.sb("even_row", [1, QB], BF16)
        recip = st.sb("recip", [P, 2, 2, GP])
        y = st.sb("y", [P, PAIRS, 2, DH])
        yT = st.sb("yT", [P, P])
        wo_sb = st.sb("wo_sb", [P, D])
        raw = st.sb("raw", [P, D])
        bo_sb = st.sb("bo_sb", [P, D])
        ps_max = st.ps("ps_max", [P, 2, MAXW])
        ps_att = st.ps("ps_att", [P, 3, 512])
        ps_acc = st.ps("ps_acc", [P, 512])

        units1 = [(i, h, o, w) for i in range(NPIECE) for h in range(H) for o, w in OPS[i]]
        units1 = units1[:-8] + [("check", 0, 0, P)] + units1[-8:] + [("turn", 0, 0, P)]
        n_u1 = len(units1)
        check_at = units1.index(("check", 0, 0, P))
        piece_last = {i: n + 1 for n, (i, *_r) in enumerate(units1)}
        n_exp = KT * GP
        TAIL = [("sums", GP), ("turn", 3 * GP), ("out", 5 * GP)]

        def second_units(second, tail):
            units = []
            for e in range(n_exp if second is not None else 0):
                if tail is not None:
                    units += [(kind, 0, 0, 0) for kind, at in TAIL if at == e]
                units.append(("exp", e // GP, e % GP, e))
            if second is None and tail is not None:
                units = [(kind, 0, 0, 0) for kind, _ in TAIL]
            return units

        begins = [o / T for o, _ in PIECES] + [1.0]
        piece_at = {int(KT * (0.6 * begins[n - 1] + 0.4 * begins[n])): n for n in range(1, NPIECE)}

        w_loaded, w_turned, w_ready, filled = st.sem("w_loaded"), st.sem("w_turned"), st.sem("w_ready"), st.sem("filled")
        shut_ready, bo_added = st.sem("shut_ready"), st.sem("bo_added")
        scored1, maxed = st.sem("scored1"), st.sem("maxed")
        piece_in = [st.sem(f"piece_in{i}") for i in range(2)]
        piece_ready = st.sem("piece_ready")
        q_ahead, piece_ahead, turned_ahead = st.sem("q_ahead"), st.sem("piece_ahead"), st.sem("turned_ahead")
        reduced, max_split = st.sem("reduced"), st.sem("max_split")
        apart_ready, folds = st.sem("apart_ready"), st.sem("folds")
        judged = st.sem("judged")
        m_stored, qm_in, q_in = st.sem("m_stored"), st.sem("qm_in"), st.sem("q_in")
        chunk_in = [st.sem(f"chunk_in{i}") for i in range(3)]
        chunk_ready, bias_in = st.sem("chunk_ready"), st.sem("bias_in")
        scored2, valued = st.sem("scored2"), st.sem("valued")
        read2 = {"exp": st.sem("exp_done"), "sums": st.sem("sums_read"), "turn": st.sem("turn_read"),
                 "out": st.sem("out_read")}
        copied, y_recip, y_half = st.sem("copied"), st.sem("y_recip"), st.sem("y_half")
        block_sems = [scored1, maxed, *piece_in, piece_ready, q_ahead, piece_ahead, turned_ahead, reduced, max_split,
                      apart_ready, folds, judged, m_stored, qm_in, q_in, bias_in, *chunk_in,
                      chunk_ready, scored2, valued, *read2.values(), copied, y_recip, y_half]

        def fold_after(k):
            n = FOLDS[k][0]
            start = FOLD_END[n - 1] if n else 0
            part = (k - start + 1) / (FOLD_END[n] - start + 1)
            return int((begins[n] + part * (begins[n + 1] - begins[n])) * (n_exp - 6 * GP))

        def interleaved(first, units2):
            n1, n2 = (n_u1 if first is not None else 0), len(units2)
            if not n2:
                return [(1, i) for i in range(n1)]
            cost = [w + 64 for *_r, w in units1]
            done = min(n1, AHEAD)
            out, spent = [(1, i) for i in range(done)], sum(cost[:done])
            for u in range(n2):
                out.append((2, u))
                while done < n1 and spent * (n2 - LEAD) < (u + 1) * sum(cost):
                    out.append((1, done))
                    spent += cost[done]
                    done += 1
            assert done == n1
            return out

        block = nc.Block()
        with block:
            @block.sync
            def _(sp):
                sp.dma_start(wo_sb[:] if bo is None else raw[:], wo).then_inc(w_loaded, 16)
                if bo is not None:
                    sp.dma_start(bo_sb[:], row(bo, D).partition_broadcast(P)).then_inc(w_loaded, 16)
                sp.wait_ge(sides.loaded, 16 * sides.n_loads)

            @block.gpsimd
            def _(pool):
                if masked:
                    pool.memset(ones_sb[:], 1.0).then_inc(filled, 1)

            @block.tensor
            def _(pe):
                if bo is not None:
                    pe.wait_ge(w_loaded, 32)
                    pe.transpose(ps_acc[:, 0:P], raw[:], ident[:]).then_inc(w_turned, 1)

            @block.scalar
            def _(act):
                if bo is not None:
                    act.wait_ge(w_turned, 1)
                    act.activation(wo_sb[:], ps_acc[:, 0:P], ACT.Copy).then_inc(w_ready, 1)

            @block.vector
            def _(dve):
                if bo is not None:
                    dve.wait_ge(w_loaded, 32)
                    for t in range(NT):
                        dve.tensor_tensor(x_sb[:, t, :], x_sb[:, t, :], bo_sb[:], ALU.add).then_inc(bo_added, 1)
                if masked:
                    dve.wait_ge(sides.loaded, 16 * sides.n_loads)
                    dve.tensor_reduce(shut[:], first_row[0:1, :], AX.X, ALU.min).then_inc(shut_ready, 1)

        def run_block(first, second, tail, following=None, asked=True):
            units2 = second_units(second, tail)
            order = interleaved(first, units2)
            block = nc.Block()
            with block:
                def wait_piece(eng, n, turned):
                    before = 1 if asked else 0
                    if n >= before and turned:
                        eng.wait_ge(piece_ready, n + 1 - before)
                    elif n >= before:
                        eng.wait_ge(piece_in[n % 2], 16 * (n // 2 + 1 - (before if n % 2 == 0 else 0)))

                def by_flag(eng, program):
                    if second is None:
                        return program(False)
                    flag = eng.value_load(uneven[0:1, 0:1], min_val=0, max_val=1)
                    with eng.If(flag > 0):
                        program(True)
                    with eng.Else():
                        program(False)

                @block.sync
                def _(sp):
                    q_rows = ROW_M + (6 if masked else 3)

                    def load_piece(b, n, sem):
                        o, w = PIECES[n]
                        dst = piece[:, n % 2, 0:w]
                        sp.dma_start(dst.bitcast(I32) if masked else dst, bias[span(b, 0, P), o:o + w]).then_inc(sem, 16)

                    def load_q_max(b, sem):
                        for a in range(2):
                            sp.dma_start(q_max[HALF * a:HALF * a + ROW_M, :, a, :],
                                         q_scr[a, 0:ROW_M, :, span(b, 0, QB)]).then_inc(sem, 16)

                    def next_piece(n):
                        if n >= 2:
                            sp.wait_ge(maxed, piece_last[n - 2])
                            sp.wait_ge(folds, FOLD_END[n - 2])
                        load_piece(first, n, piece_in[n % 2])

                    def fetch(kt):
                        if kt >= 3:
                            sp.wait_ge(scored2, GP * (kt - 2) + (len(TAIL) if tail is not None else 0))
                        n = P if kt < KT - 1 else T_LAST
                        dst = chunk[:, kt % 3, 0:n]
                        sp.dma_start(dst.bitcast(I32) if masked else dst,
                                     bias_scr[:, kt * P:kt * P + n]).then_inc(chunk_in[kt % 3], 16)

                    def program(uneven_block):
                        if second is not None:
                            for a in range(2):
                                sp.dma_start(q_att[HALF * a:HALF * a + q_rows, :, a, :],
                                             q_scr[a, 0:q_rows, :, span(second, 0, QB)]).then_inc(q_in, 16)
                        if first is not None and not asked:
                            load_q_max(first, qm_in)
                            load_piece(first, 0, piece_in[0])
                        if uneven_block:
                            sp.dma_start(bias_scr, bias[span(second, 0, QB), :]).then_inc(bias_in, 16)
                            sp.wait_ge(bias_in, 16)
                            for kt in range(KT):
                                fetch(kt)
                                if first is not None and kt in piece_at:
                                    next_piece(piece_at[kt])
                        elif first is not None:
                            for n in range(1, NPIECE):
                                next_piece(n)

                    by_flag(sp, program)
                    if first is None:
                        return
                    if following is not None:
                        sp.wait_ge(maxed, piece_last[NPIECE - 2])
                        sp.wait_ge(folds, FOLD_END[NPIECE - 2])
                        load_piece(following, 0, piece_ahead)
                    if masked:
                        sp.wait_ge(judged, 4)
                        for a in range(2):
                            sp.dma_start(q_scr[a:a + 1, ROW_M + 3:ROW_M + 6, :, span(first, 0, QB)].rearrange(
                                             "a c p q -> a (c p) q"),
                                         even_row[:, None, :].to_broadcast([1, 3 * PAIRS, QB])).then_inc(m_stored, 16)
                    if following is not None:
                        sp.wait_ge(maxed, n_u1 - 1)
                        load_q_max(following, q_ahead)
                    sp.wait_ge(max_split, 4)
                    for a in range(2):
                        sp.dma_start(q_scr[a, ROW_M:ROW_M + 3, :, span(first, 0, QB)].rearrange("c p q -> p c q"),
                                     m_parts[a:H:2]).then_inc(m_stored, 16)
                    sp.wait_ge(m_stored, 16 * (4 if masked else 2))
                    if following is not None:
                        sp.wait_ge(q_ahead, 32)
                        sp.wait_ge(piece_ahead, 16)

                @block.tensor
                def _(pe):
                    def max_unit(u):
                        after(pe, maxed, u - 1)
                        dst = ps_max[:, u % 2, :]
                        if units1[u][0] == "check":
                            pe.wait_ge(judged, 1)
                            pe.transpose(dst[0:1, 0:P], apart_max[:], ident[:]).then_inc(scored1, 1)
                            return
                        if units1[u][0] == "turn":
                            pe.wait_ge(reduced, 1)
                            pe.transpose(dst[0:H, 0:P], neg_max[:], ident[:]).then_inc(scored1, 1)
                            return
                        i, h, o, w = units1[u]
                        for c in range(0, w, 512):
                            n = min(512, w - c)
                            k0 = PIECES[i][0] + o + c
                            mm = pe.matmul(dst[:, c:c + n], q_max[:, h // 2, h % 2, :],
                                           k_side[:, h // 2, k0:k0 + n], start=True, stop=True)
                        mm.then_inc(scored1, 1)

                    def scores(u, uneven_block):
                        kind, kt, j, e = units2[u]
                        if u == 0 and second is not None:
                            pe.wait_ge(q_in, 32)
                        if u >= 3:
                            pe.wait_ge(read2[units2[u - 3][0]], units2[u - 3][3] + 1)
                        if kind == "exp":
                            n = P if kt < KT - 1 else T_LAST
                            if uneven_block and j == 0 and masked:
                                pe.wait_ge(chunk_ready, kt + 1)
                            elif uneven_block and j == 0:
                                pe.wait_ge(chunk_in[kt % 3], 16 * (kt // 3 + 1))
                            dst = ps_att[0:n, u % 3, :]
                            if uneven_block:
                                pe.matmul(dst, chunk[:, kt % 3, 0:n], ident[:, None, :].to_broadcast([P, 4, P]),
                                          start=True, stop=False, skip_group_check=True)
                            for c in range(2):
                                pair = 2 * j + c
                                mm = pe.matmul(dst[:, c * 2 * QB:(c + 1) * 2 * QB], k_side[:, pair, kt * P:kt * P + n],
                                               q_att[:, pair, :, :], start=not uneven_block, stop=True,
                                               skip_group_check=True)
                            mm.then_inc(scored2, 1)
                        elif kind == "sums":
                            pe.wait_ge(copied, GP)
                            for i in range(4):
                                mm = pe.transpose(ps_att[:, u % 3, i * P:(i + 1) * P], summed[:, i // 2, i % 2, :],
                                                  ident[:])
                            mm.then_inc(scored2, 1)
                        elif kind == "turn":
                            pe.wait_ge(read2["sums"], 1)
                            pe.transpose(ps_att[:, u % 3, 0:P], y[:].rearrange("p a b e -> p (a b e)"),
                                         ident[:]).then_inc(scored2, 1)
                        else:
                            pe.wait_ge(read2["turn"], 1)
                            pe.matmul(ps_att[:, u % 3, 0:D], yT[:], wo_sb[:], start=True,
                                      stop=True).then_inc(scored2, 1)

                    def values(u):
                        kind, kt, j, e = units2[u]
                        n = P if kt < KT - 1 else T_LAST
                        pe.wait_ge(read2["exp"], e + 1)
                        if e == 0 and tail is not None:
                            pe.wait_ge(copied, GP)
                        for c in range(2):
                            cols = slice(c * 2 * QB, (c + 1) * 2 * QB)
                            mm = pe.matmul(ps_acc[32 * j:32 * j + VW, cols], v_sb[0:n, kt, 2 * j + c, :],
                                           probs[0:n, e % 3, cols], start=(kt == 0 and c == 0),
                                           stop=(kt == KT - 1), skip_group_check=True)
                        mm.then_inc(valued, 1)

                    def program(uneven_block):
                        if first is not None and not asked:
                            pe.wait_ge(qm_in, 32)
                        behind = []
                        for which, u in order:
                            if which == 1:
                                max_unit(u)
                                continue
                            scores(u, uneven_block)
                            if units2[u][0] == "exp":
                                behind.append(u)
                                if len(behind) > 2:
                                    values(behind.pop(0))
                        for u in behind:
                            values(u)

                    by_flag(pe, program)

                @block.scalar
                def _(act):
                    def sum_fold(k):
                        n, o, w = FOLDS[k]
                        if masked:
                            act.wait_ge(apart_ready, k + 1)
                        else:
                            wait_piece(act, n, False)
                        after(act, folds, k - 1)
                        if masked:
                            act.activation(apart[:, k % 2, 0:w], apart[:, k % 2, 0:w], ACT.Square, scale=1.0 / NEG,
                                           accum_out=apart_sum[:, k:k + 1]).then_inc(folds, 1)
                        else:
                            act.activation(apart[:, k % 2, 0:w], piece[:, n % 2, o:o + w], ACT.Abs,
                                           accum_out=apart_sum[:, k:k + 1]).then_inc(folds, 1)

                    if tail is not None:
                        for j in range(GP):
                            act.activation(summed[32 * j:32 * j + VW].rearrange("p c a q -> p (c a q)"),
                                           ps_acc[32 * j:32 * j + VW, :], ACT.Copy).then_inc(copied, 1)
                    if second is None and first is not None:
                        for k in range(NFOLDS):
                            sum_fold(k)
                    k = 0
                    for u, (kind, kt, j, e) in enumerate(units2):
                        if kind == "exp" and first is not None and k < NFOLDS and e == fold_after(k):
                            sum_fold(k)
                            k += 1
                        if kind == "exp":
                            n = P if kt < KT - 1 else T_LAST
                            act.wait_ge(scored2, u + 1)
                            after(act, valued, e - 2)
                            act.activation(probs[0:n, e % 3, :], ps_att[0:n, u % 3, :], ACT.Exp).then_inc(read2["exp"], 1)
                        elif kind == "turn":
                            act.wait_ge(scored2, u + 1)
                            act.activation(yT[:], ps_att[:, u % 3, 0:P], ACT.Copy).then_inc(read2["turn"], 1)

                @block.gpsimd
                def _(pool):
                    def convert(ap):
                        return pool.tensor_scalar(ap, ap.bitcast(I32), 0, NEG, ALU.is_equal, ALU.mult)

                    def convert_piece(n):
                        wait_piece(pool, n, False)
                        convert(piece[:, n % 2, 0:PIECES[n][1]]).then_inc(piece_ready, 1)

                    def set_apart(k):
                        n, o, w = FOLDS[k]
                        if o == 0:
                            wait_piece(pool, n, True)
                        after(pool, folds, k - 1)
                        c = PIECES[n][0] + o
                        pool.tensor_tensor(apart[:, k % 2, 0:w], piece[:, n % 2, o:o + w], first_row[:, c:c + w],
                                           ALU.add).then_inc(apart_ready, 1)

                    def program(uneven_block):
                        k = 0
                        for s in range(KT if uneven_block else 0):
                            if first is not None and s in piece_at:
                                convert_piece(piece_at[s])
                            if first is not None and k < NFOLDS and s == fold_after(k) // GP - 1:
                                set_apart(k)
                                k += 1
                            n = P if s < KT - 1 else T_LAST
                            pool.wait_ge(chunk_in[s % 3], 16 * (s // 3 + 1))
                            convert(chunk[:, s % 3, 0:n]).then_inc(chunk_ready, 1)
                        if not uneven_block and first is not None:
                            for k, (n, o, w) in enumerate(FOLDS):
                                if o == 0 and (n or not asked):
                                    convert_piece(n)
                                set_apart(k)

                    if masked:
                        by_flag(pool, program)
                    if masked and following is not None:
                        pool.wait_ge(piece_ahead, 16)
                        convert(piece[:, 0, 0:PIECES[0][1]]).then_inc(turned_ahead, 1)

                @block.vector
                def _(dve):
                    def max_unit(u):
                        dve.wait_ge(scored1, u + 1)
                        if u == check_at - 2:
                            dve.wait_ge(folds, NFOLDS)
                            dve.tensor_reduce(apart_max[:], apart_sum[:], AX.X, ALU.max).then_inc(judged, 1)
                        if units1[u][0] == "check":
                            dve.tensor_reduce(worst[:], ps_max[0:1, u % 2, 0:P], AX.X, ALU.max).then_inc(maxed, 1)
                            dve.wait_ge(maxed, u + 1)
                            if masked:
                                dve.tensor_scalar(uneven_f[:], worst[:], shut[:], 0.5, ALU.max,
                                                  ALU.is_gt).then_inc(judged, 1)
                            else:
                                dve.tensor_scalar(uneven_f[:], worst[:], 0.0, None, ALU.is_gt).then_inc(judged, 1)
                            dve.wait_ge(judged, 2)
                            dve.tensor_copy(uneven[:], uneven_f[:]).then_inc(judged, 1)
                            if masked:
                                dve.tensor_scalar(even_row[:], ones_sb[:], uneven_f[:], 0.0, ALU.mult,
                                                  ALU.is_equal).then_inc(judged, 1)
                            return
                        if units1[u][0] == "turn":
                            src = ps_max[0:H, u % 2, 0:P]
                            dve.tensor_copy(m_parts[:, 0, :], src).then_inc(max_split, 1)
                            dve.wait_ge(max_split, 1)
                            dve.tensor_tensor(m_rest[:, 0], src, m_parts[:, 0, :], ALU.subtract).then_inc(maxed, 1)
                            dve.wait_ge(maxed, u + 1)
                            dve.tensor_copy(m_parts[:, 1, :], m_rest[:, 0]).then_inc(max_split, 1)
                            dve.wait_ge(max_split, 2)
                            dve.tensor_tensor(m_rest[:, 1], m_rest[:, 0], m_parts[:, 1, :],
                                              ALU.subtract).then_inc(max_split, 1)
                            dve.wait_ge(max_split, 3)
                            dve.tensor_copy(m_parts[:, 2, :], m_rest[:, 1]).then_inc(max_split, 1)
                            return
                        n, h, o, w = units1[u]
                        if h == 0 and o == 0:
                            wait_piece(dve, n, masked)
                        slot = sum(map(len, OPS[:n])) + o // OPW
                        dve.tensor_tensor_reduce(ps_max[:, u % 2, 0:w], ps_max[:, u % 2, 0:w], piece[:, n % 2, o:o + w], 1.0,
                                                 LOW, ALU.add, ALU.max, part_max[:, h, slot:slot + 1]).then_inc(maxed, 1)
                        if u == n_u1 - 2:
                            dve.wait_ge(maxed, u + 1)
                            dve.tensor_reduce(neg_max[:], part_max[:], AX.X, ALU.max, negate=True).then_inc(reduced, 1)

                    def second_unit(u):
                        kind = units2[u][0]
                        bank = ps_att[:, u % 3, :]
                        if kind == "sums":
                            dve.wait_ge(scored2, u + 1)
                            cols = bank.rearrange("p (c a j r) -> p c a j r", c=2, a=2, j=GP)
                            y_cols = y[:].rearrange("p (j c) a e -> p c a j e", c=2)
                            dve.reciprocal(recip[:], cols[:, :, :, :, 2 * DH]).then_inc(y_recip, 1)
                            dve.wait_ge(y_recip, 1)
                            for a in range(2):
                                dve.tensor_tensor(y_cols[:, :, a], cols[:, :, a, :, a * DH:(a + 1) * DH],
                                                  recip[:, :, a, :, None].to_broadcast([P, 2, GP, DH]),
                                                  ALU.mult).then_inc(y_half if a == 0 else read2["sums"], 1)
                            dve.wait_ge(y_half, 1)
                        if kind == "out":
                            dve.wait_ge(scored2, u + 1)
                            if isinstance(tail, int):
                                xs = x_sb[:, tail, :]
                            else:
                                xs = x_sb[:, bass.ds(tail, 1), :].rearrange("p o d -> p (o d)")
                            dve.tensor_tensor(xs, xs, bank[:, 0:D], ALU.add).then_inc(read2["out"], 1)

                    for which, u in order:
                        max_unit(u) if which == 1 else second_unit(u)

        assert NPIECE % 2 == 0
        run_block(0, None, None, following=1, asked=False)
        clear(nc, block_sems)
        run_block(1, 0, None, following=2)
        with nc.Fori(1, NB - 2) as b:
            clear(nc, block_sems)
            run_block(b + 1, b, b - 1, following=b + 2)
        clear(nc, block_sems)
        run_block(NB - 1, NB - 2, NB - 3)
        clear(nc, block_sems)
        run_block(None, NB - 1, NB - 2)
        clear(nc, block_sems)
        run_block(None, None, NB - 1)


PH = 8
NK = 32
NE = NK * NK
ET = NE // P
TOPK = 8
BN_EPS = 1e-5


def product_key_stage(nc, w_q, gamma, beta, keys, down, up, x_sb, xnT, ident):
    SIDE = 2
    F = SIDE * PH
    POOL_HEADS = 5
    RING = 4
    LAG = 2
    EARLY = 4
    with Stage(nc, "pk") as st:
        wq_sb = st.sb("wq_sb", [P, F * P])
        g_sb, b_sb = st.sb("g_sb", [P, F]), st.sb("b_sb", [P, F])
        keys_in = st.sb("keys_in", [P, 4, D])
        keys_T = st.sb("keys_T", [P, PH, NK, SIDE])
        down_in = st.sb("down_in", [P, ET, D])
        down_T = st.sb("down_T", [P, ET, P])
        up_sb = st.sb("up_sb", [P, ET, D])
        q_T = st.sb("q_T", [P, F, N])
        gelu_T = st.sb("gelu_T", [P, ET, N])
        stats, mv = st.sb("stats", [P, F, 2, 6]), st.sb("mv", [P, F, 2])
        bn = st.sb("bn", [P, F, 4])
        sim = st.sb("sim", [P, 2, SIDE, PH, NK])
        top = st.sb("top", [P, SIDE, PH, TOPK])
        pair = st.sb("pair", [P, PH, TOPK, TOPK])
        best = st.sb("best", [P, 2, PH, TOPK])
        neg = st.sb("neg", [P, 2, PH])
        ex, z = st.sb("ex", [P, PH, TOPK]), st.sb("z", [P, PH])
        rz = st.sb("rz", [P, 2, PH])
        total = st.sb("total", [P, RING, NK, NK])
        expo = st.sb("expo", [P, 3, NE])
        weight = st.sb("weight", [P, 2, NE])
        diag = st.sb("diag", [P, 2, P])
        act_T = st.sb("act_T", [P, ET, P])
        s = {n: st.sem(n) for n in (
            "w_in", "k_in", "d_in", "u_in", "gb_in", "turned", "turned_out", "q_ready", "q_stats", "var", "root",
            "rroot", "scale", "shift0", "shift", "q_used", "h_ready", "gelu", "sim_ready", "sim_out", "top", "pair",
            "best", "neg", "exd", "ex", "z", "rz", "total_d", "total_p", "expo", "weight", "diag", "wT", "act_T",
            "out", "added")}

        def load(sp):
            sp.dma_start(wq_sb[:], w_q).then_inc(s["w_in"], 16)
            sp.dma_start(keys_in[:], keys.rearrange("h k s d -> (h k s) d").rearrange("(t p) d -> p t d", p=P)
                         ).then_inc(s["k_in"], 16)
            sp.dma_start(down_in[:], down.rearrange("(t p) d -> p t d", p=P)).then_inc(s["d_in"], 16)
            sp.dma_start(up_sb[:], up.rearrange("(t p) d -> p t d", p=P)).then_inc(s["u_in"], 16)
            with nc.allow_non_contiguous_dma(reason="4096 scale and shift values, once"):
                sp.dma_start(g_sb[:], gamma.rearrange("(f p) -> p f", p=P)).then_inc(s["gb_in"], 16)
                sp.dma_start(b_sb[:], beta.rearrange("(f p) -> p f", p=P)).then_inc(s["gb_in"], 16)

        layernorm_stage(nc, "ln2", x_sb, xnT, ident, load)
        banks = st.ps("banks", [P, 8, 512])
        block = st.block()

        def store_q(act, f):
            act.wait_ge(s["shift"], f + 1)
            act.activation(q_T[:, f, :], banks[:, 2 * (f % 3):2 * (f % 3) + 2, :].rearrange("p b c -> p (b c)"),
                           ACT.Identity, scale=bn[:, f, 2:3], bias=bn[:, f, 3:4]).then_inc(s["q_used"], 1)

        def sim_copy(act, t):
            act.wait_ge(s["sim_ready"], t + 1)
            if t >= 2:
                act.wait_ge(s["weight"], PH * (t - 1))
            act.activation(sim[:, t % 2].rearrange("p s h k -> p (s h k)"), banks[:, t % 2, :], ACT.Copy).then_inc(s["sim_out"], 1)

        def total_sem(t, h):
            if h < POOL_HEADS:
                return s["total_p"], POOL_HEADS * t + h + 1
            return s["total_d"], (PH - POOL_HEADS) * t + h - POOL_HEADS + 1

        def form_total(eng, t, h):
            n = PH * t + h
            if n >= RING:
                eng.wait_ge(s["weight"], n - RING + 1)
            return eng.tensor_tensor(total[:, n % RING], sim[:, t % 2, 0, h, :, None].to_broadcast([P, NK, NK]),
                                     sim[:, t % 2, 1, h, None, :].to_broadcast([P, NK, NK]), ALU.add)

        @block.scalar
        def _(act):
            act.wait_ge(s["turned"], 1)
            act.activation(keys_T[:].rearrange("p h k s -> p (h k s)"), banks[:, 6, :], ACT.Copy).then_inc(s["turned_out"], 1)
            for i in range(2):
                act.wait_ge(s["turned"], 2 + i)
                act.activation(down_T[:, 4 * i:4 * i + 4, :].rearrange("p t e -> p (t e)"), banks[:, 7 - i, :],
                               ACT.Copy).then_inc(s["turned_out"], 1)
            for f in range(F):
                act.wait_ge(s["var"], f + 1)
                act.activation(bn[:, f, 1:2], bn[:, f, 0:1], ACT.Sqrt).then_inc(s["root"], 1)
                if f >= 1:
                    store_q(act, f - 1)
            store_q(act, F - 1)
            for i in range(2 * ET):
                act.wait_ge(s["h_ready"], i + 1)
                act.activation(gelu_T[:, i // 2, (i % 2) * 512:(i % 2) * 512 + 512], banks[:, i % 4, :],
                               ACT.Gelu_apprx_tanh).then_inc(s["gelu"], 1)

            def exponents(t):
                act.wait_ge(s["exd"], t + 1)
                act.activation(ex[:], ex[:], ACT.Exp).then_inc(s["ex"], 1)

            sim_copy(act, 0)
            exponents(0)
            for t in range(NT):
                for h in range(PH):
                    n = PH * t + h
                    if h == LAG and t + 1 < NT:
                        sim_copy(act, t + 1)
                    if h == EARLY and t + 1 < NT:
                        exponents(t + 1)
                    act.wait_ge(*total_sem(t, h))
                    if n >= 3:
                        act.wait_ge(s["weight"], n - 2)
                    act.activation(expo[:, n % 3, :], total[:, n % RING].rearrange("p i j -> p (i j)"), ACT.Exp,
                                   bias=neg[:, t % 2, h:h + 1]).then_inc(s["expo"], 1)

        @block.gpsimd
        def _(pool):
            for t in range(NT):
                pool.wait_ge(s["sim_out"], t + 1)
                for h in range(PH):
                    n = PH * t + h
                    if h < POOL_HEADS:
                        form_total(pool, t, h).then_inc(s["total_p"], 1)
                    if h == 0:
                        pool.wait_ge(s["rz"], t + 1)
                    if n >= 2:
                        pool.wait_ge(s["wT"], n - 1)
                    pool.tensor_scalar(diag[:, n % 2, :], ident[:], rz[:, t % 2, h:h + 1], None, ALU.mult).then_inc(s["diag"], 1)

        @block.tensor
        def _(pe):
            pe.wait_ge(s["k_in"], 16)
            for i in range(4):
                mm = pe.transpose(banks[:, 6, i * P:(i + 1) * P], keys_in[:, i, :], ident[:])
            mm.then_inc(s["turned"], 1)
            pe.wait_ge(s["d_in"], 16)
            for i in range(ET):
                if i == 4:
                    pe.wait_ge(s["turned_out"], 1)
                mm = pe.transpose(banks[:, 7 - i // 4, (i % 4) * P:(i % 4 + 1) * P], down_in[:, i, :], ident[:])
                if i % 4 == 3:
                    mm.then_inc(s["turned"], 1)
            pe.wait_ge(s["w_in"], 16)
            for f in range(F):
                if f >= 3:
                    pe.wait_ge(s["q_used"], f - 2)
                for c in range(2):
                    mm = pe.matmul(banks[:, 2 * (f % 3) + c, :], wq_sb[:, f * P:(f + 1) * P],
                                   xnT[:, 512 * c:512 * c + 512], start=True, stop=True)
                mm.then_inc(s["q_ready"], 1)
            pe.wait_ge(s["q_used"], F)
            pe.wait_ge(s["turned_out"], 3)
            for i in range(2 * ET):
                if i >= 4:
                    pe.wait_ge(s["gelu"], i - 3)
                pe.matmul(banks[:, i % 4, :], down_T[:, i // 2, :], xnT[:, (i % 2) * 512:(i % 2) * 512 + 512],
                          start=True, stop=True).then_inc(s["h_ready"], 1)
            pe.wait_ge(s["gelu"], 2 * ET)

            def similarities(t):
                if t >= 2:
                    pe.wait_ge(s["sim_out"], t - 1)
                for side in range(SIDE):
                    for h in range(PH):
                        c = (side * PH + h) * NK
                        mm = pe.matmul(banks[:, t % 2, c:c + NK], q_T[:, side * PH + h, t * P:(t + 1) * P],
                                       keys_T[:, h, :, side], start=True, stop=True)
                mm.then_inc(s["sim_ready"], 1)

            def up_product(t):
                pe.wait_ge(s["act_T"], t + 1)
                if t >= 1:
                    pe.wait_ge(s["added"], t)
                for i in range(ET):
                    mm = pe.matmul(banks[:, 6, 0:D], act_T[:, i, :], up_sb[:, i, :], start=(i == 0), stop=(i == ET - 1))
                mm.then_inc(s["out"], 1)

            similarities(0)
            pe.wait_ge(s["u_in"], 16)
            for t in range(NT):
                if t + 1 < NT:
                    similarities(t + 1)
                for h in range(PH):
                    n = PH * t + h
                    pe.wait_ge(s["weight"], n + 1)
                    pe.wait_ge(s["diag"], n + 1)
                    if h == 0 and t >= 2:
                        pe.wait_ge(s["act_T"], t - 1)
                    for i in range(ET):
                        mm = pe.matmul(banks[:, 2 + 2 * (t % 2) + i // 4, (i % 4) * P:(i % 4 + 1) * P],
                                       weight[:, n % 2, i * P:(i + 1) * P], diag[:, n % 2, :],
                                       start=(h == 0 and i % 4 == 0), stop=(h == PH - 1), skip_group_check=True)
                    mm.then_inc(s["wT"], 1)
                    if h == LAG and t >= 1:
                        up_product(t - 1)
            up_product(NT - 1)

        @block.vector
        def _(dve):
            for f in range(F):
                dve.wait_ge(s["q_ready"], f + 1)
                for c in range(2):
                    dve.bn_stats(stats[:, f, c, :], banks[:, 2 * (f % 3) + c, :]).then_inc(s["q_stats"], 1)
                dve.wait_ge(s["q_stats"], 3 * f + 2)
                dve.bn_aggr(mv[:, f, :], stats[:, f].rearrange("p c k -> p (c k)")).then_inc(s["q_stats"], 1)
                dve.wait_ge(s["q_stats"], 3 * f + 3)
                dve.tensor_scalar(bn[:, f, 0:1], mv[:, f, 1:2], BN_EPS, None, ALU.add).then_inc(s["var"], 1)
                if f == 0:
                    dve.wait_ge(s["gb_in"], 32)
                dve.wait_ge(s["root"], f + 1)
                dve.reciprocal(bn[:, f, 1:2], bn[:, f, 1:2]).then_inc(s["rroot"], 1)
                dve.wait_ge(s["rroot"], f + 1)
                dve.tensor_tensor(bn[:, f, 2:3], bn[:, f, 1:2], g_sb[:, f:f + 1], ALU.mult).then_inc(s["scale"], 1)
                dve.wait_ge(s["scale"], f + 1)
                dve.tensor_tensor(bn[:, f, 3:4], mv[:, f, 0:1], bn[:, f, 2:3], ALU.mult).then_inc(s["shift0"], 1)
                dve.wait_ge(s["shift0"], f + 1)
                dve.tensor_tensor(bn[:, f, 3:4], b_sb[:, f:f + 1], bn[:, f, 3:4], ALU.subtract).then_inc(s["shift"], 1)

            def select(t):
                dve.wait_ge(s["sim_out"], t + 1)
                for side in range(SIDE):
                    for h in range(PH):
                        dve.max(top[:, side, h, :], sim[:, t % 2, side, h, :]).then_inc(s["top"], 1)
                dve.wait_ge(s["top"], F * (t + 1))
                dve.tensor_tensor(pair[:], top[:, 0, :, :, None].to_broadcast([P, PH, TOPK, TOPK]),
                                  top[:, 1, :, None, :].to_broadcast([P, PH, TOPK, TOPK]), ALU.add).then_inc(s["pair"], 1)
                dve.wait_ge(s["pair"], t + 1)
                if t >= 2:
                    dve.wait_ge(s["weight"], PH * (t - 1))
                for h in range(PH):
                    dve.max(best[:, t % 2, h, :], pair[:, h].rearrange("p a b -> p (a b)")).then_inc(s["best"], 1)
                dve.wait_ge(s["best"], PH * (t + 1))
                if t >= 2:
                    dve.wait_ge(s["expo"], PH * (t - 1))
                dve.tensor_scalar(neg[:, t % 2, :], best[:, t % 2, :, 0], -1.0, None, ALU.mult).then_inc(s["neg"], 1)
                dve.wait_ge(s["neg"], t + 1)
                dve.tensor_tensor(ex[:], best[:, t % 2], neg[:, t % 2, :, None].to_broadcast([P, PH, TOPK]),
                                  ALU.add).then_inc(s["exd"], 1)

            def normalise(t):
                dve.wait_ge(s["ex"], t + 1)
                dve.tensor_reduce(z[:], ex[:], AX.X, ALU.add).then_inc(s["z"], 1)
                dve.wait_ge(s["z"], t + 1)
                if t >= 2:
                    dve.wait_ge(s["diag"], PH * (t - 1))
                dve.reciprocal(rz[:, t % 2, :], z[:]).then_inc(s["rz"], 1)

            def activate(t):
                dve.wait_ge(s["wT"], PH * (t + 1))
                if t >= 1:
                    dve.wait_ge(s["out"], t)
                dve.tensor_tensor(act_T[:], banks[:, 2 + 2 * (t % 2):4 + 2 * (t % 2), :]
                                  .rearrange("p b (i n) -> p (b i) n", i=4), gelu_T[:, :, t * P:(t + 1) * P],
                                  ALU.mult).then_inc(s["act_T"], 1)

            def add(t):
                dve.wait_ge(s["out"], t + 1)
                dve.tensor_tensor(x_sb[:, t, :], x_sb[:, t, :], banks[:, 6, 0:D], ALU.add).then_inc(s["added"], 1)

            def mask(n):
                t, h = divmod(n, PH)
                dve.wait_ge(s["expo"], n + 1)
                if n >= 2:
                    dve.wait_ge(s["wT"], n - 1)
                dve.scalar_tensor_tensor(weight[:, n % 2, :], total[:, n % RING].rearrange("p i j -> p (i j)"),
                                         best[:, t % 2, h, TOPK - 1:TOPK], expo[:, n % 3, :], ALU.is_ge,
                                         ALU.mult).then_inc(s["weight"], 1)

            select(0)
            normalise(0)
            for n in range(PH * NT + LAG):
                t, h = divmod(n, PH)
                if h == LAG + 1 and t >= 1:
                    activate(t - 1)
                if h == EARLY and t + 1 < NT:
                    select(t + 1)
                if h == EARLY + 2 and t + 1 < NT:
                    normalise(t + 1)
                if h >= POOL_HEADS and t < NT:
                    form_total(dve, t, h).then_inc(s["total_d"], 1)
                if n >= LAG:
                    mask(n - LAG)
                if h == PH - 1 and t >= 1:
                    add(t - 1)
            activate(NT - 1)
            add(NT - 1)


DI = 256
CT = DI // P
NS = 16
TAPS = 4


def state_space_stage(nc, w_in, conv_w, conv_b, w_x, w_dt, b_dt, a_log, d_par, w_out, x_sb, xnT, ident, ssm_scr,
                      beside):
    R = 1 + 2 * NS
    with Stage(nc, "ssm") as st:
        w_sb = st.sb("w_sb", [P, 2 * DI])
        wx_sb, wo_sb = st.sb("wx_sb", [P, CT, R]), st.sb("wo_sb", [P, CT, D])
        cw, cb = st.sb("cw", [P, CT, TAPS]), st.sb("cb", [P, CT])
        wdt, bdt, dpar = st.sb("wdt", [P, CT]), st.sb("bdt", [P, CT]), st.sb("dpar", [P, CT])
        a_sb = st.sb("a_sb", [P, CT, NS])
        x_in = st.sb("x_in", [P, CT, TAPS - 1 + N])
        conv = st.sb("conv", [P, 2, N])
        xc, gate = st.sb("xc", [P, CT, N]), st.sb("gate", [P, CT, N])
        ssm_T = st.sb("ssm_T", [R, N])
        row_b = st.sb("row_b", [P, N])
        v, soft = st.sb("v", [P, N]), st.sb("soft", [P, N])
        delta, u = st.sb("delta", [P, CT, N]), st.sb("u", [P, CT, N])
        bc = st.sb("bc", [P, 2, 2, N])
        decay, drive = st.sb("decay", [P, 3, N]), st.sb("drive", [P, 3, N])
        state, read = st.sb("state", [P, 2, N]), st.sb("read", [P, 2, N])
        y = st.sb("y", [P, CT, N])
        s = {n: st.sem(n) for n in (
            "w_in", "p_in", "xz", "zeros", "xz_used", "conv", "xc", "gate", "x_ssm", "ssm_T", "ssm_out", "row", "v",
            "dv", "e1", "e2", "max0", "delta", "u", "a_exp", "a_neg", "decay", "drive", "state", "read", "summed",
            "skip", "y", "out", "added")}
        bc_in = [st.sem(f"bc_in{i}") for i in range(2)]
        N_PAR = 9

        def load(sp):
            sp.dma_start(w_sb[:], w_in).then_inc(s["w_in"], 16)
            with nc.allow_non_contiguous_dma(reason="a few values per channel, once"):
                sp.dma_start(wx_sb[:], w_x.rearrange("(c p) r -> p c r", p=P)).then_inc(s["p_in"], 16)
                sp.dma_start(wo_sb[:], w_out.rearrange("(c p) r -> p c r", p=P)).then_inc(s["p_in"], 16)
                sp.dma_start(cw[:], conv_w.rearrange("(c p) a k -> p c (a k)", p=P)).then_inc(s["p_in"], 16)
                sp.dma_start(a_sb[:], a_log.rearrange("(c p) s -> p c s", p=P)).then_inc(s["p_in"], 16)
                for dst, src in ((cb, conv_b), (wdt, w_dt), (bdt, b_dt), (dpar, d_par)):
                    sp.dma_start(dst[:], src.rearrange("(c p) -> p c", p=P)).then_inc(s["p_in"], 16)
            beside(sp)

        layernorm_stage(nc, "ln3", x_sb, xnT, ident, load)
        banks = st.ps("banks", [P, 8, 512])
        block = st.block()

        @block.sync
        def _(sp):
            sp.wait_ge(s["ssm_T"], 2)
            sp.dma_start(ssm_scr, ssm_T[:]).then_inc(s["ssm_out"], 16)
            sp.wait_ge(s["ssm_out"], 16)
            sp.dma_start(row_b[:], ssm_scr[0:1, :].partition_broadcast(P)).then_inc(s["row"], 16)
            for i in range(NS):
                if i >= 2:
                    sp.wait_ge(s["drive"], CT * (i - 1))
                    sp.wait_ge(s["read"], CT * (i - 1))
                sp.dma_start(bc[:, i % 2, 0, :], ssm_scr[1 + i:2 + i, :].partition_broadcast(P)).then_inc(bc_in[i % 2], 16)
                sp.dma_start(bc[:, i % 2, 1, :], ssm_scr[1 + NS + i:2 + NS + i, :].partition_broadcast(P)).then_inc(bc_in[i % 2], 16)

        @block.tensor
        def _(pe):
            pe.wait_ge(s["w_in"], 16)
            for f in range(2 * CT):
                for c in range(2):
                    mm = pe.matmul(banks[:, 2 * f + c, :], w_sb[:, f * P:(f + 1) * P], xnT[:, 512 * c:512 * c + 512],
                                   start=True, stop=True)
                mm.then_inc(s["xz"], 1)
            pe.wait_ge(s["p_in"], 16 * (N_PAR - 1))
            pe.wait_ge(s["xc"], CT)
            pe.wait_ge(s["xz_used"], CT)
            for c in range(2):
                for ct in range(CT):
                    mm = pe.matmul(banks[0:R, c, :], wx_sb[:, ct, :], xc[:, ct, 512 * c:512 * c + 512],
                                   start=(ct == 0), stop=(ct == CT - 1))
                mm.then_inc(s["x_ssm"], 1)
            pe.wait_ge(s["gate"], CT)
            pe.wait_ge(s["ssm_T"], 2)
            for i in range(NS):
                for ct in range(CT):
                    k = CT * i + ct
                    pe.wait_ge(s["read"], k + 1)
                    for c in range(2):
                        mm = pe.matmul(banks[:, 4 + 2 * ct + c, :], ident[:], read[:, k % 2, 512 * c:512 * c + 512],
                                       start=(i == 0), stop=(i == NS - 1), skip_group_check=True)
                    mm.then_inc(s["summed"], 1)
            pe.wait_ge(s["y"], CT)
            for t in range(NT):
                for ct in range(CT):
                    mm = pe.matmul(banks[:, t // 4, (t % 4) * D:(t % 4 + 1) * D], y[:, ct, t * P:(t + 1) * P],
                                   wo_sb[:, ct, :], start=(ct == 0), stop=(ct == CT - 1))
                mm.then_inc(s["out"], 1)

        @block.scalar
        def _(act):
            act.wait_ge(s["p_in"], 16 * (N_PAR - 1))
            for ct in range(CT):
                act.wait_ge(s["xz"], ct + 1)
                act.activation(x_in[:, ct, TAPS - 1:], banks[:, 2 * ct:2 * ct + 2, :].rearrange("p b n -> p (b n)"),
                               ACT.Copy).then_inc(s["xz_used"], 1)
            for ct in range(CT):
                act.wait_ge(s["xz"], CT + ct + 1)
                act.activation(gate[:, ct, :], banks[:, 2 * (CT + ct):2 * (CT + ct) + 2, :].rearrange("p b n -> p (b n)"),
                               ACT.Silu).then_inc(s["gate"], 1)
            for ct in range(CT):
                act.wait_ge(s["conv"], TAPS * (ct + 1))
                act.activation(xc[:, ct, :], conv[:, ct, :], ACT.Silu).then_inc(s["xc"], 1)
            for c in range(2):
                act.wait_ge(s["x_ssm"], c + 1)
                act.activation(ssm_T[:, 512 * c:512 * c + 512], banks[0:R, c, :], ACT.Copy).then_inc(s["ssm_T"], 1)
            act.activation(a_sb[:], a_sb[:], ACT.Exp).then_inc(s["a_exp"], 1)
            for ct in range(CT):
                act.wait_ge(s["dv"], 2 * ct + 2)
                act.activation(soft[:], soft[:], ACT.Exp, scale=-1.0).then_inc(s["e1"], 1)
                act.wait_ge(s["e1"], ct + 1)
                act.activation(soft[:], soft[:], ACT.Ln, bias=1.0).then_inc(s["e2"], 1)
            act.wait_ge(s["a_neg"], 1)
            for i in range(NS):
                for ct in range(CT):
                    k = CT * i + ct
                    if k >= 3:
                        act.wait_ge(s["state"], k - 2)
                    act.wait_ge(s["delta"], ct + 1)
                    act.activation(decay[:, k % 3, :], delta[:, ct, :], ACT.Exp, scale=a_sb[:, ct, i:i + 1]).then_inc(s["decay"], 1)

        @block.gpsimd
        def _(pool):
            pool.memset(x_in[:, :, 0:TAPS - 1], 0.0).then_inc(s["zeros"], 1)
            for i in range(NS):
                for ct in range(CT):
                    k = CT * i + ct
                    if k >= 3:
                        pool.wait_ge(s["state"], k - 2)
                    if ct == 0:
                        pool.wait_ge(bc_in[i % 2], 32 * (i // 2 + 1))
                    pool.wait_ge(s["u"], ct + 1)
                    pool.tensor_tensor(drive[:, k % 3, :], u[:, ct, :], bc[:, i % 2, 0, :], ALU.mult).then_inc(s["drive"], 1)

        @block.vector
        def _(dve):
            dve.wait_ge(s["p_in"], 16 * (N_PAR - 1))
            dve.wait_ge(s["zeros"], 1)
            for ct in range(CT):
                dve.wait_ge(s["xz_used"], ct + 1)
                dve.tensor_scalar(conv[:, ct, :], x_in[:, ct, 0:N], cw[:, ct, 0:1], cb[:, ct:ct + 1], ALU.mult,
                                  ALU.add).then_inc(s["conv"], 1)
                for k in range(1, TAPS):
                    dve.wait_ge(s["conv"], TAPS * ct + k)
                    dve.scalar_tensor_tensor(conv[:, ct, :], x_in[:, ct, k:k + N], cw[:, ct, k:k + 1], conv[:, ct, :],
                                             ALU.mult, ALU.add).then_inc(s["conv"], 1)
            dve.wait_ge(s["a_exp"], 1)
            dve.tensor_scalar(a_sb[:], a_sb[:], -1.0, None, ALU.mult).then_inc(s["a_neg"], 1)
            dve.wait_ge(s["row"], 16)
            for ct in range(CT):
                if ct >= 1:
                    dve.wait_ge(s["delta"], ct)
                dve.tensor_scalar(v[:], row_b[:], wdt[:, ct:ct + 1], bdt[:, ct:ct + 1], ALU.mult, ALU.add).then_inc(s["dv"], 1)
                dve.wait_ge(s["dv"], 2 * ct + 1)
                dve.scalar_tensor_tensor(soft[:], v[:], -1.0, v[:], ALU.mult, ALU.max).then_inc(s["dv"], 1)
                dve.wait_ge(s["e2"], ct + 1)
                dve.scalar_tensor_tensor(delta[:, ct, :], v[:], 0.0, soft[:], ALU.max, ALU.add).then_inc(s["delta"], 1)
                dve.wait_ge(s["delta"], ct + 1)
                dve.wait_ge(s["xc"], ct + 1)
                dve.tensor_tensor(u[:, ct, :], delta[:, ct, :], xc[:, ct, :], ALU.mult).then_inc(s["u"], 1)
            for i in range(NS):
                for ct in range(CT):
                    k = CT * i + ct
                    dve.wait_ge(s["decay"], k + 1)
                    dve.wait_ge(s["drive"], k + 1)
                    if k >= 2:
                        dve.wait_ge(s["read"], k - 1)
                    dve.tensor_tensor_scan(state[:, k % 2, :], decay[:, k % 3, :], drive[:, k % 3, :], 0.0,
                                           ALU.mult, ALU.add).then_inc(s["state"], 1)
                    dve.wait_ge(bc_in[i % 2], 32 * (i // 2 + 1))
                    dve.wait_ge(s["state"], k + 1)
                    if k >= 2:
                        dve.wait_ge(s["summed"], k - 1)
                    dve.tensor_tensor(read[:, k % 2, :], state[:, k % 2, :], bc[:, i % 2, 1, :], ALU.mult).then_inc(s["read"], 1)
            for ct in range(CT):
                dve.wait_ge(s["summed"], CT * NS)
                dve.scalar_tensor_tensor(y[:, ct, :], xc[:, ct, :], dpar[:, ct:ct + 1],
                                         banks[:, 4 + 2 * ct:6 + 2 * ct, :].rearrange("p b n -> p (b n)"), ALU.mult,
                                         ALU.add).then_inc(s["skip"], 1)
                dve.wait_ge(s["skip"], ct + 1)
                dve.wait_ge(s["gate"], ct + 1)
                dve.tensor_tensor(y[:, ct, :], y[:, ct, :], gate[:, ct, :], ALU.mult).then_inc(s["y"], 1)
            for g in range(2):
                dve.wait_ge(s["out"], 4 * (g + 1))
                xs = x_sb[:, 4 * g:4 * g + 4, :]
                dve.tensor_tensor(xs, xs, banks[:, g, :].rearrange("p (t d) -> p t d", t=4), ALU.add).then_inc(s["added"], 1)


EX = 8
FF = 512
FT = FF // P
CAP = N // EX


def expert_choice_stage(nc, ws, bs, w1, b1, w2, b2, x_sb, xnT, ident):
    TAKEN = -1.0
    with Stage(nc, "moe") as st:
        ws_sb, bs_sb = st.sb("ws_sb", [P, EX]), st.sb("bs_sb", [P, EX])
        w1_sb, w2_sb = st.sb("w1_sb", [P, 2, FF]), st.sb("w2_sb", [P, 2, FT, D])
        b1_sb, b2_sb = st.sb("b1_sb", [P, EX, FT]), st.sb("b2_sb", [EX, D])
        logit = st.sb("logit", [P, NT, EX])
        top, total, rtotal = st.sb("top", [P, NT]), st.sb("total", [P, NT]), st.sb("rtotal", [P, NT])
        prob_T, left = st.sb("prob_T", [EX, N]), st.sb("left", [EX, N])
        eight = st.sb("eight", [EX, CAP // 8, 8])
        gate_T = st.sb("gate_T", [EX, N])
        gate = st.sb("gate", [P, NT, EX])
        hid = st.sb("hid", [P, 2, FT, N])
        s = {n: st.sem(n) for n in (
            "s_in", "bs_in", "b_in", "logits", "step", "exp", "prob", "probT", "probT_out", "left", "gateT", "gate",
            "gate_out", "hid_ps", "hid", "out", "added")}
        w_in = [st.sem(f"w_in{i}") for i in range(2)]

        def load_expert(sp, e):
            sp.dma_start(w1_sb[:, e % 2, :], w1[e]).then_inc(w_in[e % 2], 16)
            sp.dma_start(w2_sb[:, e % 2], w2[e].rearrange("(f p) d -> p f d", p=P)).then_inc(w_in[e % 2], 16)

        def load(sp):
            sp.dma_start(ws_sb[:], ws).then_inc(s["s_in"], 16)
            sp.dma_start(bs_sb[:], row(bs, EX).partition_broadcast(P)).then_inc(s["bs_in"], 16)
            with nc.allow_non_contiguous_dma(reason="4096 bias values, once"):
                sp.dma_start(b1_sb[:], b1.rearrange("e (f p) -> p e f", p=P)).then_inc(s["b_in"], 16)
            sp.dma_start(b2_sb[:], b2).then_inc(s["b_in"], 16)
            for e in range(2):
                load_expert(sp, e)

        layernorm_stage(nc, "ln5", x_sb, xnT, ident, load)
        banks = st.ps("banks", [P, 8, 512])
        block = st.block()

        @block.sync
        def _(sp):
            for e in range(2, EX):
                sp.wait_ge(s["out"], 2 * (e - 1))
                load_expert(sp, e)

        @block.tensor
        def _(pe):
            pe.wait_ge(s["s_in"], 16)
            for t in range(NT):
                mm = pe.matmul(banks[:, 0, t * EX:(t + 1) * EX], xnT[:, t * P:(t + 1) * P], ws_sb[:], start=True, stop=True)
            mm.then_inc(s["logits"], 1)
            pe.wait_ge(s["prob"], 1)
            for t in range(NT):
                mm = pe.transpose(banks[0:EX, 1 + t // 4, (t % 4) * P:(t % 4 + 1) * P], logit[:, t, :], ident[:])
            mm.then_inc(s["probT"], 1)

            def hidden(e, k):
                n = 2 * FT * e + k
                f, c = k // 2, k % 2
                if n >= 3:
                    pe.wait_ge(s["hid"], n - 2)
                else:
                    pe.wait_ge(s["probT_out"], 1)
                pe.matmul(banks[:, 1 + n % 3, :], w1_sb[:, e % 2, f * P:(f + 1) * P], xnT[:, 512 * c:512 * c + 512],
                          start=True, stop=True).then_inc(s["hid_ps"], 1)

            def output(e, half):
                n = 2 * e + half
                if n >= 2:
                    pe.wait_ge(s["added"], 4 * (n - 1))
                pe.wait_ge(s["hid"], 2 * FT * (e + 1))
                for t in range(4 * half, 4 * half + 4):
                    for f in range(FT):
                        mm = pe.matmul(banks[:, 4 + n % 2, (t % 4) * D:(t % 4 + 1) * D], hid[:, e % 2, f, t * P:(t + 1) * P],
                                       w2_sb[:, e % 2, f, :], start=(f == 0), stop=(f == FT - 1))
                mm.then_inc(s["out"], 1)

            for e in range(EX):
                pe.wait_ge(w_in[e % 2], 32 * (e // 2 + 1))
                for k in range(2 * FT):
                    hidden(e, k)
                if e == 1:
                    pe.wait_ge(s["gateT"], 1)
                    for t in range(NT):
                        mm = pe.transpose(banks[:, 6, t * EX:(t + 1) * EX], gate_T[:, t * P:(t + 1) * P], ident[0:EX, 0:EX])
                    mm.then_inc(s["gate"], 1)
                output(e, 0)
                output(e, 1)
            pe.wait_ge(s["b_in"], 32)
            for g in range(2):
                pe.wait_ge(s["added"], 4 * (2 * EX - 1 + g))
                for t in range(4 * g, 4 * g + 4):
                    mm = pe.matmul(banks[:, 4 + g, (t % 4) * D:(t % 4 + 1) * D], gate_T[:, t * P:(t + 1) * P], b2_sb[:],
                                   start=True, stop=True)
                mm.then_inc(s["out"], 1)

        @block.scalar
        def _(act):
            act.wait_ge(s["step"], 3)
            act.activation(logit[:], logit[:], ACT.Exp).then_inc(s["exp"], 1)
            act.wait_ge(s["probT"], 1)
            act.activation(prob_T[:], banks[0:EX, 1:3, :].rearrange("p b n -> p (b n)"), ACT.Copy).then_inc(s["probT_out"], 1)
            act.wait_ge(s["b_in"], 32)
            for e in range(EX):
                for k in range(2 * FT):
                    n = 2 * FT * e + k
                    f, c = k // 2, k % 2
                    act.wait_ge(s["hid_ps"], n + 1)
                    if e >= 2 and k == 0:
                        act.wait_ge(s["out"], 2 * (e - 1))
                    act.activation(hid[:, e % 2, f, 512 * c:512 * c + 512], banks[:, 1 + n % 3, :], ACT.Gelu_apprx_tanh,
                                   bias=b1_sb[:, e, f:f + 1]).then_inc(s["hid"], 1)

        @block.vector
        def _(dve):
            chain = Chain(dve, s["step"])
            wide = [P, NT, EX]
            dve.wait_ge(s["logits"], 1)
            dve.wait_ge(s["bs_in"], 16)
            chain(dve.tensor_tensor(logit[:], banks[:, 0, 0:NT * EX].rearrange("p (t e) -> p t e", t=NT),
                                    bs_sb[:, None, :].to_broadcast(wide), ALU.add))
            chain(dve.tensor_reduce(top[:], logit[:], AX.X, ALU.max))
            chain(dve.tensor_tensor(logit[:], logit[:], top[:, :, None].to_broadcast(wide), ALU.subtract))
            dve.wait_ge(s["exp"], 1)
            chain(dve.tensor_reduce(total[:], logit[:], AX.X, ALU.add))
            chain(dve.reciprocal(rtotal[:], total[:]))
            dve.tensor_tensor(logit[:], logit[:], rtotal[:, :, None].to_broadcast(wide), ALU.mult).then_inc(s["prob"], 1)
            dve.wait_ge(s["probT_out"], 1)
            for r in range(CAP // 8):
                src = prob_T if r == 0 else left
                dve.max(eight[:, r, :], src[:]).then_inc(s["left"], 1)
                dve.wait_ge(s["left"], 2 * r + 1)
                dve.match_replace(left[:], eight[:, r, :], src[:], TAKEN).then_inc(s["left"], 1)
                dve.wait_ge(s["left"], 2 * r + 2)
            dve.scalar_tensor_tensor(gate_T[:], left[:], TAKEN, prob_T[:], ALU.is_equal, ALU.mult).then_inc(s["gateT"], 1)
            dve.wait_ge(s["gate"], 1)
            dve.tensor_copy(gate[:].rearrange("p t e -> p (t e)"), banks[:, 6, 0:NT * EX]).then_inc(s["gate_out"], 1)
            dve.wait_ge(s["gate_out"], 1)
            for e in range(EX):
                for half in range(2):
                    n = 2 * e + half
                    dve.wait_ge(s["out"], n + 1)
                    if n >= 2:
                        dve.wait_ge(s["added"], 4 * (n - 1))
                    for t in range(4 * half, 4 * half + 4):
                        dve.scalar_tensor_tensor(x_sb[:, t, :], banks[:, 4 + n % 2, (t % 4) * D:(t % 4 + 1) * D],
                                                 gate[:, t, e:e + 1], x_sb[:, t, :], ALU.mult, ALU.add).then_inc(s["added"], 1)
            for g in range(2):
                dve.wait_ge(s["out"], 2 * EX + g + 1)
                dve.wait_ge(s["added"], 4 * (2 * EX - 1 + g))
                xs = x_sb[:, 4 * g:4 * g + 4, :]
                dve.tensor_tensor(xs, xs, banks[:, 4 + g, :].rearrange("p (t d) -> p t d", t=4), ALU.add).then_inc(s["added"], 4)



def decoder_program(nc, out, **a):
    x_sb = nc.alloc_sbuf_tensor("x_sb", [P, NT, D], F32)
    ident = nc.alloc_sbuf_tensor("ident", [P, P], F32)
    xnT = nc.alloc_sbuf_tensor("xnT", [P, N], F32)
    k_scr = [nc.dram_tensor(f"k_scr{l}", [3, P, T], BF16).ap() for l in range(2)]
    v_scr = [nc.dram_tensor(f"v_scr{l}", [P, KT, PAIRS, VW], F32).ap() for l in range(2)]
    q_scr = [nc.dram_tensor(f"q_scr{l}", [2, ROW_M + 6, PAIRS, N], BF16).ap() for l in range(2)]
    q_nat = [nc.dram_tensor(f"q_nat{l}", [3, P, N], BF16).ap() for l in range(2)]
    bias_scr = [nc.dram_tensor(f"bias_scr{l}", [QB, T], F32 if l == 0 else I32).ap() for l in range(2)]
    rows_scr = nc.dram_tensor("rows_scr", [5, T], BF16).ap()
    ssm_scr = nc.dram_tensor("ssm_scr", [1 + 2 * NS, N], F32).ap()

    def flat_heads(w):
        return w.rearrange("a h e -> a (h e)")

    constants_stage(nc, a["x"], x_sb, ident)
    kv_stage(nc, a["ctx_1024"][0], [flat_heads(a["L0_xattn_wk"]), a["L1_xattn_Wk"]],
             [flat_heads(a["L0_xattn_wv"]), a["L1_xattn_Wv"]], a["L1_xattn_bk"], a["L1_xattn_bv"], ident, k_scr, v_scr)

    even_rows_stage(nc, a["mask_1x1xSxS2_ik0"][0, 0, 0:1, :], rows_scr)

    with Sides(nc, "sides0", False, flat_heads(a["L0_xattn_wq"]), None, k_scr[0], v_scr[0], rows_scr) as sides:
        sides.make_keys()
        layernorm_stage(nc, "ln0", x_sb, xnT, ident)
        linear_attention_stage(nc, a["L0_attn_wqkv"], a["L0_attn_wo"], x_sb, xnT, ident, sides.load)
        layernorm_stage(nc, "ln1", x_sb, xnT, ident)
        q_stage(nc, "q0", sides, DH ** -0.5, xnT, ident, q_nat[0], q_scr[0])
        cross_attention_stage(nc, "xa0", sides, a["mask_Bx1xSxS2_ff0"][0, 0],
                              a["L0_xattn_wo"].rearrange("h e d -> (h e) d"), None, x_sb, ident, q_scr[0], bias_scr[0])
    product_key_stage(nc, a["L0_ffn_w_q"], a["L0_ffn_bn_gamma"], a["L0_ffn_bn_beta"], a["L0_ffn_keys"],
                      a["L0_ffn_down_embed"], a["L0_ffn_up_embed"], x_sb, xnT, ident)

    with Sides(nc, "sides1", True, a["L1_xattn_Wq"], a["L1_xattn_bq"], k_scr[1], v_scr[1], rows_scr) as sides:
        state_space_stage(nc, *[a["L1_attn_" + n] for n in ("W_in", "conv_w", "conv_b", "W_xproj", "w_dt", "b_dt",
                                                            "A_log", "D_param", "W_out")],
                          x_sb, xnT, ident, ssm_scr, sides.load_values)
        sides.make_keys()
        layernorm_stage(nc, "ln4", x_sb, xnT, ident, sides.load_keys)
        q_stage(nc, "q1", sides, DH ** -0.5, xnT, ident, q_nat[1], q_scr[1])
        cross_attention_stage(nc, "xa1", sides, a["mask_1x1xSxS2_ik0"][0, 0], a["L1_xattn_Wo"], a["L1_xattn_bo"],
                              x_sb, ident, q_scr[1], bias_scr[1])
    expert_choice_stage(nc, *[a["L1_ffn_" + n] for n in ("Ws", "bs", "W1", "b1", "W2", "b2")], x_sb, xnT, ident)

    with Stage(nc, "store") as st:
        stored = st.sem("stored")
        block = st.block()

        @block.sync
        def _(sp):
            sp.dma_start(out[0].rearrange("(t p) d -> p t d", p=P), x_sb[:]).then_inc(stored, 16)
            sp.wait_ge(stored, 16)


INPUTS = (["x", "ctx_1024", "mask_Bx1xSxS2_ff0", "mask_1x1xSxS2_ik0", "L0_attn_wqkv", "L0_attn_wo"]
          + ["L0_xattn_" + n for n in ("wq", "wk", "wv", "wo")]
          + ["L0_ffn_" + n for n in ("w_q", "bn_gamma", "bn_beta", "keys", "down_embed", "up_embed")]
          + ["L1_attn_" + n for n in ("W_in", "conv_w", "conv_b", "W_xproj", "w_dt", "b_dt", "A_log", "D_param", "W_out")]
          + ["L1_xattn_" + n for n in ("Wq", "bq", "Wk", "bk", "Wv", "bv", "Wo", "bo")]
          + ["L1_ffn_" + n for n in ("Ws", "bs", "W1", "b1", "W2", "b2")])


def kernel(**inputs):
    import numpy as np
    import concourse.bacc as bacc
    from concourse.bass_utils import run_bass_kernel_spmd

    nc = bacc.Bacc("TRN2", target_bir_lowering=False, num_devices=1)
    arrays, aps = {}, {}
    for name in INPUTS:
        a = np.ascontiguousarray(inputs[name])
        arrays["in_" + name] = a
        aps[name] = nc.dram_tensor("in_" + name, a.shape, mybir.dt.from_np(a.dtype), kind="ExternalInput").ap()
    out = nc.dram_tensor("out", [1, N, D], F32, kind="ExternalOutput").ap()
    decoder_program(nc, out, **aps)
    r = run_bass_kernel_spmd(nc, [arrays], core_ids=[0])
    return r.results[0]["out"]
```
